# Optimizing a Trainium2 kernel written in Bass

```python
import numpy as np
import jax
import jax.numpy as jnp

def _softmax(x, axis=-1):
    return jax.nn.softmax(x, axis=axis)

def _gelu(x):
    return jax.nn.gelu(x, approximate=True)

def _silu(x):
    return jax.nn.silu(x)

def _sigmoid(x):
    return jax.nn.sigmoid(x)

def _layernorm(x, axis=-1, eps=1e-05):
    m = jnp.mean(x, axis=axis, keepdims=True)
    v = jnp.var(x, axis=axis, keepdims=True)
    return (x - m) / jnp.sqrt(v + eps)

def _scatter_add(tgt, idx, src, axis=0):
    return tgt.at[idx].add(src)

def _segment_sum(src, seg, n):
    return jax.ops.segment_sum(src, seg, n)
kernel_name = 'mk_xattn_ffn_d1_seqx_r4_eddcf5'

def setup_inputs(seed: int=0):
    np.random.seed(seed)
    _w = jnp.asarray

    def _rec_inputs():
        import jax
        import jax.numpy as jnp
        _rk = jax.random.key(seed)
        x = -0.000125 + 0.9999 * jax.random.normal(jax.random.fold_in(_rk, 1), (4, 512, 512), jnp.float32)
        _lenS = 512 - jax.random.randint(jax.random.fold_in(_rk, 7), (4,), 0, max(1, 512 // 4) + 1, jnp.int32)
        _lenS2 = 512 - jax.random.randint(jax.random.fold_in(_rk, 8), (4,), 0, max(1, 512 // 4) + 1, jnp.int32)
        itok_BxS_13_99985 = jax.random.randint(jax.random.fold_in(_rk, 11), (4, 512), 13, 99986, jnp.int32)
        _ctx_2048P = jax.random.normal(jax.random.fold_in(_rk, 12), (4, 16, 512), jnp.float32)
        _ctx_2048c = jax.random.dirichlet(jax.random.fold_in(_rk, 512), 0.3 * jnp.ones((16,), jnp.float32), (4, 512))
        _ctx_2048t = jnp.einsum('bsk,bkd->bsd', _ctx_2048c, _ctx_2048P)
        _ctx_2048t = _ctx_2048t * jax.lax.rsqrt(jnp.mean(jnp.square(_ctx_2048t)) + 1e-12) * 0.953939
        ctx_2048 = 6.82029e-06 + 0.0200006 * (_ctx_2048t + 0.3 * jax.random.normal(jax.random.fold_in(_rk, 612), (4, 512, 512), jnp.float32))
        return (x, itok_BxS_13_99985, ctx_2048)
    x, itok_BxS_13_99985, ctx_2048 = _rec_inputs()

    def _L0_xattn_setup():
        import jax, jax.numpy as jnp
        import numpy as np
        B, S, D = (4, 1024, 512)
        E = 4
        F = 2048 // E
        VOCAB = 25000
        key = jax.random.key(seed)
        k1, k2, k3, k4, k5 = jax.random.split(key, 5)
        hidden_states = jax.random.normal(k1, (B, S, D), dtype=jnp.float32)
        token_ids = jax.random.randint(k2, (B, S), 0, VOCAB, dtype=jnp.int64)
        Wg = jax.random.normal(k3, (E, F, D), dtype=jnp.float32) * 0.02
        Wu = jax.random.normal(k4, (E, F, D), dtype=jnp.float32) * 0.02
        Wd = jax.random.normal(k5, (E, D, F), dtype=jnp.float32) * 0.02
        return {'hidden_states': hidden_states, 'token_ids': token_ids, 'Wg': Wg, 'Wu': Wu, 'Wd': Wd}
    _L0_xattn_all = _L0_xattn_setup()
    _L0_xattn_in = {k: v for k, v in _L0_xattn_all.items() if k in ()}
    del _L0_xattn_all

    def _L0_ffn_setup():
        import jax, jax.numpy as jnp
        import numpy as np
        B, S, D = (4, 1024, 512)
        E, K, I, J = (8, 2, 352, 1408)
        CAP_FACTOR = 1.25
        STD = 0.02

        def _moe_routed(x_flat, router, w_up_gate, w_down):
            T, d = x_flat.shape
            logits = jnp.einsum('td,de->te', x_flat, router)
            topk_logits, sel = jax.lax.top_k(logits, K)
            cw = jax.nn.softmax(topk_logits, axis=-1).astype(x_flat.dtype)
            C = int(np.ceil(T * K / E * CAP_FACTOR))
            e_flat = sel.reshape(-1)
            oh = jax.nn.one_hot(e_flat, E, dtype=jnp.int32)
            pos_all = jnp.cumsum(oh, axis=0) - oh
            pos = jnp.take_along_axis(pos_all, e_flat[:, None], axis=1)[:, 0]
            valid = pos < C
            safe_pos = jnp.where(valid, pos, C)
            tok = jnp.repeat(jnp.arange(T), K)
            buf = jnp.zeros((E, C, d), x_flat.dtype).at[e_flat, safe_pos].set(x_flat[tok], mode='drop')
            gate_up = jnp.einsum('ecd,edm->ecm', buf, w_up_gate)
            gate, up = jnp.split(gate_up, [I], axis=-1)
            h = jax.nn.silu(gate) * up
            out_buf = jnp.einsum('eci,eid->ecd', h, w_down)
            gathered = out_buf[e_flat, jnp.minimum(safe_pos, C - 1)]
            gathered = gathered * valid[:, None].astype(x_flat.dtype)
            w = cw.reshape(-1)
            y = jnp.zeros((T, d), x_flat.dtype).at[tok].add(w[:, None] * gathered)
            return y

        def _shared_mlp(x_flat, shared_w_up_gate, shared_w_down):
            gu = jnp.einsum('td,dm->tm', x_flat, shared_w_up_gate)
            gate, up = jnp.split(gu, [J], axis=-1)
            return jnp.einsum('tm,md->td', jax.nn.silu(gate) * up, shared_w_down)
        key = jax.random.key(seed)
        kx, kr, ku, kd, ksu, ksd = jax.random.split(key, 6)
        x = jax.random.normal(kx, (B, S, D), dtype=jnp.float32)
        router = STD * jax.random.truncated_normal(kr, -3, 3, (D, E), dtype=jnp.float32)
        w_up_gate = STD * jax.random.truncated_normal(ku, -3, 3, (E, D, 2 * I), dtype=jnp.float32)
        w_down = STD * jax.random.truncated_normal(kd, -3, 3, (E, I, D), dtype=jnp.float32)
        shared_w_up_gate = STD * jax.random.truncated_normal(ksu, -3, 3, (D, 2 * J), dtype=jnp.float32)
        shared_w_down = STD * jax.random.truncated_normal(ksd, -3, 3, (J, D), dtype=jnp.float32)
        return {'x': x, 'router': router, 'w_up_gate': w_up_gate, 'w_down': w_down, 'shared_w_up_gate': shared_w_up_gate, 'shared_w_down': shared_w_down}
    _L0_ffn_all = _L0_ffn_setup()
    _L0_ffn_in = {k: v for k, v in _L0_ffn_all.items() if k in ('router', 'w_up_gate', 'w_down', 'shared_w_up_gate', 'shared_w_down')}
    del _L0_ffn_all
    return {'x': x, 'itok_BxS_13_99985': itok_BxS_13_99985, 'ctx_2048': ctx_2048, 'L0_ffn_router': _L0_ffn_in['router'], 'L0_ffn_w_up_gate': _L0_ffn_in['w_up_gate'], 'L0_ffn_w_down': _L0_ffn_in['w_down'], 'L0_ffn_shared_w_up_gate': _L0_ffn_in['shared_w_up_gate'], 'L0_ffn_shared_w_down': _L0_ffn_in['shared_w_down']}

def reference(x, itok_BxS_13_99985, ctx_2048, L0_ffn_router, L0_ffn_w_up_gate, L0_ffn_w_down, L0_ffn_shared_w_up_gate, L0_ffn_shared_w_down):
    import jax
    import jax.numpy as jnp

    def _L0_xattn_ref(hidden_states, token_ids, Wg, Wu, Wd):
        import jax, jax.numpy as jnp
        import numpy as np
        B, S, D = (4, 1024, 512)
        E = 4
        F = 2048 // E
        VOCAB = 25000
        tokens_per_expert = VOCAB // E
        tid = jnp.clip(token_ids, 0, VOCAB - 1)
        expert_ids = jnp.minimum(tid // tokens_per_expert, E - 1)
        out = jnp.zeros_like(hidden_states)
        for e in range(E):
            g = jax.nn.silu(jnp.einsum('bsd,fd->bsf', hidden_states, Wg[e]))
            u = jnp.einsum('bsd,fd->bsf', hidden_states, Wu[e])
            y = jnp.einsum('bsf,df->bsd', g * u, Wd[e])
            out = jnp.where((expert_ids == e)[..., None], y, out)
        return out

    def _L0_ffn_ref(x, router, w_up_gate, w_down, shared_w_up_gate, shared_w_down):
        import jax, jax.numpy as jnp
        import numpy as np
        B, S, D = (4, 1024, 512)
        E, K, I, J = (8, 2, 352, 1408)
        CAP_FACTOR = 1.25
        STD = 0.02

        def _moe_routed(x_flat, router, w_up_gate, w_down):
            T, d = x_flat.shape
            logits = jnp.einsum('td,de->te', x_flat, router)
            topk_logits, sel = jax.lax.top_k(logits, K)
            cw = jax.nn.softmax(topk_logits, axis=-1).astype(x_flat.dtype)
            C = int(np.ceil(T * K / E * CAP_FACTOR))
            e_flat = sel.reshape(-1)
            oh = jax.nn.one_hot(e_flat, E, dtype=jnp.int32)
            pos_all = jnp.cumsum(oh, axis=0) - oh
            pos = jnp.take_along_axis(pos_all, e_flat[:, None], axis=1)[:, 0]
            valid = pos < C
            safe_pos = jnp.where(valid, pos, C)
            tok = jnp.repeat(jnp.arange(T), K)
            buf = jnp.zeros((E, C, d), x_flat.dtype).at[e_flat, safe_pos].set(x_flat[tok], mode='drop')
            gate_up = jnp.einsum('ecd,edm->ecm', buf, w_up_gate)
            gate, up = jnp.split(gate_up, [I], axis=-1)
            h = jax.nn.silu(gate) * up
            out_buf = jnp.einsum('eci,eid->ecd', h, w_down)
            gathered = out_buf[e_flat, jnp.minimum(safe_pos, C - 1)]
            gathered = gathered * valid[:, None].astype(x_flat.dtype)
            w = cw.reshape(-1)
            y = jnp.zeros((T, d), x_flat.dtype).at[tok].add(w[:, None] * gathered)
            return y

        def _shared_mlp(x_flat, shared_w_up_gate, shared_w_down):
            gu = jnp.einsum('td,dm->tm', x_flat, shared_w_up_gate)
            gate, up = jnp.split(gu, [J], axis=-1)
            return jnp.einsum('tm,md->td', jax.nn.silu(gate) * up, shared_w_down)
        b, s, d = x.shape
        x_flat = x.reshape(b * s, d)
        routed = _moe_routed(x_flat, router, w_up_gate, w_down)
        shared = _shared_mlp(x_flat, shared_w_up_gate, shared_w_down)
        return (routed + shared).reshape(b, s, d)
    x = x + _L0_xattn_ref(_layernorm(x, axis=-1), itok_BxS_13_99985, ctx_2048, ctx_2048, ctx_2048)
    x = x + _L0_ffn_ref(_layernorm(x, axis=-1), L0_ffn_router, L0_ffn_w_up_gate, L0_ffn_w_down, L0_ffn_shared_w_up_gate, L0_ffn_shared_w_down)
    return x

_drawn_inputs = setup_inputs


def setup_inputs(seed=0):
    import zlib

    import numpy as np

    out = dict(_drawn_inputs(seed))
    spreads = {}
    factors = {}
    for name, (base, spread) in spreads.items():
        noise = np.random.default_rng([zlib.crc32(name.encode()), seed]).standard_normal(out[name].shape)
        drawn = base * np.exp(spread * noise) if base else spread * noise
        out[name] = jnp.asarray(drawn.astype(out[name].dtype))
    for name, factor in factors.items():
        out[name] = (out[name] * factor).astype(out[name].dtype)
    return out
```

```python
from contextlib import ExitStack

import concourse.bass as bass
from concourse import mybir

ALU = mybir.AluOpType
ACT = mybir.ActivationFunctionType
AX = mybir.AxisListType
F32 = mybir.dt.float32
F32R = mybir.dt.float32r
I32 = mybir.dt.int32

P = 128
HI, LO = 0, 1
PASSES = ((LO, HI), (HI, LO), (HI, HI))
EPS = 1e-5


def after(eng, sem, count):
    if not isinstance(count, int) or count > 0:
        eng.wait_ge(sem, count)


def apart(eng, passed):
    eng.sem_inc(passed, 1)


def inside(i, low, high):
    return not isinstance(i, int) or low <= i < high


def routed_block_program(nc, x, ids, ctx_w, router, w_ug, w_dn, sh_ug, sh_dn, out):
    B, S, D = x.shape
    T = B * S
    KD = D // P
    NT = T // P
    EC = ctx_w.shape[0]
    E = w_ug.shape[0]
    I = w_dn.shape[1]
    J = sh_dn.shape[0]
    NJ = J // P
    CAP = -(-T * 2 * 5 // (E * 4))
    CT = CAP // P
    GT = NT + EC - 1
    VOCAB_PART = 25000 // EC
    CH = [P, P, I - 2 * P]
    NC = len(CH)
    rounds = (GT - 4) // 4
    NB = 4
    BT = NT // NB
    N = BT * P
    HALF = [(0, 2), (2, CT)]
    SLOTS = E * CT
    NBLK = NJ * NB
    EARLY = [[], [0, 1], [2, 3], [4]]
    assert D == 512 and N == 512 and CAP == 640 and J % P == 0 and 0 < CH[2] <= P

    xf = x.rearrange("b s d -> (b s) d")
    of = out.rearrange("b s d -> (b s) d")
    x1_rows = nc.dram_tensor("x1_rows", (T, D), F32).ap()
    h2_rows = nc.dram_tensor("h2_rows", (T, D), F32).ap()

    with ExitStack() as ctx:
        def sb(name, shape, dt=F32):
            return ctx.enter_context(nc.sbuf_tensor(name, shape, dt))

        def sem(name):
            return ctx.enter_context(nc.semaphore(name))

        area_a = sb("area_a", [P, 16384], F32R)
        area_b = sb("area_b", [P, 16384], F32R)
        ctx_t = area_a[:, :].rearrange("p (e h k m) -> p e h k m", e=EC, h=2, k=KD)
        h1_t = area_b[:, 0:1024].rearrange("p (h k m) -> p h k m", h=2, k=KD)
        a1_t = area_b[:, 1024:2048].rearrange("p (h k m) -> p h k m", h=2, k=KD)
        pick1 = area_b[:, 2048:4096].rearrange("p (j c) -> p j c", j=NT)
        vals1 = area_b[:, 4096:4096 + NT * 2 * (GT + 1)].rearrange("p (j w c) -> p j w c", j=NT, w=2)
        h2_t = area_b[:, :].rearrange("p (h k n) -> p h k n", h=2, k=KD)
        pick2 = area_a[:, 0:2048].rearrange("p (j c) -> p j c", j=NT)
        vals2 = area_a[:, 2048:2048 + NT * 4 * SLOTS].rearrange("p (j w c) -> p j w c", j=NT, w=4)
        up_w = area_a[:, 0:6144].rearrange("p (c g h k m) -> p c g h k m", c=NC, g=2, h=2, k=KD)
        g_t = area_a[:, 6144:16384].rearrange("p (b h k n) -> p b h k n", b=2, h=2, k=KD)
        a2_t = area_a[:, 11264:13312].rearrange("p (b h n) -> p b h n", b=2, h=2)
        sh_d = area_a[:, 13312:14336].rearrange("p (h n) -> p h n", h=2)
        sh_u = area_a[:, 14336:16384].rearrange("p (g h k m) -> p g h k m", g=2, h=2, k=KD)
        dn_w = area_b[:, 0:6144].rearrange("p (b c h n) -> p b c h n", b=2, c=NC, h=2)
        a3_t = area_b[:, 6144:9984].rearrange("p (c h n) -> p c h n", c=NC, h=2)
        rt_w = sb("rt_w", [P, KD, 2, E], F32R)

        acc = sb("acc", [P, NT, D])
        ctx_raw = acc[:, :, :].rearrange("p (e r) d -> p e r d", e=EC)
        out_new = acc
        raw_u = sb("raw_u", [P, 2, 2, KD, P])
        raw_d = sb("raw_d", [P, 2, D])
        gated = sb("gated", [P, 2, D])
        rows = sb("rows", [P, 9 * D])
        x_in = rows[:, 0:4 * D].rearrange("p (s d) -> p s d", s=4)
        h1 = rows[:, 4 * D:5 * D]
        x1 = rows[:, 5 * D:7 * D].rearrange("p (s d) -> p s d", s=2)
        h2 = rows[:, 7 * D:9 * D].rearrange("p (s d) -> p s d", s=2)
        h2_in = rows[:, 0:8 * D].rearrange("p (s r d) -> p s r d", s=2, r=BT)
        g_in = rows[:, 0:CT * D].rearrange("p (s d) -> p s d", s=CT)

        ident = sb("ident", [P, P])
        ones = sb("ones", [P, P])
        below = sb("below", [P, P])
        lane = sb("lane", [P, P])
        tok_pj = sb("tok_pj", [P, NT])
        tok_tp = sb("tok_tp", [P, NT])
        descend = sb("descend", [P, E])
        slot0 = sb("slot0", [P, E])
        expo = sb("expo", [P, 1])
        rt_raw = sb("rt_raw", [P, KD, E])
        ids_i = sb("ids_i", [P, NT], I32)
        ids_f = sb("ids_f", [P, NT])
        eid = sb("eid", [P, NT])
        member1 = sb("member1", [P, EC, NT])
        run1 = sb("run1", [P, EC, NT])
        tiles_i = sb("tiles_i", [P, EC], I32)
        tiles_f = sb("tiles_f", [P, EC])
        tile_end = sb("tile_end", [P, EC + 1])
        base_row = sb("base_row", [P, EC])
        slot_f = sb("slot_f", [P, NT])
        slot_i = sb("slot_i", [P, NT], I32)
        lane_i = sb("lane_i", [P, NT], I32)
        col_i = sb("col_i", [P, NT], I32)
        lane_f = sb("lane_f", [P, NT])
        col_f = sb("col_f", [P, NT])
        tile_e = sb("tile_e", [P, GT + 1])
        tile_ei = sb("tile_ei", [P, GT + 1], I32)
        put1_f = sb("put1_f", [P, GT + 1])
        put1 = sb("put1", [P, GT + 1], I32)
        get1 = sb("get1", [P, GT + 1], I32)
        get_now = sb("get_now", [P, 4], I32)
        put_now = sb("put_now", [P, 2], I32)
        part1, part2 = sb("part1", [P, 6]), sb("part2", [P, 6])
        mv1, mv2 = sb("mv1", [P, 2]), sb("mv2", [P, 2])
        ve1, ve2 = sb("ve1", [P, 1]), sb("ve2", [P, 1])
        rstd1, rstd2 = sb("rstd1", [P, 1]), sb("rstd2", [P, 1])
        logit = sb("logit", [P, NT, E])
        cand = sb("cand", [P, NT, E])
        top = sb("top", [P, 2, NT])
        first = sb("first", [P, NT])
        hot = sb("hot", [P, 2, NT, E])
        member2 = sb("member2", [P, NT, E])
        run2 = sb("run2", [P, NT, E])
        late = sb("late", [P, NT, E])
        gap = sb("gap", [P, NT])
        exp_gap = sb("exp_gap", [P, NT])
        weight = sb("weight", [P, 2, NT])
        w_hl = sb("w_hl", [P, 2, NT], F32R)
        put2_f = sb("put2_f", [P, SLOTS])
        put2 = sb("put2", [P, SLOTS], I32)
        get2 = sb("get2", [P, SLOTS], I32)
        slot_w = sb("slot_w", [P, SLOTS])
        g_idx = sb("g_idx", [P, CT], I32)
        o_idx = sb("o_idx", [P, CT], I32)
        p_idx = sb("p_idx", [P, CT], I32)

        ps = ctx.enter_context(nc.psum_tensor("ps", [P, 8, 512], F32))

        s_const = sem("const_ready")
        s_passed = [sem(f"waits_passed_{who}") for who in ("dve", "pool", "sp")]
        s_ids = sem("ids_landed")
        s_ctx = [sem(f"ctx{e}_landed") for e in range(EC)]
        s_rt = sem("router_landed")
        s_rt_hi, s_rt_lo = sem("router_hi"), sem("router_lo")
        s_v = sem("dve_table_step")
        s_mem1, s_cnt1 = sem("member1_ready"), sem("counts1_ready")
        s_pick1, s_perm1, s_tab1 = sem("pick1_ready"), sem("perm1_ready"), sem("table1_ready")
        s_ct, s_cth, s_ctl = sem("ctx_transposed"), sem("ctx_hi"), sem("ctx_lo")
        s_idx = sem("index_column_staged")
        s_get, s_put1 = sem("get_column_staged"), sem("put_column_staged")
        s_xin = [sem(f"x_rows_landed{c}") for c in range(4)]
        s_xout = [sem(f"x1_rows_stored{c}") for c in range(2)]
        s_hout = [sem(f"h2_rows_stored{c}") for c in range(2)]
        s_part1, s_st1, s_ve1, s_rs1, s_h1 = (sem("part1_ready"), sem("stats1_ready"), sem("vareps1_ready"),
                                              sem("rstd1_ready"), sem("h1_ready"))
        s_part2, s_st2, s_ve2, s_rs2, s_h2 = (sem("part2_ready"), sem("stats2_ready"), sem("vareps2_ready"),
                                              sem("rstd2_ready"), sem("h2_ready"))
        s_t1, s_hi1, s_lo1 = sem("h1_transposed"), sem("h1_hi"), sem("h1_lo")
        s_m1, s_sl1, s_a1 = sem("z_ready"), sem("silu1_ready"), sem("a1_ready")
        s_t2, s_hi2, s_lo2 = sem("a1_transposed"), sem("a1_hi"), sem("a1_lo")
        s_m2, s_x1 = sem("y1_ready"), sem("x1_ready")
        s_hin = [sem(f"h2_block_landed{k}") for k in range(2)]
        s_yin = sem("x1_block_landed")
        s_tt, s_tth, s_ttl = sem("h2_transposed"), sem("h2_hi"), sem("h2_lo")
        s_raw = sem("weights_landed")
        s_uh, s_ul, s_dh, s_dl = sem("up_w_hi"), sem("up_w_lo"), sem("down_w_hi"), sem("down_w_lo")
        s_g, s_u, s_sl, s_mul = sem("gate_ready"), sem("up_ready"), sem("silu2_ready"), sem("gated2_ready")
        s_ah, s_al = sem("a2_hi"), sem("a2_lo")
        s_dn, s_add = sem("down_ready"), sem("acc_added")
        s_lg, s_mem2, s_cnt2 = sem("logits_ready"), sem("member2_ready"), sem("counts2_ready")
        s_gap, s_exp = sem("gap_ready"), sem("exp_ready")
        s_pick2, s_perm2, s_tab2 = sem("pick2_ready"), sem("perm2_ready"), sem("table2_ready")
        s_out = sem("output_written")
        s_gin = [sem(f"g_rows_landed{t}") for t in range(CT)]
        s_oin = [sem(f"out_rows_landed{t}") for t in range(CT)]
        s_t3, s_th3, s_tl3 = sem("g_transposed"), sem("g_hi"), sem("g_lo")
        s_g3, s_u3, s_sl3, s_mul3 = sem("gate3_ready"), sem("up3_ready"), sem("silu3_ready"), sem("gated3_ready")
        s_ah3, s_al3, s_d3, s_y3 = sem("a3_hi"), sem("a3_lo"), sem("down3_ready"), sem("rows3_ready")
        s_put = sem("rows3_stored")

        block = ctx.enter_context(nc.Block())

        @block.sync
        def _(sp):
            def hold(sem, count):
                after(sp, sem, count)
                if not isinstance(count, int):
                    apart(sp, s_passed[2])

            def load_shared(q):
                hold(s_raw, q * 48)
                hold(s_ul, (q - 1) * 2)
                hold(s_dl, q - 1)
                for g in range(2):
                    sp.dma_start(raw_u[:, q % 2, g],
                                 sh_ug.rearrange("(k p) m -> p k m", p=P)[:, :, bass.ds(q * P + g * J, P)]
                                 ).then_inc(s_raw, 16)
                sp.dma_start(raw_d[:, q % 2], sh_dn.rearrange("(j p) d -> j p d", p=P)[q]).then_inc(s_raw, 16)

            def load_expert(e, c):
                q = NJ + e * NC + c
                hold(s_raw, q * 48)
                hold(s_ul, (q - 1) * 2)
                hold(s_dl, q - 1)
                for g in range(2):
                    sp.dma_start(raw_u[:, q % 2, g, :, 0:CH[c]],
                                 w_ug.rearrange("e (k p) m -> e p k m", p=P)[e, :, :, g * I + c * P:g * I + c * P + CH[c]]
                                 ).then_inc(s_raw, 16)
                sp.dma_start(raw_d[0:CH[c], q % 2], w_dn[e, c * P:c * P + CH[c], :]).then_inc(s_raw, 16)

            sp.dma_start(ids_i[:, :], ids.rearrange("b (p j) -> (b p) j", j=NT)).then_inc(s_ids, 16)
            for e in range(EC):
                sp.dma_start(ctx_raw[:, e], ctx_w[e].rearrange("(r p) d -> p r d", p=P)).then_inc(s_ctx[e], 16)
            sp.dma_start(rt_raw[:, :, :], router.rearrange("(k p) e -> p k e", p=P)).then_inc(s_rt, 16)
            load_shared(0)
            load_shared(1)
            for c in range(2):
                hold(s_xout[c], 16 * ((GT + 1 - c) // 2))
                hold(s_hout[c], 16 * ((GT + 1 - c) // 2))
            for b in range(NB):
                if b >= 2:
                    hold(s_tt, (b - 1) * KD)
                sp.dma_start(h2_in[:, b % 2], h2_rows[b * N:(b + 1) * N, :].rearrange("(r p) d -> p r d", p=P)
                             ).then_inc(s_hin[b % 2], 16)
                if b >= 1:
                    hold(s_yin, 16 * b)
                sp.dma_start(acc[:, b * BT:(b + 1) * BT, :],
                             x1_rows[b * N:(b + 1) * N, :].rearrange("(r p) d -> p r d", p=P)).then_inc(s_yin, 16)
            with sp.Fori(2, NJ) as q:
                load_shared(q)
            load_expert(0, 0)
            load_expert(0, 1)
            for b in range(NB):
                hold(s_add, (NBLK - NB + b + 1) * BT)
                sp.dma_start(of[b * N:(b + 1) * N, :].rearrange("(r p) d -> p r d", p=P),
                             acc[:, b * BT:(b + 1) * BT, :]).then_inc(s_out, 16)
            load_expert(0, 2)
            with sp.Fori(1, E) as e:
                for c in range(NC):
                    load_expert(e, c)
            hold(s_out, 16 * NB)

        @block.gpsimd
        def _(pool):
            def hold(sem, count):
                after(pool, sem, count)
                if not isinstance(count, int):
                    apart(pool, s_passed[1])

            pool.memset(ident[:, :], 0.0).then_inc(s_const, 1)
            pool.memset(ones[:, :], 1.0).then_inc(s_const, 1)
            pool.memset(below[:, :], 1.0).then_inc(s_const, 1)
            pool.memset(expo[:, :], -0.5).then_inc(s_const, 1)
            pool.iota(lane[:, :], pattern=[[1, P]], base=0, channel_multiplier=0,
                      allow_small_or_imprecise_dtypes=True).then_inc(s_const, 1)
            pool.iota(tok_pj[:, :], pattern=[[1, NT]], base=0, channel_multiplier=NT,
                      allow_small_or_imprecise_dtypes=True).then_inc(s_const, 1)
            pool.wait_ge(s_const, 6)
            pool.affine_select(out=ident[:, :], in_=ident[:, :], compare_op=ALU.not_equal, fill=1.0, base=0,
                               pattern=[[-1, P]], channel_multiplier=1).then_inc(s_const, 1)
            pool.affine_select(out=below[:, :], in_=below[:, :], compare_op=ALU.is_gt, fill=0.0, base=0,
                               pattern=[[1, P]], channel_multiplier=-1).then_inc(s_const, 1)
            pool.iota(tok_tp[:, :], pattern=[[P, NT]], base=0, channel_multiplier=1,
                      allow_small_or_imprecise_dtypes=True).then_inc(s_const, 1)
            pool.iota(descend[:, :], pattern=[[-1, E]], base=E, channel_multiplier=0,
                      allow_small_or_imprecise_dtypes=True).then_inc(s_const, 1)
            pool.iota(slot0[:, :], pattern=[[CAP, E]], base=0, channel_multiplier=0,
                      allow_small_or_imprecise_dtypes=True).then_inc(s_const, 1)

            def gather(k, q, c):
                hold(s_x1, k - 3)
                pool.tensor_copy(get_now[:, c:c + 1], get1[:, bass.ds(k, 1)]).then_inc(s_get, 1)
                hold(s_get, k + 1)
                pool.indirect_dma_start(x_in[:, c], None, xf,
                                        bass.IndirectOffsetOnAxis(ap=get_now[:, c:c + 1], axis=0),
                                        bounds_check=T - 1, oob_is_err=False).then_inc(s_xin[c], 16)

            def scatter_x(k, c, before):
                hold(s_xout[c], 16 * before)
                hold(s_hout[c], 16 * before)
                pool.tensor_copy(put_now[:, c:c + 1], put1[:, bass.ds(k, 1)]).then_inc(s_put1, 1)
                hold(s_put1, k + 1)
                hold(s_x1, k + 1)
                pool.indirect_dma_start(x1_rows, bass.IndirectOffsetOnAxis(ap=put_now[:, c:c + 1], axis=0),
                                        x1[:, c], None, bounds_check=T - 1, oob_is_err=False).then_inc(s_xout[c], 16)

            def scatter_h(k, c):
                hold(s_h2, k + 1)
                pool.indirect_dma_start(h2_rows, bass.IndirectOffsetOnAxis(ap=put_now[:, c:c + 1], axis=0),
                                        h2[:, c], None, bounds_check=T - 1, oob_is_err=False).then_inc(s_hout[c], 16)

            def root(st, mv, ve, s_ve, rstd, s_rs, k):
                hold(st, k + 1)
                pool.tensor_scalar(ve[:, :], mv[:, 1:2], EPS, 1.0, ALU.add, ALU.mult).then_inc(s_ve, 1)
                hold(s_ve, k + 1)
                pool.tensor_tensor(rstd[:, :], ve[:, :], expo[:, :], ALU.pow).then_inc(s_rs, 1)

            def pool_step(i, q, c):
                if inside(i, 0, GT - 4):
                    gather(i + 4, q + 1, c)
                if inside(i, 0, GT):
                    scatter_x(i, c % 2, 2 * q + c // 2)
                    root(s_st2, mv2, ve2, s_ve2, rstd2, s_rs2, i)
                    scatter_h(i, c % 2)
                if inside(i, -4, GT - 4):
                    root(s_st1, mv1, ve1, s_ve1, rstd1, s_rs1, i + 4)

            pool.wait_ge(s_tab1, 1)
            for k in range(4):
                gather(k, 0, k)
            for i in range(-4, 4):
                pool_step(i, i // 4, i % 4)
            with pool.Fori(1, rounds) as q:
                for c in range(4):
                    pool_step(4 * q + c, q, c)
            for i in range(4 * rounds, GT):
                pool_step(i, i // 4, i % 4)

            def gather_g(e):
                for t in range(CT):
                    hold(s_gin[t], 16 * e)
                pool.tensor_copy(g_idx[:, :], get2[:, bass.ds(e * CT, CT)]).then_inc(s_idx, 1)
                hold(s_idx, (1 if isinstance(e, int) and e == 0 else e * 3 - 1))
                for t in range(CT):
                    hold(s_t3, (e - 1) * CT + t + 1)
                    pool.indirect_dma_start(g_in[:, t], None, h2_rows,
                                            bass.IndirectOffsetOnAxis(ap=g_idx[:, t:t + 1], axis=0),
                                            bounds_check=T - 1, oob_is_err=False).then_inc(s_gin[t], 16)

            def gather_out(e, more):
                hold(s_put, 16 * CT * e)
                staged = e * 3 + (4 if more else 3)
                pool.tensor_copy(o_idx[:, :], get2[:, bass.ds(e * CT, CT)]).then_inc(s_idx, 1)
                pool.tensor_copy(p_idx[:, :], put2[:, bass.ds(e * CT, CT)]).then_inc(s_idx, 1)
                hold(s_idx, staged)
                for t in range(CT):
                    pool.indirect_dma_start(out_new[:, t], None, of,
                                            bass.IndirectOffsetOnAxis(ap=o_idx[:, t:t + 1], axis=0),
                                            bounds_check=T - 1, oob_is_err=False).then_inc(s_oin[t], 16)
                for t in range(CT):
                    hold(s_oin[t], 16 * (e + 1))

            def store_out(e, t):
                hold(s_y3, e * CT + t + 1)
                pool.indirect_dma_start(of, bass.IndirectOffsetOnAxis(ap=p_idx[:, t:t + 1], axis=0),
                                        out_new[:, t], None, bounds_check=T - 1, oob_is_err=False).then_inc(s_put, 16)

            def pool_expert(e, first, last):
                if not last:
                    gather_g(e + 1)
                if not first:
                    for t in range(HALF[1][0], CT):
                        store_out(e - 1, t)
                gather_out(e, not last)
                for t in range(*HALF[0]):
                    store_out(e, t)

            pool.wait_ge(s_tt, NB * KD)
            pool.wait_ge(s_tab2, 1)
            gather_g(0)
            pool.wait_ge(s_out, 16 * NB)
            pool_expert(0, True, False)
            with pool.Fori(1, E - 1) as e:
                pool_expert(e, False, False)
            pool_expert(E - 1, False, True)
            for t in range(HALF[1][0], CT):
                store_out(E - 1, t)
            pool.wait_ge(s_put, 16 * SLOTS)

        @block.scalar
        def _(act):
            def copy_hi(dst, src, signal):
                act.activation(dst, src, ACT.Copy).then_inc(signal, 1)

            act.wait_ge(s_rt, 16)
            copy_hi(rt_w[:, :, HI, :], rt_raw[:, :, :], s_rt_hi)
            for n in range(EC * 2):
                e, k = n // 2, n % 2 * 2
                act.wait_ge(s_ct, n + 1)
                copy_hi(ctx_t[:, e, HI, k:k + 2, :], ps[:, 2 * (n % 2):2 * (n % 2) + 2, :], s_cth)

            def act_step(i):
                if inside(i, 0, GT):
                    after(act, s_t2, i + 1)
                    copy_hi(a1_t[:, HI], ps[:, 1, :].rearrange("p (k m) -> p k m", k=KD), s_hi2)
                if inside(i, -1, GT - 1):
                    after(act, s_m1, i + 2)
                    act.activation(gated[:, 0], ps[:, 2, :], ACT.Silu).then_inc(s_sl1, 1)
                if inside(i, -2, GT - 2):
                    after(act, s_t1, i + 3)
                    copy_hi(h1_t[:, HI], ps[:, 0, :].rearrange("p (k m) -> p k m", k=KD), s_hi1)

            for i in range(-2, 0):
                act_step(i)
            with act.Fori(0, GT - 2) as i:
                act_step(i)
            for i in range(GT - 2, GT):
                act_step(i)

            def hi_up_shared(j, g):
                after(act, s_raw, 48 * (j + 1))
                after(act, s_g if g == 0 else s_u, j * NB)
                copy_hi(sh_u[:, g, HI], raw_u[:, j % 2, g], s_uh)

            def hi_down_shared(j):
                after(act, s_raw, 48 * (j + 1))
                after(act, s_dn, j * NB * BT)
                copy_hi(sh_d[:, HI], raw_d[:, j % 2], s_dh)

            def hi_expert_up(e, c):
                q = NJ + e * NC + c
                after(act, s_raw, 48 * (q + 1))
                after(act, s_u3, (e - 1) * 6 + 4 + c)
                for g in range(2):
                    copy_hi(up_w[:, c, g, HI, :, 0:CH[c]], raw_u[:, q % 2, g, :, 0:CH[c]], s_uh)

            def hi_expert_down(e, c):
                q = NJ + e * NC + c
                after(act, s_d3, (e - 1) * CT)
                copy_hi(dn_w[0:CH[c], e % 2, c, HI], raw_d[0:CH[c], q % 2], s_dh)

            def hi_h2(u):
                act.wait_ge(s_tt, u + 1)
                copy_hi(h2_t[:, HI, u % KD, u // KD * N:(u // KD + 1) * N], ps[:, 6 + u % 2, :], s_tth)

            def act_block(j, b, last):
                n = j * NB + b
                after(act, s_g, n + 1)
                after(act, s_al, n - 1)
                act.activation(gated[:, b % 2], ps[:, 0, :], ACT.Silu).then_inc(s_sl, 1)
                if b == NB - 1 and not last:
                    hi_up_shared(j + 1, 0)
                    hi_up_shared(j + 1, 1)
                after(act, s_mul, n + 1)
                after(act, s_dn, (n - 1) * BT)
                copy_hi(a2_t[:, b % 2, HI], gated[:, b % 2], s_ah)
                if b == 0:
                    hi_down_shared(j)

            act.wait_ge(s_m2, GT)
            hi_up_shared(0, 0)
            hi_up_shared(0, 1)
            for u in range(KD):
                hi_h2(u)
            for j in range(4):
                for b in range(NB):
                    act_block(j, b, False)
                    n = j * NB + b
                    for u in range((n + 1) * KD, min(n + 2, NB) * KD):
                        hi_h2(u)
                    if n == 8:
                        act.wait_ge(s_gap, 1)
                        act.activation(exp_gap[:, :], gap[:, :], ACT.Exp).then_inc(s_exp, 1)
            with act.Fori(4, NJ - 1) as j:
                for b in range(NB):
                    act_block(j, b, False)

            def hi_g(e, t):
                w = e * CT + t
                after(act, s_t3, w + 1)
                after(act, s_u3, (e - 1) * 6)
                copy_hi(g_t[:, e % 2, HI, :, t * P:(t + 1) * P],
                        ps[:, 6 + t % 2, :].rearrange("p (k m) -> p k m", k=KD), s_th3)

            def act_unit(e, u):
                h, c = u // NC, u % NC
                v, m, t0, t1 = e * 6 + u, CH[c], HALF[h][0], HALF[h][1]
                n = (t1 - t0) * P
                after(act, s_g3, v + 1)
                after(act, s_al3, v - 1)
                act.activation(gated[0:m, u % 2, 0:n], ps[0:m, 0, 0:n], ACT.Silu).then_inc(s_sl3, 1)
                after(act, s_mul3, v + 1)
                after(act, s_d3, (e - 1) * CT + t1)
                copy_hi(a3_t[0:m, c, HI, t0 * P:t1 * P], gated[0:m, u % 2, 0:n], s_ah3)

            act.wait_ge(s_perm2, 2)
            for b in range(NB):
                act_block(NJ - 1, b, True)
                if b < 2:
                    hi_expert_up(0, b)
                for t in EARLY[b]:
                    hi_g(0, t)
            act.wait_ge(s_u, NBLK)
            hi_expert_down(0, 0)
            hi_expert_down(0, 1)
            hi_expert_up(0, 2)
            hi_expert_down(0, 2)
            act.wait_ge(s_dn, NBLK * BT)

            def act_expert(e, last):
                for u in range(6):
                    act_unit(e, u)
                    if not last:
                        if u < 3:
                            hi_g(e + 1, u)
                        if u == 4:
                            hi_g(e + 1, 3)
                        if u == 5:
                            hi_g(e + 1, 4)
                        if u >= 3:
                            hi_expert_up(e + 1, u - 3)
                            hi_expert_down(e + 1, u - 3)

            act_expert(0, False)
            with act.Fori(1, E - 1) as e:
                act_expert(e, False)
            act_expert(E - 1, True)

        @block.vector
        def _(dve):
            steps = [0]

            def link(ins):
                steps[0] += 1
                ins.then_inc(s_v, 1)
                dve.wait_ge(s_v, steps[0])

            def copy_lo(dst, src, hi, signal):
                dve.tensor_tensor(dst, src, hi.bitcast(F32), ALU.subtract).then_inc(signal, 1)

            def running_sum(dst, counts, ones_row):
                dve.tensor_tensor_scan(dst, ones_row, counts, 0.0, ALU.mult, ALU.add)

            def slot_parts():
                link(dve.tensor_copy(slot_i[:, :], slot_f[:, :]))
                link(dve.tensor_single_scalar(lane_i[:, :], slot_i[:, :], P - 1, ALU.bitwise_and))
                link(dve.tensor_single_scalar(col_i[:, :], slot_i[:, :], 7, ALU.arith_shift_right))
                link(dve.tensor_copy(lane_f[:, :], lane_i[:, :]))
                link(dve.tensor_copy(col_f[:, :], col_i[:, :]))

            dve.wait_ge(s_ids, 16)
            link(dve.tensor_copy(ids_f[:, :], ids_i[:, :]))
            link(dve.tensor_scalar(eid[:, :], ids_f[:, :], float(VOCAB_PART), None, ALU.is_ge))
            for e in range(2, EC):
                link(dve.scalar_tensor_tensor(out=eid[:, :], in0=ids_f[:, :], scalar=float(VOCAB_PART * e),
                                              in1=eid[:, :], op0=ALU.is_ge, op1=ALU.add))
            for e in range(EC):
                dve.tensor_scalar(member1[:, e], eid[:, :], float(e), None, ALU.is_equal).then_inc(s_mem1, 1)
            dve.wait_ge(s_cnt1, 1)
            dve.wait_ge(s_const, 11)
            within = ps[:, 4, 0:EC * NT].rearrange("p (e j) -> p e j", e=EC)
            totals = ps[:, 5, 0:EC * NT].rearrange("p (e j) -> p e j", e=EC)
            for e in range(EC):
                link(dve.tensor_tensor_scan(run1[:, e], ones[:, 0:NT], totals[:, e], 0.0, ALU.mult, ALU.add))
            link(dve.tensor_scalar(tiles_f[:, :], run1[:, :, NT - 1], float(P - 1), None, ALU.add))
            link(dve.tensor_copy(tiles_i[:, :], tiles_f[:, :]))
            link(dve.tensor_single_scalar(tiles_i[:, :], tiles_i[:, :], 7, ALU.arith_shift_right))
            link(dve.tensor_copy(tiles_f[:, :], tiles_i[:, :]))
            link(dve.memset(tile_end[:, 0:1], 0.0))
            link(dve.tensor_tensor_scan(tile_end[:, 1:EC + 1], ones[:, 0:EC], tiles_f[:, :], 0.0, ALU.mult, ALU.add))
            link(dve.tensor_scalar(base_row[:, :], tile_end[:, 0:EC], float(P), None, ALU.mult))
            link(dve.tensor_tensor(run1[:, :, :], run1[:, :, :], totals, ALU.subtract))
            link(dve.tensor_tensor(run1[:, :, :], run1[:, :, :], within, ALU.add))
            link(dve.tensor_tensor(run1[:, :, :], run1[:, :, :],
                                   base_row[:, :].unsqueeze(2).to_broadcast([P, EC, NT]), ALU.add))
            link(dve.tensor_tensor(run1[:, :, :], run1[:, :, :], member1[:, :, :], ALU.mult))
            link(dve.tensor_reduce(slot_f[:, :], run1[:, :, :].rearrange("p e j -> p j e"), AX.X, ALU.add))
            slot_parts()
            dve.tensor_tensor(pick1[:, :, :], lane[:, :].unsqueeze(1).to_broadcast([P, NT, P]),
                              lane_f[:, :].unsqueeze(2).to_broadcast([P, NT, P]), ALU.is_equal).then_inc(s_pick1, 1)
            G = GT + 1
            link(dve.tensor_tensor(vals1[:, :, 1, :], lane[:, 0:G].unsqueeze(1).to_broadcast([P, NT, G]),
                                   col_f[:, :].unsqueeze(2).to_broadcast([P, NT, G]), ALU.is_equal))
            dve.tensor_tensor(vals1[:, :, 0, :], vals1[:, :, 1, :].bitcast(F32),
                              tok_pj[:, :].unsqueeze(2).to_broadcast([P, NT, G]), ALU.mult).then_inc(s_pick1, 1)
            link(dve.tensor_scalar(tile_e[:, :], lane[:, 0:G], tile_end[:, 1:2], None, ALU.is_ge))
            for e in range(2, EC):
                link(dve.scalar_tensor_tensor(out=tile_e[:, :], in0=lane[:, 0:G], scalar=tile_end[:, e:e + 1],
                                              in1=tile_e[:, :], op0=ALU.is_ge, op1=ALU.add))
            link(dve.tensor_copy(tile_ei[:, :], tile_e[:, :]))
            dve.wait_ge(s_perm1, 1)
            found = ps[:, 6, 0:2 * G].rearrange("p (w c) -> p w c", w=2)
            link(dve.tensor_scalar(put1_f[:, :], found[:, 1], -float(T), float(T), ALU.mult, ALU.add))
            link(dve.tensor_tensor(put1_f[:, :], put1_f[:, :], found[:, 0], ALU.add))
            link(dve.tensor_copy(put1[:, :], put1_f[:, :]))
            link(dve.tensor_scalar(get1[:, :], put1_f[:, :], float(T - 1), None, ALU.min))
            dve.memset(ve1[:, :], 0.0).then_inc(s_tab1, 1)

            for n in range(EC * 2):
                e, k = n // 2, n % 2 * 2
                dve.wait_ge(s_cth, n + 1)
                copy_lo(ctx_t[:, e, LO, k:k + 2, :], ps[:, 2 * (n % 2):2 * (n % 2) + 2, :],
                        ctx_t[:, e, HI, k:k + 2, :], s_ctl)
            dve.wait_ge(s_rt_hi, 1)
            copy_lo(rt_w[:, :, LO, :], rt_raw[:, :, :], rt_w[:, :, HI, :], s_rt_lo)

            def stats(src, part, s_part, mv, s_st, k):
                apart(dve, s_passed[0])
                dve.bn_stats(part[:, :], src).then_inc(s_part, 1)
                after(dve, s_part, k + 1)
                apart(dve, s_passed[0])
                dve.bn_aggr(mv[:, :], part[:, :]).then_inc(s_st, 1)

            def stats_x(k, q, c):
                after(dve, s_xin[c], 16 * (q + 1))
                after(dve, s_h1, k)
                stats(x_in[:, c], part1, s_part1, mv1, s_st1, k)

            def norm_x(k, c):
                after(dve, s_rs1, k + 1)
                after(dve, s_t1, k)
                dve.tensor_scalar(h1, x_in[:, c], mv1[:, 0:1], rstd1[:, 0:1],
                                  ALU.subtract, ALU.mult).then_inc(s_h1, 1)

            def lo_h1(k):
                after(dve, s_hi1, k + 1)
                copy_lo(h1_t[:, LO], ps[:, 0, :].rearrange("p (k m) -> p k m", k=KD), h1_t[:, HI], s_lo1)

            def dve_step(i, q, c):
                if inside(i, 0, GT):
                    after(dve, s_m2, i + 1)
                    after(dve, s_xout[c % 2], 16 * (2 * q + c // 2))
                    dve.tensor_tensor(x1[:, c % 2], x_in[:, c], ps[:, 3, :], ALU.add).then_inc(s_x1, 1)
                if inside(i, -3, GT - 3):
                    norm_x(i + 3, (c + 3) % 4)
                if inside(i, -1, GT - 1):
                    after(dve, s_hi2, i + 2)
                    copy_lo(a1_t[:, LO], ps[:, 1, :].rearrange("p (k m) -> p k m", k=KD), a1_t[:, HI], s_lo2)
                if inside(i, 0, GT):
                    after(dve, s_x1, i + 1)
                    after(dve, s_h2, i)
                    stats(x1[:, c % 2], part2, s_part2, mv2, s_st2, i)
                if inside(i, -2, GT - 2):
                    after(dve, s_sl1, i + 3)
                    dve.tensor_tensor(gated[:, 0], gated[:, 0], ps[:, 2, :],
                                      ALU.mult).then_inc(s_a1, 1)
                if inside(i, -3, GT - 3):
                    lo_h1(i + 3)
                if inside(i, 0, GT):
                    after(dve, s_rs2, i + 1)
                    after(dve, s_hout[c % 2], 16 * (2 * q + c // 2))
                    dve.tensor_scalar(h2[:, c % 2], x1[:, c % 2], mv2[:, 0:1], rstd2[:, 0:1],
                                      ALU.subtract, ALU.mult).then_inc(s_h2, 1)
                if inside(i, -4, GT - 4):
                    stats_x(i + 4, q + 1, c)

            for i in range(-4, 4):
                dve_step(i, i // 4, i % 4)
            with dve.Fori(1, rounds) as q:
                for c in range(4):
                    dve_step(4 * q + c, q, c)
            for i in range(4 * rounds, GT):
                dve_step(i, i // 4, i % 4)

            def lo_up_shared(j, g):
                after(dve, s_uh, j * 2 + g + 1)
                copy_lo(sh_u[:, g, LO], raw_u[:, j % 2, g], sh_u[:, g, HI], s_ul)

            def lo_down_shared(j):
                after(dve, s_dh, j + 1)
                copy_lo(sh_d[:, LO], raw_d[:, j % 2], sh_d[:, HI], s_dl)

            def lo_expert_up(e, c):
                q = NJ + e * NC + c
                for g in range(2):
                    after(dve, s_uh, q * 2 + g + 1)
                    copy_lo(up_w[:, c, g, LO, :, 0:CH[c]], raw_u[:, q % 2, g, :, 0:CH[c]],
                            up_w[:, c, g, HI, :, 0:CH[c]], s_ul)

            def lo_expert_down(e, c):
                q = NJ + e * NC + c
                after(dve, s_dh, q + 1)
                copy_lo(dn_w[0:CH[c], e % 2, c, LO], raw_d[0:CH[c], q % 2], dn_w[0:CH[c], e % 2, c, HI], s_dl)

            def lo_h2(u):
                dve.wait_ge(s_tth, u + 1)
                cols = slice(u // KD * N, (u // KD + 1) * N)
                copy_lo(h2_t[:, LO, u % KD, cols], ps[:, 6 + u % 2, :], h2_t[:, HI, u % KD, cols], s_ttl)

            def add_down(j, b, t):
                after(dve, s_dn, (j * NB + b) * BT + t + 1)
                y = acc[:, b * BT + t, :]
                dve.tensor_tensor(y, y, ps[:, 2 + t, :], ALU.add).then_inc(s_add, 1)

            def dve_block(j, b, first, last):
                n = j * NB + b
                jp, bp = (j, b - 1) if b else (j - 1, NB - 1)
                if b == NB - 1 and not last:
                    lo_up_shared(j + 1, 0)
                after(dve, s_sl, n + 1)
                after(dve, s_u, n + 1)
                dve.tensor_tensor(gated[:, b % 2], gated[:, b % 2], ps[:, 1, :], ALU.mult).then_inc(s_mul, 1)
                if b == NB - 1 and not last:
                    lo_up_shared(j + 1, 1)
                if not first:
                    add_down(jp, bp, 0)
                    add_down(jp, bp, 1)
                after(dve, s_ah, n + 1)
                copy_lo(a2_t[:, b % 2, LO], gated[:, b % 2], a2_t[:, b % 2, HI], s_al)
                if not first:
                    add_down(jp, bp, 2)
                    add_down(jp, bp, 3)
                if b == 0:
                    lo_down_shared(j)

            over_e = [P, NT, E]

            def choose(k):
                link(dve.tensor_reduce(top[:, k], cand[:, :, :], AX.X, ALU.max))
                link(dve.tensor_tensor(hot[:, k], cand[:, :, :], top[:, k].unsqueeze(2).to_broadcast(over_e), ALU.is_equal))
                link(dve.tensor_tensor(hot[:, k], hot[:, k], descend[:, :].unsqueeze(1).to_broadcast(over_e), ALU.mult))
                link(dve.tensor_reduce(first[:, :], hot[:, k], AX.X, ALU.max))
                link(dve.tensor_tensor(hot[:, k], descend[:, :].unsqueeze(1).to_broadcast(over_e),
                                       first[:, :].unsqueeze(2).to_broadcast(over_e), ALU.is_equal))

            def top_first():
                dve.wait_ge(s_lg, 2)
                halves = ps[:, 6, 0:NT * 2 * E].rearrange("p (t h e) -> p t h e", t=NT, h=2)
                link(dve.tensor_copy(logit[:, :, :], halves[:, :, LO]))
                link(dve.tensor_tensor(logit[:, :, :], logit[:, :, :], halves[:, :, HI], ALU.add))
                link(dve.tensor_copy(cand[:, :, :], logit[:, :, :]))
                choose(0)

            def top_second():
                link(dve.scalar_tensor_tensor(out=cand[:, :, :], in0=hot[:, 0], scalar=-3e38, in1=logit[:, :, :],
                                              op0=ALU.mult, op1=ALU.add))
                choose(1)
                dve.tensor_tensor(member2[:, :, :], hot[:, 0], hot[:, 1], ALU.add).then_inc(s_mem2, 1)
                dve.tensor_tensor(gap[:, :], top[:, 1], top[:, 0], ALU.subtract).then_inc(s_gap, 1)

            def top_weights():
                dve.wait_ge(s_exp, 1)
                link(dve.tensor_scalar(first[:, :], exp_gap[:, :], 1.0, None, ALU.add))
                link(dve.reciprocal(weight[:, 0], first[:, :]))
                link(dve.tensor_tensor(weight[:, 1], exp_gap[:, :], weight[:, 0], ALU.mult))

            def positions():
                dve.wait_ge(s_cnt2, 1)
                within2 = ps[:, 7, 0:NT * E].rearrange("p (t e) -> p t e", t=NT)
                totals2 = ps[:, 7, NT * E:2 * NT * E].rearrange("p (t e) -> p t e", t=NT)
                for e in range(E):
                    link(dve.tensor_tensor_scan(run2[:, :, e], ones[:, 0:NT], totals2[:, :, e], 0.0, ALU.mult, ALU.add))
                link(dve.tensor_tensor(run2[:, :, :], run2[:, :, :], totals2, ALU.subtract))
                link(dve.tensor_tensor(run2[:, :, :], run2[:, :, :], within2, ALU.add))
                link(dve.tensor_scalar(late[:, :, :], run2[:, :, :], float(CAP), float(2 * E * CAP), ALU.is_ge, ALU.mult))
                link(dve.tensor_tensor(late[:, :, :], late[:, :, :], run2[:, :, :], ALU.add))
                link(dve.tensor_tensor(late[:, :, :], late[:, :, :], slot0[:, :].unsqueeze(1).to_broadcast(over_e), ALU.add))

            def choice_slots(k):
                link(dve.tensor_tensor(run2[:, :, :], hot[:, k], late[:, :, :], ALU.mult))
                link(dve.tensor_reduce(slot_f[:, :], run2[:, :, :], AX.X, ALU.add))
                slot_parts()
                link(dve.tensor_copy(w_hl[:, HI], weight[:, k]))
                link(dve.tensor_tensor(w_hl[:, LO], weight[:, k], w_hl[:, HI].bitcast(F32), ALU.subtract))

            def choice_pick(k):
                if k:
                    dve.wait_ge(s_perm2, 1)
                dve.tensor_tensor(pick2[:, :, :], lane[:, :].unsqueeze(1).to_broadcast([P, NT, P]),
                                  lane_f[:, :].unsqueeze(2).to_broadcast([P, NT, P]), ALU.is_equal).then_inc(s_pick2, 1)

            def choice_vals(k):
                cols = [P, NT, SLOTS]
                link(dve.tensor_tensor(vals2[:, :, 1, :], lane[:, 0:SLOTS].unsqueeze(1).to_broadcast(cols),
                                       col_f[:, :].unsqueeze(2).to_broadcast(cols), ALU.is_equal))
                for w, v in ((0, tok_tp[:, :]), (2, w_hl[:, HI].bitcast(F32)), (3, w_hl[:, LO].bitcast(F32))):
                    dve.tensor_tensor(vals2[:, :, w, :], vals2[:, :, 1, :].bitcast(F32),
                                      v.unsqueeze(2).to_broadcast(cols), ALU.mult).then_inc(s_pick2, 1)

            def slot_tables():
                dve.wait_ge(s_perm2, 2)
                got = ps[:, 7, 256:256 + 4 * SLOTS].rearrange("p (w c) -> p w c", w=4)
                link(dve.tensor_scalar(put2_f[:, :], got[:, 1], -float(T), float(T), ALU.mult, ALU.add))
                link(dve.tensor_tensor(put2_f[:, :], put2_f[:, :], got[:, 0], ALU.add))
                link(dve.tensor_copy(put2[:, :], put2_f[:, :]))
                link(dve.tensor_scalar(get2[:, :], put2_f[:, :], float(T - 1), None, ALU.min))
                link(dve.tensor_copy(slot_w[:, :], got[:, 2]))
                link(dve.tensor_tensor(slot_w[:, :], slot_w[:, :], got[:, 3], ALU.add))
                dve.memset(ve1[:, :], 0.0).then_inc(s_tab2, 1)

            extra = {6: [top_first], 7: [top_second], 8: [top_weights], 9: [positions],
                     10: [lambda: choice_slots(0), lambda: choice_pick(0)], 11: [lambda: choice_vals(0)],
                     12: [lambda: choice_slots(1)], 13: [lambda: choice_pick(1)],
                     14: [lambda: choice_vals(1)], 15: [slot_tables]}
            lo_up_shared(0, 0)
            lo_up_shared(0, 1)
            for u in range(KD):
                lo_h2(u)
            for j in range(4):
                for b in range(NB):
                    n = j * NB + b
                    if 1 <= n <= NB:
                        dve.wait_ge(s_yin, 16 * n)
                    dve_block(j, b, n == 0, False)
                    for u in range((n + 1) * KD, min(n + 2, NB) * KD):
                        lo_h2(u)
                    for piece in extra.get(n, ()):
                        piece()
            with dve.Fori(4, NJ - 1) as j:
                for b in range(NB):
                    dve_block(j, b, False, False)

            def lo_g(e, t):
                after(dve, s_th3, e * CT + t + 1)
                copy_lo(g_t[:, e % 2, LO, :, t * P:(t + 1) * P],
                        ps[:, 6 + t % 2, :].rearrange("p (k m) -> p k m", k=KD),
                        g_t[:, e % 2, HI, :, t * P:(t + 1) * P], s_tl3)

            def dve_unit(e, u):
                h, c = u // NC, u % NC
                v, m, t0, t1 = e * 6 + u, CH[c], HALF[h][0], HALF[h][1]
                n = (t1 - t0) * P
                after(dve, s_sl3, v + 1)
                after(dve, s_u3, v + 1)
                dve.tensor_tensor(gated[0:m, u % 2, 0:n], gated[0:m, u % 2, 0:n], ps[0:m, 1, 0:n],
                                  ALU.mult).then_inc(s_mul3, 1)
                after(dve, s_ah3, v + 1)
                copy_lo(a3_t[0:m, c, LO, t0 * P:t1 * P], gated[0:m, u % 2, 0:n],
                        a3_t[0:m, c, HI, t0 * P:t1 * P], s_al3)

            def weighted(e, t):
                after(dve, s_d3, e * CT + t + 1)
                after(dve, s_oin[t], 16 * (e + 1))
                dve.scalar_tensor_tensor(out=out_new[:, t], in0=ps[:, 2 + t % 4, :],
                                         scalar=slot_w[:, bass.ds(e * CT + t, 1)], in1=out_new[:, t],
                                         op0=ALU.mult, op1=ALU.add).then_inc(s_y3, 1)

            for b in range(NB):
                dve_block(NJ - 1, b, False, True)
                if b < 2:
                    lo_expert_up(0, b)
                for t in EARLY[b]:
                    lo_g(0, t)
            for t in range(BT):
                add_down(NJ - 1, NB - 1, t)
            lo_expert_down(0, 0)
            lo_expert_down(0, 1)
            lo_expert_up(0, 2)
            lo_expert_down(0, 2)

            def dve_expert(e, first, last):
                for u in range(6):
                    dve_unit(e, u)
                    if u < 3:
                        if not first:
                            weighted(e - 1, 2 + u)
                        if not last:
                            lo_g(e + 1, u)
                    if u >= 3:
                        if not last:
                            if u == 4:
                                lo_g(e + 1, 3)
                            if u == 5:
                                lo_g(e + 1, 4)
                            lo_expert_up(e + 1, u - 3)
                            lo_expert_down(e + 1, u - 3)
                        if u < 5:
                            weighted(e, u - 3)

            dve_expert(0, True, False)
            with dve.Fori(1, E - 1) as e:
                dve_expert(e, False, False)
            dve_expert(E - 1, False, True)
            for t in range(HALF[1][0], CT):
                weighted(E - 1, t)

        @block.tensor
        def _(pe):
            pe.wait_ge(s_const, 8)
            pe.wait_ge(s_mem1, EC)
            flat = member1[:, :, :].rearrange("p e j -> p (e j)")
            pe.matmul(ps[:, 4, 0:EC * NT], below[:, :], flat, start=True, stop=True)
            pe.matmul(ps[:, 5, 0:EC * NT], ones[:, :], flat, start=True, stop=True).then_inc(s_cnt1, 1)

            def turn_ctx(n):
                e, k0 = n // 2, n % 2 * 2
                if n % 2 == 0:
                    pe.wait_ge(s_ctx[e], 16)
                if n >= 2:
                    pe.wait_ge(s_ctl, n - 1)
                for k in range(2):
                    for r in range(KD):
                        mm = pe.transpose(ps[:, 2 * (n % 2) + k, r * P:(r + 1) * P],
                                          ctx_raw[:, e, r, (k0 + k) * P:(k0 + k + 1) * P], ident[:, :])
                mm.then_inc(s_ct, 1)

            turn_ctx(0)
            turn_ctx(1)
            pe.wait_ge(s_pick1, 2)
            for j in range(NT):
                mm = pe.matmul(ps[:, 6, 0:2 * (GT + 1)], pick1[:, j, :], vals1[:, j].rearrange("p w c -> p (w c)"),
                               start=(j == 0), stop=(j == NT - 1))
            mm.then_inc(s_perm1, 1)
            for n in range(2, EC * 2):
                turn_ctx(n)

            def turn(bank, src):
                for k in range(KD):
                    mm = pe.transpose(ps[:, bank, k * P:(k + 1) * P], src[:, k * P:(k + 1) * P], ident[:, :])
                return mm

            def by_ctx(bank, lhs, e):
                n = 0
                for a, b in PASSES:
                    for k in range(KD):
                        mm = pe.matmul(ps[:, bank, :], lhs[:, a, k, :],
                                       area_a[:, bass.ds(e * (2 * KD * D) + (b * KD + k) * D, D)],
                                       start=(n == 0), stop=(n == 3 * KD - 1))
                        n += 1
                return mm

            def tile_expert(k):
                return pe.value_load(tile_ei[0:1, bass.ds(k, 1)], min_val=0, max_val=EC - 1)

            def pe_step(i):
                if inside(i, 0, GT):
                    after(pe, s_a1, i + 1)
                    after(pe, s_lo2, i)
                    turn(1, gated[:, 0]).then_inc(s_t2, 1)
                if inside(i, -1, GT - 1):
                    after(pe, s_lo1, i + 2)
                    by_ctx(2, h1_t, tile_expert(i + 1)).then_inc(s_m1, 1)
                if inside(i, -2, GT - 2):
                    after(pe, s_h1, i + 3)
                    after(pe, s_lo1, i + 2)
                    turn(0, h1).then_inc(s_t1, 1)
                if inside(i, 0, GT):
                    after(pe, s_lo2, i + 1)
                    after(pe, s_x1, i)
                    by_ctx(3, a1_t, tile_expert(i)).then_inc(s_m2, 1)

            pe.wait_ge(s_ctl, EC * 2)
            for i in range(-2, 1):
                pe_step(i)
            with pe.Fori(1, GT - 2) as i:
                pe_step(i)
            for i in range(GT - 2, GT):
                pe_step(i)

            def turn_h2(u):
                b, k = u // KD, u % KD
                if k == 0:
                    pe.wait_ge(s_hin[b % 2], 16 * (b // 2 + 1))
                after(pe, s_ttl, u - 1)
                for r in range(BT):
                    mm = pe.transpose(ps[:, 6 + u % 2, r * P:(r + 1) * P],
                                      h2_in[:, b % 2, r, k * P:(k + 1) * P], ident[:, :])
                mm.then_inc(s_tt, 1)

            def up(j, b, g, signal):
                i = 0
                for w, m in PASSES:
                    for k in range(KD):
                        mm = pe.matmul(ps[:, g, :], sh_u[:, g, w, k, :], h2_t[:, m, k, b * N:(b + 1) * N],
                                       start=(i == 0), stop=(i == 3 * KD - 1))
                        i += 1
                mm.then_inc(signal, 1)

            def up_block(j, b):
                n = j * NB + b
                after(pe, s_ul, j * 2 + 1)
                after(pe, s_sl, n)
                up(j, b, 0, s_g)
                after(pe, s_ul, j * 2 + 2)
                after(pe, s_mul, n)
                up(j, b, 1, s_u)

            def down_block(j, b):
                n = j * NB + b
                after(pe, s_al, n + 1)
                after(pe, s_dl, j + 1)
                for t in range(BT):
                    after(pe, s_add, (n - 1) * BT + t + 1)
                    for i, (a, w) in enumerate(PASSES):
                        mm = pe.matmul(ps[:, 2 + t, :], a2_t[:, b % 2, a, t * P:(t + 1) * P], sh_d[:, w, :],
                                       start=(i == 0), stop=(i == 2))
                    mm.then_inc(s_dn, 1)

            def router_logits(t0, t1):
                for t in range(t0, t1):
                    i = 0
                    for a in (LO, HI):
                        for k in range(KD):
                            mm = pe.matmul(ps[:, 6, t * 2 * E:(t + 1) * 2 * E], h2_t[:, a, k, t * P:(t + 1) * P],
                                           rt_w[:, k].rearrange("p h e -> p (h e)"),
                                           start=(i == 0), stop=(i == 2 * KD - 1))
                            i += 1
                mm.then_inc(s_lg, 1)

            def choice_perm(k):
                pe.wait_ge(s_pick2, 4 * (k + 1))
                for j in range(NT):
                    mm = pe.matmul(ps[:, 7, 256:256 + 4 * SLOTS], pick2[:, j, :],
                                   vals2[:, j].rearrange("p w c -> p (w c)"),
                                   start=(k == 0 and j == 0), stop=(k == 1 and j == NT - 1))
                mm.then_inc(s_perm2, 1)

            for u in range(KD):
                turn_h2(u)
            for j in range(4):
                for b in range(NB):
                    n = j * NB + b
                    pe.wait_ge(s_ttl, (min(n, NB - 1) + 1) * KD)
                    up_block(j, b)
                    turns = range((n + 1) * KD, min(n + 2, NB) * KD)
                    for u in turns[:2]:
                        turn_h2(u)
                    if n:
                        jp, bp = (j, b - 1) if b else (j - 1, NB - 1)
                        down_block(jp, bp)
                    for u in turns[2:]:
                        turn_h2(u)
                    if n == 4:
                        pe.wait_ge(s_rt_lo, 1)
                        router_logits(0, NT // 2)
                    if n == 5:
                        router_logits(NT // 2, NT)
                    if n == 8:
                        pe.wait_ge(s_mem2, 1)
                        flat2 = member2[:, :, :].rearrange("p t e -> p (t e)")
                        pe.matmul(ps[:, 7, 0:NT * E], below[:, :], flat2, start=True, stop=True)
                        pe.matmul(ps[:, 7, NT * E:2 * NT * E], ones[:, :], flat2,
                                  start=True, stop=True).then_inc(s_cnt2, 1)
                    if n == 12:
                        choice_perm(0)
                    if n == 15:
                        choice_perm(1)
            with pe.Fori(4, NJ - 1) as j:
                for b in range(NB):
                    up_block(j, b)
                    down_block(j if b else j - 1, (b - 1) % NB)

            def turn_g(e, t):
                w = e * CT + t
                after(pe, s_gin[t], 16 * (e + 1))
                after(pe, s_tl3, w - (t > 0))
                turn(6 + t % 2, g_in[:, t]).then_inc(s_t3, 1)

            def up_unit(e, u):
                h, c = u // NC, u % NC
                v, m, t0, t1 = e * 6 + u, CH[c], HALF[h][0], HALF[h][1]
                n = (t1 - t0) * P
                after(pe, s_tl3, e * CT + t1)
                for g, read, signal in ((0, s_sl3, s_g3), (1, s_mul3, s_u3)):
                    after(pe, s_ul, (NJ + e * NC + c) * 2 + g + 1)
                    after(pe, read, v)
                    i = 0
                    for w, a in PASSES:
                        for k in range(KD):
                            mm = pe.matmul(ps[0:m, g, 0:n], up_w[:, c, g, w, k, 0:m],
                                           g_t[:, e % 2, a, k, t0 * P:t1 * P],
                                           start=(i == 0), stop=(i == 3 * KD - 1))
                            i += 1
                    mm.then_inc(signal, 1)

            def down_unit(e, t):
                h = 0 if t < HALF[0][1] else 1
                after(pe, s_al3, e * 6 + (h + 1) * NC)
                after(pe, s_dl, NJ + (e + 1) * NC)
                after(pe, s_y3, e * CT + t - (t > 0))
                i = 0
                for a, w in PASSES:
                    for c in range(NC):
                        mm = pe.matmul(ps[:, 2 + t % 4, :], a3_t[0:CH[c], c, a, t * P:(t + 1) * P],
                                       dn_w[0:CH[c], e % 2, c, w, :], start=(i == 0), stop=(i == 3 * NC - 1))
                        i += 1
                mm.then_inc(s_d3, 1)

            for b in range(NB):
                up_block(NJ - 1, b)
                for t in EARLY[b]:
                    turn_g(0, t)
                down_block(NJ - 1 if b else NJ - 2, (b - 1) % NB)
            down_block(NJ - 1, NB - 1)

            def pe_expert(e, first, last):
                for u in range(6):
                    up_unit(e, u)
                    if u < 3 and not first:
                        down_unit(e - 1, 2 + u)
                    if 3 <= u < 5:
                        down_unit(e, u - 3)
                    if not last:
                        if u < 3:
                            turn_g(e + 1, u)
                        if u > 3:
                            turn_g(e + 1, u - 1)

            pe_expert(0, True, False)
            with pe.Fori(1, E - 1) as e:
                pe_expert(e, False, False)
            pe_expert(E - 1, False, True)
            for t in range(HALF[1][0], CT):
                down_unit(E - 1, t)


_INS = ['x', 'itok_BxS_13_99985', 'ctx_2048', 'L0_ffn_router', 'L0_ffn_w_up_gate', 'L0_ffn_w_down',
        'L0_ffn_shared_w_up_gate', 'L0_ffn_shared_w_down']


def kernel(**inputs):
    import numpy as np
    import concourse.bacc as bacc
    from concourse.bass_utils import run_bass_kernel_spmd

    nc = bacc.Bacc("TRN2", target_bir_lowering=False, num_devices=1)
    arrays, args = {}, []
    for name in _INS:
        a = np.ascontiguousarray(inputs[name])
        arrays[f"in_{name}"] = a
        args.append(nc.dram_tensor(f"in_{name}", a.shape, mybir.dt.from_np(a.dtype), kind="ExternalInput").ap())
    args.append(nc.dram_tensor("out_x", tuple(inputs["x"].shape), F32, kind="ExternalOutput").ap())
    routed_block_program(nc, *args)
    r = run_bass_kernel_spmd(nc, [arrays], core_ids=[0])
    return r.results[0]["out_x"]
```

```python
from contextlib import ExitStack

import concourse.bass as bass
from concourse import mybir

ALU = mybir.AluOpType
ACT = mybir.ActivationFunctionType
AX = mybir.AxisListType
F32 = mybir.dt.float32
F32R = mybir.dt.float32r
I32 = mybir.dt.int32

P = 128
HI, LO = 0, 1
PASSES = ((LO, HI), (HI, LO), (HI, HI))
EPS = 1e-5


def after(eng, sem, count):
    if not isinstance(count, int) or count > 0:
        eng.wait_ge(sem, count)


def apart(eng, passed):
    eng.sem_inc(passed, 1)


def inside(i, low, high):
    return not isinstance(i, int) or low <= i < high


def h2_bank(u):
    return (6, 7, 4, 5)[u % 4] if u < 8 else 6 + u % 2


def turns_early(n):
    return (range(4, 8), (8, 9), (12, 13))[n] if isinstance(n, int) and n < 3 else ()


def turns_late(n):
    return ((), (10, 11), (14, 15))[n] if isinstance(n, int) and n < 3 else ()


def routed_block_program(nc, x, ids, ctx_w, router, w_ug, w_dn, sh_ug, sh_dn, out):
    B, S, D = x.shape
    T = B * S
    KD = D // P
    NT = T // P
    EC = ctx_w.shape[0]
    E = w_ug.shape[0]
    I = w_dn.shape[1]
    J = sh_dn.shape[0]
    NJ = J // P
    CAP = -(-T * 2 * 5 // (E * 4))
    CT = CAP // P
    GT = NT + EC - 1
    VOCAB_PART = 25000 // EC
    CH = [P, P, I - 2 * P]
    NC = len(CH)
    rounds = (GT - 4) // 4
    NB = 4
    BT = NT // NB
    N = BT * P
    HALF = [(0, 2), (2, CT)]
    SLOTS = E * CT
    NBLK = NJ * NB
    CTX_BANK = [0, 2, 6]
    EARLY = [[], [0, 1], [2, 3], [4]]
    assert D == 512 and N == 512 and CAP == 640 and J % P == 0 and 0 < CH[2] <= P

    xf = x.rearrange("b s d -> (b s) d")
    of = out.rearrange("b s d -> (b s) d")
    x1_rows = nc.dram_tensor("x1_rows", (T, D), F32).ap()
    h2_rows = nc.dram_tensor("h2_rows", (T, D), F32).ap()

    with ExitStack() as ctx:
        def sb(name, shape, dt=F32):
            return ctx.enter_context(nc.sbuf_tensor(name, shape, dt))

        def sem(name):
            return ctx.enter_context(nc.semaphore(name))

        area_a = sb("area_a", [P, 16384], F32R)
        area_b = sb("area_b", [P, 16384], F32R)
        ctx_t = area_a[:, :].rearrange("p (e h k m) -> p e h k m", e=EC, h=2, k=KD)
        h1_t = area_b[:, 0:1024].rearrange("p (h k m) -> p h k m", h=2, k=KD)
        a1_t = area_b[:, 1024:2048].rearrange("p (h k m) -> p h k m", h=2, k=KD)
        pick1 = area_b[:, 2048:4096].rearrange("p (j c) -> p j c", j=NT)
        vals1 = area_b[:, 4096:4096 + NT * 2 * (GT + 1)].rearrange("p (j w c) -> p j w c", j=NT, w=2)
        h2_t = area_b[:, :].rearrange("p (h k n) -> p h k n", h=2, k=KD)
        pick2 = area_a[:, 0:2048].rearrange("p (j c) -> p j c", j=NT)
        vals2 = area_a[:, 2048:2048 + NT * 4 * SLOTS].rearrange("p (j w c) -> p j w c", j=NT, w=4)
        up_w = area_a[:, 0:6144].rearrange("p (c g h k m) -> p c g h k m", c=NC, g=2, h=2, k=KD)
        g_t = area_a[:, 6144:16384].rearrange("p (b h k n) -> p b h k n", b=2, h=2, k=KD)
        a2_t = area_a[:, 11264:13312].rearrange("p (b h n) -> p b h n", b=2, h=2)
        sh_d = area_a[:, 13312:14336].rearrange("p (h n) -> p h n", h=2)
        sh_u = area_a[:, 14336:16384].rearrange("p (g h k m) -> p g h k m", g=2, h=2, k=KD)
        dn_w = area_b[:, 0:6144].rearrange("p (b c h n) -> p b c h n", b=2, c=NC, h=2)
        a3_t = area_b[:, 6144:9984].rearrange("p (c h n) -> p c h n", c=NC, h=2)
        rt_w = sb("rt_w", [P, KD, 2, E], F32R)

        acc = sb("acc", [P, NT, D])
        ctx_raw = acc[:, :, :].rearrange("p (e r) d -> p e r d", e=EC)
        out_new = acc
        raw_u = sb("raw_u", [P, 2, 2, KD, P])
        raw_d = sb("raw_d", [P, 2, D])
        gated = sb("gated", [P, 2, D])
        rows = sb("rows", [P, 9 * D])
        x_in = rows[:, 0:4 * D].rearrange("p (s d) -> p s d", s=4)
        h1 = rows[:, 4 * D:5 * D]
        x1 = rows[:, 5 * D:7 * D].rearrange("p (s d) -> p s d", s=2)
        h2 = rows[:, 7 * D:9 * D].rearrange("p (s d) -> p s d", s=2)
        h2_in = rows[:, 0:8 * D].rearrange("p (s d) -> p s d", s=8)
        logit_rows = rows[0:2 * E, 0:T]
        g_in = rows[:, 0:CT * D].rearrange("p (s d) -> p s d", s=CT)
        ahead_u = rows[:, CT * D:CT * D + 2 * KD * CH[2]].rearrange("p (g k m) -> p g k m", g=2, k=KD)
        ahead_d = rows[:, 8 * D:9 * D]

        def expert_raw(e, c):
            if isinstance(e, int) and (e, c) == (0, NC - 1):
                return ahead_u, ahead_d[0:CH[c]]
            q = NJ + e * NC + c
            return raw_u[:, q % 2, :, :, 0:CH[c]], raw_d[0:CH[c], q % 2]

        ident = sb("ident", [P, P])
        ones = sb("ones", [P, P])
        not_below = sb("not_below", [P, P])
        restart = sb("restart", [P, EC, NT])
        lane = sb("lane", [P, P])
        tok_pj = sb("tok_pj", [P, NT])
        tok_tp = sb("tok_tp", [P, NT])
        descend = sb("descend", [P, E])
        slot0 = sb("slot0", [P, E])
        expo = sb("expo", [P, 1])
        rt_raw = sb("rt_raw", [P, KD, E])
        ids_i = sb("ids_i", [P, NT], I32)
        at_least = sb("at_least", [P, EC + 1, NT])
        member1 = sb("member1", [P, EC, NT])
        run1 = sb("run1", [P, EC, NT])
        tiles_i = sb("tiles_i", [P, EC], I32)
        tile_end = sb("tile_end", [P, EC + 1])
        slot_f = sb("slot_f", [P, NT])
        slot_i = sb("slot_i", [P, NT], I32)
        lane_i = sb("lane_i", [P, NT], I32)
        col_i = sb("col_i", [P, NT], I32)
        tile_e = sb("tile_e", [P, GT + 1])
        tile_ei = sb("tile_ei", [P, GT + 1], I32)
        put1_f = sb("put1_f", [P, GT + 1])
        put1 = sb("put1", [P, GT + 1], I32)
        get1 = sb("get1", [P, GT + 1], I32)
        get_now = sb("get_now", [P, 4], I32)
        put_now = sb("put_now", [P, 2], I32)
        part1, part2 = sb("part1", [P, 6]), sb("part2", [P, 6])
        mv1, mv2 = sb("mv1", [P, 2]), sb("mv2", [P, 2])
        ve1, ve2 = sb("ve1", [P, 1]), sb("ve2", [P, 1])
        rstd1, rstd2 = sb("rstd1", [P, 1]), sb("rstd2", [P, 1])
        logit = sb("logit", [P, NT, E])
        cand = sb("cand", [P, NT, E])
        top = sb("top", [P, 2, NT])
        first = sb("first", [P, NT])
        hot = sb("hot", [P, 2, NT, E])
        member2 = sb("member2", [P, NT, E])
        run2 = sb("run2", [P, NT, E])
        late = sb("late", [P, NT, E])
        gap = sb("gap", [P, NT])
        exp_gap = sb("exp_gap", [P, NT])
        weight = sb("weight", [P, 2, NT])
        w_hl = sb("w_hl", [P, 2, NT], F32R)
        put2_f = sb("put2_f", [P, SLOTS])
        put2 = sb("put2", [P, SLOTS], I32)
        get2 = sb("get2", [P, SLOTS], I32)
        slot_w = sb("slot_w", [P, SLOTS])
        g_idx = sb("g_idx", [P, CT], I32)
        o_idx = sb("o_idx", [P, CT], I32)
        p_idx = sb("p_idx", [P, CT], I32)

        ps = ctx.enter_context(nc.psum_tensor("ps", [P, 8, 512], F32))

        s_const = sem("const_ready")
        s_passed = [sem(f"waits_passed_{who}") for who in ("dve", "pool", "sp")]
        s_ids = sem("ids_landed")
        s_ctx = [sem(f"ctx{e}_landed") for e in range(EC)]
        s_rt = sem("router_landed")
        s_warm = sem("silu_table_loaded")
        s_rt_hi, s_rt_lo = sem("router_hi"), sem("router_lo")
        s_v = sem("dve_table_step")
        s_col = sem("slot_columns_ready")
        s_edge = sem("thresholds_ready")
        s_mem1, s_cnt1 = sem("member1_ready"), sem("counts1_ready")
        s_pick1, s_perm1, s_tab1 = sem("pick1_ready"), sem("perm1_ready"), sem("table1_ready")
        s_ct, s_cth, s_ctl = sem("ctx_transposed"), sem("ctx_hi"), sem("ctx_lo")
        s_idx = sem("index_column_staged")
        s_get, s_put1 = sem("get_column_staged"), sem("put_column_staged")
        s_xin = [sem(f"x_rows_landed{c}") for c in range(4)]
        s_xout = [sem(f"x1_rows_stored{c}") for c in range(2)]
        s_hout = [sem(f"h2_rows_stored{c}") for c in range(2)]
        s_part1, s_st1, s_ve1, s_rs1, s_h1 = (sem("part1_ready"), sem("stats1_ready"), sem("vareps1_ready"),
                                              sem("rstd1_ready"), sem("h1_ready"))
        s_part2, s_st2, s_ve2, s_rs2, s_h2 = (sem("part2_ready"), sem("stats2_ready"), sem("vareps2_ready"),
                                              sem("rstd2_ready"), sem("h2_ready"))
        s_t1, s_hi1, s_lo1 = sem("h1_transposed"), sem("h1_hi"), sem("h1_lo")
        s_m1, s_sl1, s_a1 = sem("z_ready"), sem("silu1_ready"), sem("a1_ready")
        s_t2, s_hi2, s_lo2 = sem("a1_transposed"), sem("a1_hi"), sem("a1_lo")
        s_m2, s_x1 = sem("y1_ready"), sem("x1_ready")
        s_hin = [sem(f"h2_tile_landed{k}") for k in range(8)]
        s_yin = [sem(f"x1_block_landed{b}") for b in range(NB)]
        s_tt, s_tth, s_ttl = sem("h2_transposed"), sem("h2_hi"), sem("h2_lo")
        s_raw = sem("weights_landed")
        s_uh, s_ul, s_dh, s_dl = sem("up_w_hi"), sem("up_w_lo"), sem("down_w_hi"), sem("down_w_lo")
        s_g, s_u, s_sl, s_mul = sem("gate_ready"), sem("up_ready"), sem("silu2_ready"), sem("gated2_ready")
        s_ah, s_al = sem("a2_hi"), sem("a2_lo")
        s_dn, s_add = sem("down_ready"), sem("acc_added")
        s_lgt, s_lgc = sem("logit_rows_ready"), sem("logit_rows_copied")
        s_lg, s_mem2, s_cnt2 = sem("logits_ready"), sem("member2_ready"), sem("counts2_ready")
        s_scan = sem("sums2_ready")
        s_gap, s_exp = sem("gap_ready"), sem("exp_ready")
        s_pick2, s_perm2, s_tab2 = sem("pick2_ready"), sem("perm2_ready"), sem("table2_ready")
        s_out = sem("output_written")
        s_gin = [sem(f"g_rows_landed{t}") for t in range(CT)]
        s_oin = [sem(f"out_rows_landed{t}") for t in range(CT)]
        s_t3, s_th3, s_tl3 = sem("g_transposed"), sem("g_hi"), sem("g_lo")
        s_g3, s_u3, s_sl3, s_mul3 = sem("gate3_ready"), sem("up3_ready"), sem("silu3_ready"), sem("gated3_ready")
        s_ah3, s_al3, s_d3, s_y3 = sem("a3_hi"), sem("a3_lo"), sem("down3_ready"), sem("rows3_ready")
        s_put = sem("rows3_stored")

        block = ctx.enter_context(nc.Block())

        @block.sync
        def _(sp):
            def hold(sem, count):
                after(sp, sem, count)
                if not isinstance(count, int):
                    apart(sp, s_passed[2])

            def load_shared(q):
                hold(s_raw, q * 48)
                hold(s_ul, (q - 1) * 2)
                hold(s_dl, q - 1)
                for g in range(2):
                    sp.dma_start(raw_u[:, q % 2, g],
                                 sh_ug.rearrange("(k p) m -> p k m", p=P)[:, :, bass.ds(q * P + g * J, P)]
                                 ).then_inc(s_raw, 16)
                sp.dma_start(raw_d[:, q % 2], sh_dn.rearrange("(j p) d -> j p d", p=P)[q]).then_inc(s_raw, 16)

            def load_expert(e, c):
                q = NJ + e * NC + c
                up, down = expert_raw(e, c)
                hold(s_raw, q * 48)
                if isinstance(e, int) and (e, c) == (0, NC - 1):
                    hold(s_tt, NT)
                else:
                    hold(s_ul, (q - 1) * 2)
                    hold(s_dl, q - 1)
                for g in range(2):
                    sp.dma_start(up[:, g],
                                 w_ug.rearrange("e (k p) m -> e p k m", p=P)[e, :, :, g * I + c * P:g * I + c * P + CH[c]]
                                 ).then_inc(s_raw, 16)
                sp.dma_start(down, w_dn[e, c * P:c * P + CH[c], :]).then_inc(s_raw, 16)

            sp.dma_start(ids_i[:, :], ids.rearrange("b (p j) -> (b p) j", j=NT)).then_inc(s_ids, 16)
            for e in range(EC):
                sp.dma_start(ctx_raw[:, e], ctx_w[e].rearrange("(r p) d -> p r d", p=P)).then_inc(s_ctx[e], 16)
            sp.dma_start(rt_raw[:, :, :], router.rearrange("(k p) e -> p k e", p=P)).then_inc(s_rt, 16)
            load_shared(0)
            load_shared(1)
            for c in range(2):
                hold(s_xout[c], 16 * ((GT + 1 - c) // 2))
                hold(s_hout[c], 16 * ((GT + 1 - c) // 2))
            def load_h2(u):
                if u >= 8:
                    hold(s_tt, u - 7)
                sp.dma_start(h2_in[:, u % 8], h2_rows[u * P:(u + 1) * P, :]).then_inc(s_hin[u % 8], 16)

            for u in range(8):
                load_h2(u)
            for b in range(NB):
                sp.dma_start(acc[:, b * BT:(b + 1) * BT, :],
                             x1_rows[b * N:(b + 1) * N, :].rearrange("(r p) d -> p r d", p=P)).then_inc(s_yin[b], 16)
                if b < 2:
                    for u in range(8 + 4 * b, 12 + 4 * b):
                        load_h2(u)
            with sp.Fori(2, NJ) as q:
                load_shared(q)
            for c in range(NC):
                load_expert(0, c)
            with sp.Fori(1, E) as e:
                for c in range(NC):
                    load_expert(e, c)

        @block.gpsimd
        def _(pool):
            def hold(sem, count):
                after(pool, sem, count)
                if not isinstance(count, int):
                    apart(pool, s_passed[1])

            pool.memset(ident[:, :], 0.0).then_inc(s_const, 1)
            pool.memset(ones[:, :], 1.0).then_inc(s_const, 1)
            pool.memset(not_below[:, :], 0.0).then_inc(s_const, 1)
            pool.memset(expo[:, :], -0.5).then_inc(s_const, 1)
            pool.iota(lane[:, :], pattern=[[1, P]], base=0, channel_multiplier=0,
                      allow_small_or_imprecise_dtypes=True).then_inc(s_const, 1)
            pool.iota(tok_pj[:, :], pattern=[[1, NT]], base=0, channel_multiplier=NT,
                      allow_small_or_imprecise_dtypes=True).then_inc(s_const, 1)
            pool.memset(restart[:, :, :], 1.0).then_inc(s_const, 1)
            pool.wait_ge(s_const, 7)
            pool.affine_select(out=ident[:, :], in_=ident[:, :], compare_op=ALU.not_equal, fill=1.0, base=0,
                               pattern=[[-1, P]], channel_multiplier=1).then_inc(s_const, 1)
            pool.affine_select(out=not_below[:, :], in_=not_below[:, :], compare_op=ALU.is_gt, fill=-1.0, base=0,
                               pattern=[[1, P]], channel_multiplier=-1).then_inc(s_const, 1)
            pool.memset(restart[:, :, 0:1], 0.0).then_inc(s_const, 1)
            pool.iota(tok_tp[:, :], pattern=[[P, NT]], base=0, channel_multiplier=1,
                      allow_small_or_imprecise_dtypes=True).then_inc(s_const, 1)
            pool.iota(descend[:, :], pattern=[[-1, E]], base=E, channel_multiplier=0,
                      allow_small_or_imprecise_dtypes=True).then_inc(s_const, 1)
            pool.iota(slot0[:, :], pattern=[[CAP, E]], base=0, channel_multiplier=0,
                      allow_small_or_imprecise_dtypes=True).then_inc(s_const, 1)

            def gather(k, q, c):
                hold(s_x1, k - 3)
                pool.tensor_copy(get_now[:, c:c + 1], get1[:, bass.ds(k, 1)]).then_inc(s_get, 1)
                hold(s_get, k + 1)
                pool.indirect_dma_start(x_in[:, c], None, xf,
                                        bass.IndirectOffsetOnAxis(ap=get_now[:, c:c + 1], axis=0),
                                        bounds_check=T - 1, oob_is_err=False).then_inc(s_xin[c], 16)

            def scatter_x(k, c, before):
                hold(s_xout[c], 16 * before)
                hold(s_hout[c], 16 * before)
                pool.tensor_copy(put_now[:, c:c + 1], put1[:, bass.ds(k, 1)]).then_inc(s_put1, 1)
                hold(s_put1, k + 1)
                hold(s_x1, k + 1)
                pool.indirect_dma_start(x1_rows, bass.IndirectOffsetOnAxis(ap=put_now[:, c:c + 1], axis=0),
                                        x1[:, c], None, bounds_check=T - 1, oob_is_err=False).then_inc(s_xout[c], 16)

            def scatter_h(k, c):
                hold(s_h2, k + 1)
                pool.indirect_dma_start(h2_rows, bass.IndirectOffsetOnAxis(ap=put_now[:, c:c + 1], axis=0),
                                        h2[:, c], None, bounds_check=T - 1, oob_is_err=False).then_inc(s_hout[c], 16)

            def root(st, mv, ve, s_ve, rstd, s_rs, k):
                hold(st, k + 1)
                pool.tensor_scalar(ve[:, :], mv[:, 1:2], EPS, 1.0, ALU.add, ALU.mult).then_inc(s_ve, 1)
                hold(s_ve, k + 1)
                pool.tensor_tensor(rstd[:, :], ve[:, :], expo[:, :], ALU.pow).then_inc(s_rs, 1)

            def pool_step(i, q, c):
                if inside(i, 0, GT - 4):
                    gather(i + 4, q + 1, c)
                if inside(i, 0, GT):
                    scatter_x(i, c % 2, 2 * q + c // 2)
                    root(s_st2, mv2, ve2, s_ve2, rstd2, s_rs2, i)
                    scatter_h(i, c % 2)
                if inside(i, -4, GT - 4):
                    root(s_st1, mv1, ve1, s_ve1, rstd1, s_rs1, i + 4)

            pool.wait_ge(s_tab1, 1)
            for k in range(4):
                gather(k, 0, k)
            pool.wait_ge(s_tab1, 2)
            for i in range(-4, 4):
                pool_step(i, i // 4, i % 4)
            with pool.Fori(1, rounds) as q:
                for c in range(4):
                    pool_step(4 * q + c, q, c)
            for i in range(4 * rounds, GT):
                pool_step(i, i // 4, i % 4)

            def gather_g(e, tiles):
                if 0 in tiles:
                    for t in range(CT):
                        hold(s_gin[t], 16 * e)
                    pool.tensor_copy(g_idx[:, :], get2[:, bass.ds(e * CT, CT)]).then_inc(s_idx, 1)
                    hold(s_idx, 1 if isinstance(e, int) and e == 0 else e * 3 - 1)
                for t in tiles:
                    hold(s_t3, (e - 1) * CT + t + 1)
                    pool.indirect_dma_start(g_in[:, t], None, h2_rows,
                                            bass.IndirectOffsetOnAxis(ap=g_idx[:, t:t + 1], axis=0),
                                            bounds_check=T - 1, oob_is_err=False).then_inc(s_gin[t], 16)

            def gather_out(e, more):
                hold(s_put, 16 * CT * e)
                staged = e * 3 + (4 if more else 3)
                pool.tensor_copy(o_idx[:, :], get2[:, bass.ds(e * CT, CT)]).then_inc(s_idx, 1)
                pool.tensor_copy(p_idx[:, :], put2[:, bass.ds(e * CT, CT)]).then_inc(s_idx, 1)
                hold(s_idx, staged)
                for t in range(CT):
                    pool.indirect_dma_start(out_new[:, t], None, of,
                                            bass.IndirectOffsetOnAxis(ap=o_idx[:, t:t + 1], axis=0),
                                            bounds_check=T - 1, oob_is_err=False).then_inc(s_oin[t], 16)
                for t in range(CT):
                    hold(s_oin[t], 16 * (e + 1))

            def store_out(e, t):
                hold(s_y3, e * CT + t + 1)
                pool.indirect_dma_start(of, bass.IndirectOffsetOnAxis(ap=p_idx[:, t:t + 1], axis=0),
                                        out_new[:, t], None, bounds_check=T - 1, oob_is_err=False).then_inc(s_put, 16)

            def store_block(b):
                pool.wait_ge(s_add, (NBLK - NB + b + 1) * BT)
                pool.dma_start(of[b * N:(b + 1) * N, :].rearrange("(r p) d -> p r d", p=P),
                               acc[:, b * BT:(b + 1) * BT, :]).then_inc(s_out, 16)

            def pool_expert(e, first, ahead, last):
                if not first:
                    for t in range(HALF[1][0], CT):
                        store_out(e - 1, t)
                gather_out(e, not last)
                if ahead:
                    gather_g(e + 2, (0, 1, 2))
                for t in range(*HALF[0]):
                    store_out(e, t)
                if ahead:
                    gather_g(e + 2, (3, 4))

            pool.wait_ge(s_tt, NT)
            pool.wait_ge(s_tab2, 1)
            gather_g(0, range(CT))
            store_block(0)
            store_block(1)
            gather_g(1, range(CT))
            store_block(2)
            store_block(3)
            pool.wait_ge(s_out, 16 * NB)
            pool_expert(0, True, True, False)
            with pool.Fori(1, E - 2) as e:
                pool_expert(e, False, True, False)
            pool_expert(E - 2, False, False, False)
            pool_expert(E - 1, False, False, True)
            for t in range(HALF[1][0], CT):
                store_out(E - 1, t)
            pool.wait_ge(s_put, 16 * SLOTS)

        @block.scalar
        def _(act):
            def copy_hi(dst, src, signal):
                act.activation(dst, src, ACT.Copy).then_inc(signal, 1)

            act.wait_ge(s_const, 2)
            act.activation(gated[:, 1, 0:1], ones[:, 0:1], ACT.Silu).then_inc(s_warm, 1)
            for n in range(EC * 2):
                e, k = n // 2, n % 2 * 2
                act.wait_ge(s_ct, n + 1)
                copy_hi(ctx_t[:, e, HI, k:k + 2, :], ps[:, CTX_BANK[n % 3]:CTX_BANK[n % 3] + 2, :], s_cth)
            act.wait_ge(s_rt, 16)
            copy_hi(rt_w[:, :, HI, :], rt_raw[:, :, :], s_rt_hi)
            act.wait_ge(s_warm, 1)

            def act_step(i):
                if inside(i, 0, GT):
                    after(act, s_t2, i + 1)
                    copy_hi(a1_t[:, HI], ps[:, 1, :].rearrange("p (k m) -> p k m", k=KD), s_hi2)
                if inside(i, -1, GT - 1):
                    after(act, s_m1, i + 2)
                    act.activation(gated[:, 0], ps[:, 2, :], ACT.Silu).then_inc(s_sl1, 1)
                if inside(i, -2, GT - 2):
                    after(act, s_t1, i + 3)
                    copy_hi(h1_t[:, HI], ps[:, 0, :].rearrange("p (k m) -> p k m", k=KD), s_hi1)

            for i in range(-2, 0):
                act_step(i)
            with act.Fori(0, GT - 2) as i:
                act_step(i)
            for i in range(GT - 2, GT):
                act_step(i)

            def hi_up_shared(j, g):
                after(act, s_raw, 48 * (j + 1))
                after(act, s_g if g == 0 else s_u, j * NB)
                copy_hi(sh_u[:, g, HI], raw_u[:, j % 2, g], s_uh)

            def hi_down_shared(j):
                after(act, s_raw, 48 * (j + 1))
                after(act, s_dn, j * NB * BT)
                copy_hi(sh_d[:, HI], raw_d[:, j % 2], s_dh)

            def hi_expert_up(e, c):
                q = NJ + e * NC + c
                after(act, s_raw, 48 * (q + 1))
                after(act, s_u3, (e - 1) * 6 + 4 + c)
                for g in range(2):
                    copy_hi(up_w[:, c, g, HI, :, 0:CH[c]], expert_raw(e, c)[0][:, g], s_uh)

            def hi_expert_down(e, c):
                q = NJ + e * NC + c
                after(act, s_d3, (e - 1) * CT)
                copy_hi(dn_w[0:CH[c], e % 2, c, HI], expert_raw(e, c)[1], s_dh)

            def hi_h2(u):
                act.wait_ge(s_tt, u + 1)
                copy_hi(h2_t[:, HI, :, u * P:(u + 1) * P],
                        ps[:, h2_bank(u), :].rearrange("p (k m) -> p k m", k=KD), s_tth)

            def act_block(j, b, last):
                n = j * NB + b
                after(act, s_g, n + 1)
                after(act, s_al, n - 1)
                act.activation(gated[:, b % 2], ps[:, 0, :], ACT.Silu).then_inc(s_sl, 1)
                for u in turns_early(n):
                    hi_h2(u)
                if b == NB - 1 and not last:
                    hi_up_shared(j + 1, 0)
                    hi_up_shared(j + 1, 1)
                after(act, s_mul, n + 1)
                after(act, s_dn, (n - 1) * BT)
                copy_hi(a2_t[:, b % 2, HI], gated[:, b % 2], s_ah)
                for u in turns_late(n):
                    hi_h2(u)
                if b == 0:
                    hi_down_shared(j)

            act.wait_ge(s_m2, GT)
            hi_up_shared(0, 0)
            hi_up_shared(0, 1)
            for u in range(BT):
                hi_h2(u)
            for j in range(4):
                for b in range(NB):
                    act_block(j, b, False)
                    n = j * NB + b
                    if 3 <= n < 5:
                        for lb in (2 * n - 6, 2 * n - 5):
                            act.wait_ge(s_lgt, lb + 1)
                            copy_hi(logit_rows[:, lb * N:(lb + 1) * N], ps[0:2 * E, 6 + lb % 2, :], s_lgc)
                    if n == 8:
                        act.wait_ge(s_gap, 1)
                        act.activation(exp_gap[:, :], gap[:, :], ACT.Exp).then_inc(s_exp, 1)
            with act.Fori(4, NJ - 1) as j:
                for b in range(NB):
                    act_block(j, b, False)

            def hi_g(e, t):
                w = e * CT + t
                after(act, s_t3, w + 1)
                after(act, s_u3, (e - 1) * 6)
                copy_hi(g_t[:, e % 2, HI, :, t * P:(t + 1) * P],
                        ps[:, 6 + t % 2, :].rearrange("p (k m) -> p k m", k=KD), s_th3)

            def act_unit(e, u):
                h, c = u // NC, u % NC
                v, m, t0, t1 = e * 6 + u, CH[c], HALF[h][0], HALF[h][1]
                n = (t1 - t0) * P
                after(act, s_g3, v + 1)
                after(act, s_al3, v - 1)
                act.activation(gated[0:m, u % 2, 0:n], ps[0:m, 0, 0:n], ACT.Silu).then_inc(s_sl3, 1)
                after(act, s_mul3, v + 1)
                after(act, s_d3, (e - 1) * CT + t1)
                copy_hi(a3_t[0:m, c, HI, t0 * P:t1 * P], gated[0:m, u % 2, 0:n], s_ah3)

            act.wait_ge(s_perm2, 2)
            for b in range(NB):
                act_block(NJ - 1, b, True)
                if b < NC:
                    hi_expert_up(0, b)
                for t in EARLY[b]:
                    hi_g(0, t)
            act.wait_ge(s_u, NBLK)
            for c in range(NC):
                hi_expert_down(0, c)
            act.wait_ge(s_dn, NBLK * BT)

            def act_expert(e, last):
                for u in range(6):
                    act_unit(e, u)
                    if not last:
                        if u < 3:
                            hi_g(e + 1, u)
                        if u == 4:
                            hi_g(e + 1, 3)
                        if u == 5:
                            hi_g(e + 1, 4)
                        if u >= 3:
                            hi_expert_up(e + 1, u - 3)
                            hi_expert_down(e + 1, u - 3)

            act_expert(0, False)
            with act.Fori(1, E - 1) as e:
                act_expert(e, False)
            act_expert(E - 1, True)

        @block.vector
        def _(dve):
            steps = [0]

            def link(ins):
                steps[0] += 1
                ins.then_inc(s_v, 1)
                dve.wait_ge(s_v, steps[0])

            def copy_lo(dst, src, hi, signal):
                dve.tensor_tensor(dst, src, hi.bitcast(F32), ALU.subtract).then_inc(signal, 1)

            def slot_parts():
                dve.tensor_single_scalar(col_i[:, :], slot_i[:, :], 7, ALU.arith_shift_right).then_inc(s_col, 1)
                link(dve.tensor_single_scalar(lane_i[:, :], slot_i[:, :], P - 1, ALU.bitwise_and))

            dve.memset(at_least[:, 0], 1.0).then_inc(s_edge, 1)
            dve.memset(at_least[:, EC], 0.0).then_inc(s_edge, 1)
            dve.memset(tile_end[:, 0:1], 0.0).then_inc(s_edge, 1)
            dve.wait_ge(s_ids, 16)
            for e in range(1, EC):
                dve.tensor_scalar(at_least[:, e], ids_i[:, :], float(VOCAB_PART * e), None, ALU.is_ge).then_inc(s_edge, 1)
            dve.wait_ge(s_edge, EC + 2)
            dve.tensor_tensor(member1[:, :, :], at_least[:, 0:EC], at_least[:, 1:EC + 1],
                              ALU.subtract).then_inc(s_mem1, 1)
            dve.wait_ge(s_cnt1, 1)
            dve.wait_ge(s_const, 13)
            totals = ps[:, 4, 0:EC * NT]
            within = ps[:, 4, EC * NT:2 * EC * NT].rearrange("p (e j) -> p e j", e=EC)
            link(dve.tensor_tensor_scan(run1[:, :, :].rearrange("p e j -> p (e j)"),
                                        restart[:, :, :].rearrange("p e j -> p (e j)"), totals, 0.0, ALU.mult, ALU.add))
            link(dve.tensor_scalar(tiles_i[:, :], run1[:, :, NT - 1], float(P - 1), None, ALU.add))
            link(dve.tensor_single_scalar(tiles_i[:, :], tiles_i[:, :], 7, ALU.arith_shift_right))
            link(dve.tensor_tensor_scan(tile_end[:, 1:EC + 1], ones[:, 0:EC], tiles_i[:, :], 0.0, ALU.mult, ALU.add))
            link(dve.tensor_tensor(run1[:, :, :], run1[:, :, :], within, ALU.add))
            link(dve.scalar_tensor_tensor(out=run1[:, :, :], in0=tile_end[:, 0:EC].unsqueeze(2).to_broadcast([P, EC, NT]),
                                          scalar=float(P), in1=run1[:, :, :], op0=ALU.mult, op1=ALU.add))
            link(dve.tensor_tensor(run1[:, :, :], run1[:, :, :], member1[:, :, :], ALU.mult))
            link(dve.tensor_reduce(slot_f[:, :], run1[:, :, :].rearrange("p e j -> p j e"), AX.X, ALU.add))
            link(dve.tensor_copy(slot_i[:, :], slot_f[:, :]))
            slot_parts()
            dve.tensor_tensor(pick1[:, :, :], lane[:, :].unsqueeze(1).to_broadcast([P, NT, P]),
                              lane_i[:, :].unsqueeze(2).to_broadcast([P, NT, P]), ALU.is_equal).then_inc(s_pick1, 1)
            G = GT + 1
            dve.wait_ge(s_col, 1)
            link(dve.tensor_tensor(vals1[:, :, 1, :], lane[:, 0:G].unsqueeze(1).to_broadcast([P, NT, G]),
                                   col_i[:, :].unsqueeze(2).to_broadcast([P, NT, G]), ALU.is_equal))
            dve.tensor_tensor(vals1[:, :, 0, :], vals1[:, :, 1, :].bitcast(F32),
                              tok_pj[:, :].unsqueeze(2).to_broadcast([P, NT, G]), ALU.mult).then_inc(s_pick1, 1)
            link(dve.tensor_scalar(tile_e[:, :], lane[:, 0:G], tile_end[:, 1:2], None, ALU.is_ge))
            for e in range(2, EC):
                link(dve.scalar_tensor_tensor(out=tile_e[:, :] if e < EC - 1 else tile_ei[:, :], in0=lane[:, 0:G],
                                              scalar=tile_end[:, e:e + 1], in1=tile_e[:, :], op0=ALU.is_ge, op1=ALU.add))

            def lo_ctx(n):
                e, k = n // 2, n % 2 * 2
                dve.wait_ge(s_cth, n + 1)
                copy_lo(ctx_t[:, e, LO, k:k + 2, :], ps[:, CTX_BANK[n % 3]:CTX_BANK[n % 3] + 2, :],
                        ctx_t[:, e, HI, k:k + 2, :], s_ctl)

            for n in range(2):
                lo_ctx(n)
            dve.wait_ge(s_perm1, 1)
            found = ps[:, 5, 0:2 * G].rearrange("p (w c) -> p w c", w=2)
            link(dve.tensor_scalar(put1_f[:, :], found[:, 1], -float(T), float(T), ALU.mult, ALU.add))
            link(dve.tensor_tensor(put1_f[:, :], put1_f[:, :], found[:, 0], ALU.add))
            dve.tensor_scalar(get1[:, :], put1_f[:, :], float(T - 1), None, ALU.min).then_inc(s_tab1, 1)
            dve.tensor_copy(put1[:, :], put1_f[:, :]).then_inc(s_tab1, 1)

            def stats(src, part, s_part, mv, s_st, k):
                apart(dve, s_passed[0])
                dve.bn_stats(part[:, :], src).then_inc(s_part, 1)
                after(dve, s_part, k + 1)
                apart(dve, s_passed[0])
                dve.bn_aggr(mv[:, :], part[:, :]).then_inc(s_st, 1)

            def stats_x(k, q, c):
                after(dve, s_xin[c], 16 * (q + 1))
                after(dve, s_h1, k)
                stats(x_in[:, c], part1, s_part1, mv1, s_st1, k)

            def norm_x(k, c):
                after(dve, s_rs1, k + 1)
                after(dve, s_t1, k)
                dve.tensor_scalar(h1, x_in[:, c], mv1[:, 0:1], rstd1[:, 0:1],
                                  ALU.subtract, ALU.mult).then_inc(s_h1, 1)

            def lo_h1(k):
                after(dve, s_hi1, k + 1)
                copy_lo(h1_t[:, LO], ps[:, 0, :].rearrange("p (k m) -> p k m", k=KD), h1_t[:, HI], s_lo1)

            def dve_step(i, q, c):
                if inside(i, 0, GT):
                    after(dve, s_m2, i + 1)
                    after(dve, s_xout[c % 2], 16 * (2 * q + c // 2))
                    dve.tensor_tensor(x1[:, c % 2], x_in[:, c], ps[:, 3, :], ALU.add).then_inc(s_x1, 1)
                if inside(i, -2, GT - 3):
                    norm_x(i + 3, (c + 3) % 4)
                if inside(i, -1, GT - 1):
                    after(dve, s_hi2, i + 2)
                    copy_lo(a1_t[:, LO], ps[:, 1, :].rearrange("p (k m) -> p k m", k=KD), a1_t[:, HI], s_lo2)
                if inside(i, 0, GT):
                    after(dve, s_x1, i + 1)
                    after(dve, s_h2, i)
                    stats(x1[:, c % 2], part2, s_part2, mv2, s_st2, i)
                if inside(i, -2, GT - 2):
                    after(dve, s_sl1, i + 3)
                    dve.tensor_tensor(gated[:, 0], gated[:, 0], ps[:, 2, :],
                                      ALU.mult).then_inc(s_a1, 1)
                if inside(i, -2, GT - 3):
                    lo_h1(i + 3)
                if inside(i, 0, GT):
                    after(dve, s_rs2, i + 1)
                    after(dve, s_hout[c % 2], 16 * (2 * q + c // 2))
                    dve.tensor_scalar(h2[:, c % 2], x1[:, c % 2], mv2[:, 0:1], rstd2[:, 0:1],
                                      ALU.subtract, ALU.mult).then_inc(s_h2, 1)
                if inside(i, -4, GT - 4):
                    stats_x(i + 4, q + 1, c)

            for n in range(2, EC * 2 - 2):
                lo_ctx(n)
            dve_step(-4, -1, 0)
            lo_ctx(EC * 2 - 2)
            norm_x(0, 0)
            lo_ctx(EC * 2 - 1)
            lo_h1(0)
            stats_x(1, 0, 1)
            for i in range(-2, 4):
                dve_step(i, i // 4, i % 4)
            dve.wait_ge(s_rt_hi, 1)
            copy_lo(rt_w[:, :, LO, :], rt_raw[:, :, :], rt_w[:, :, HI, :], s_rt_lo)
            with dve.Fori(1, rounds) as q:
                for c in range(4):
                    dve_step(4 * q + c, q, c)
            for i in range(4 * rounds, GT):
                dve_step(i, i // 4, i % 4)

            def lo_up_shared(j, g):
                after(dve, s_uh, j * 2 + g + 1)
                copy_lo(sh_u[:, g, LO], raw_u[:, j % 2, g], sh_u[:, g, HI], s_ul)

            def lo_down_shared(j):
                after(dve, s_dh, j + 1)
                copy_lo(sh_d[:, LO], raw_d[:, j % 2], sh_d[:, HI], s_dl)

            def lo_expert_up(e, c):
                q = NJ + e * NC + c
                for g in range(2):
                    after(dve, s_uh, q * 2 + g + 1)
                    copy_lo(up_w[:, c, g, LO, :, 0:CH[c]], expert_raw(e, c)[0][:, g],
                            up_w[:, c, g, HI, :, 0:CH[c]], s_ul)

            def lo_expert_down(e, c):
                q = NJ + e * NC + c
                after(dve, s_dh, q + 1)
                copy_lo(dn_w[0:CH[c], e % 2, c, LO], expert_raw(e, c)[1], dn_w[0:CH[c], e % 2, c, HI], s_dl)

            def lo_h2(u):
                dve.wait_ge(s_tth, u + 1)
                cols = slice(u * P, (u + 1) * P)
                copy_lo(h2_t[:, LO, :, cols], ps[:, h2_bank(u), :].rearrange("p (k m) -> p k m", k=KD),
                        h2_t[:, HI, :, cols], s_ttl)

            def add_down(j, b, t):
                after(dve, s_dn, (j * NB + b) * BT + t + 1)
                y = acc[:, b * BT + t, :]
                dve.tensor_tensor(y, y, ps[:, 2 + t, :], ALU.add).then_inc(s_add, 1)

            def dve_block(j, b, first, last):
                n = j * NB + b
                jp, bp = (j, b - 1) if b else (j - 1, NB - 1)
                if b == NB - 1 and not last:
                    lo_up_shared(j + 1, 0)
                for u in turns_early(n):
                    lo_h2(u)
                after(dve, s_sl, n + 1)
                after(dve, s_u, n + 1)
                dve.tensor_tensor(gated[:, b % 2], gated[:, b % 2], ps[:, 1, :], ALU.mult).then_inc(s_mul, 1)
                if b == NB - 1 and not last:
                    lo_up_shared(j + 1, 1)
                for u in turns_late(n):
                    lo_h2(u)
                if not first:
                    add_down(jp, bp, 0)
                    add_down(jp, bp, 1)
                after(dve, s_ah, n + 1)
                copy_lo(a2_t[:, b % 2, LO], gated[:, b % 2], a2_t[:, b % 2, HI], s_al)
                if not first:
                    add_down(jp, bp, 2)
                    add_down(jp, bp, 3)
                if b == 0:
                    lo_down_shared(j)

            over_e = [P, NT, E]

            def choose(k):
                link(dve.tensor_reduce(top[:, k], cand[:, :, :], AX.X, ALU.max))
                link(dve.tensor_tensor(hot[:, k], cand[:, :, :], top[:, k].unsqueeze(2).to_broadcast(over_e), ALU.is_equal))
                link(dve.tensor_tensor(hot[:, k], hot[:, k], descend[:, :].unsqueeze(1).to_broadcast(over_e), ALU.mult))
                link(dve.tensor_reduce(first[:, :], hot[:, k], AX.X, ALU.max))
                link(dve.tensor_tensor(hot[:, k], descend[:, :].unsqueeze(1).to_broadcast(over_e),
                                       first[:, :].unsqueeze(2).to_broadcast(over_e), ALU.is_equal))

            def top_first():
                dve.wait_ge(s_lg, 1)
                halves = ps[:, 6, 0:NT * 2 * E].rearrange("p (t h e) -> p t h e", t=NT, h=2)
                link(dve.tensor_copy(logit[:, :, :], halves[:, :, LO]))
                link(dve.tensor_tensor(logit[:, :, :], logit[:, :, :], halves[:, :, HI], ALU.add))
                link(dve.tensor_copy(cand[:, :, :], logit[:, :, :]))
                choose(0)

            def top_second():
                link(dve.scalar_tensor_tensor(out=cand[:, :, :], in0=hot[:, 0], scalar=-3e38, in1=logit[:, :, :],
                                              op0=ALU.mult, op1=ALU.add))
                choose(1)
                dve.tensor_tensor(member2[:, :, :], hot[:, 0], hot[:, 1], ALU.add).then_inc(s_mem2, 1)
                dve.tensor_tensor(gap[:, :], top[:, 1], top[:, 0], ALU.subtract).then_inc(s_gap, 1)

            def top_weights():
                dve.wait_ge(s_exp, 1)
                link(dve.tensor_scalar(first[:, :], exp_gap[:, :], 1.0, None, ALU.add))
                link(dve.reciprocal(weight[:, 0], first[:, :]))
                link(dve.tensor_tensor(weight[:, 1], exp_gap[:, :], weight[:, 0], ALU.mult))

            def positions():
                dve.wait_ge(s_cnt2, 1)
                totals2 = ps[:, 7, 0:NT * E].rearrange("p (t e) -> p t e", t=NT)
                within2 = ps[:, 7, NT * E:2 * NT * E].rearrange("p (t e) -> p t e", t=NT)
                for e in range(E):
                    dve.tensor_tensor_scan(run2[:, :, e], ones[:, 0:NT], totals2[:, :, e], 0.0,
                                           ALU.mult, ALU.add).then_inc(s_scan, 1)
                dve.wait_ge(s_scan, E)
                link(dve.tensor_tensor(run2[:, :, :], run2[:, :, :], within2, ALU.add))
                link(dve.tensor_scalar(late[:, :, :], run2[:, :, :], float(CAP), float(2 * E * CAP), ALU.is_ge, ALU.mult))
                link(dve.tensor_tensor(late[:, :, :], late[:, :, :], run2[:, :, :], ALU.add))
                link(dve.tensor_tensor(late[:, :, :], late[:, :, :], slot0[:, :].unsqueeze(1).to_broadcast(over_e), ALU.add))

            def choice_slots(k):
                link(dve.tensor_tensor(run2[:, :, :], hot[:, k], late[:, :, :], ALU.mult))
                link(dve.tensor_reduce(slot_f[:, :], run2[:, :, :], AX.X, ALU.add))
                link(dve.tensor_copy(slot_i[:, :], slot_f[:, :]))
                slot_parts()
                link(dve.tensor_copy(w_hl[:, HI], weight[:, k]))
                link(dve.tensor_tensor(w_hl[:, LO], weight[:, k], w_hl[:, HI].bitcast(F32), ALU.subtract))

            def choice_pick(k):
                if k:
                    dve.wait_ge(s_perm2, 1)
                dve.tensor_tensor(pick2[:, :, :], lane[:, :].unsqueeze(1).to_broadcast([P, NT, P]),
                                  lane_i[:, :].unsqueeze(2).to_broadcast([P, NT, P]), ALU.is_equal).then_inc(s_pick2, 1)

            def choice_vals(k):
                cols = [P, NT, SLOTS]
                dve.wait_ge(s_col, k + 2)
                link(dve.tensor_tensor(vals2[:, :, 1, :], lane[:, 0:SLOTS].unsqueeze(1).to_broadcast(cols),
                                       col_i[:, :].unsqueeze(2).to_broadcast(cols), ALU.is_equal))
                for w, v in ((0, tok_tp[:, :]), (2, w_hl[:, HI].bitcast(F32)), (3, w_hl[:, LO].bitcast(F32))):
                    dve.tensor_tensor(vals2[:, :, w, :], vals2[:, :, 1, :].bitcast(F32),
                                      v.unsqueeze(2).to_broadcast(cols), ALU.mult).then_inc(s_pick2, 1)

            def slot_tables():
                dve.wait_ge(s_perm2, 2)
                got = ps[:, 7, 256:256 + 4 * SLOTS].rearrange("p (w c) -> p w c", w=4)
                link(dve.tensor_scalar(put2_f[:, :], got[:, 1], -float(T), float(T), ALU.mult, ALU.add))
                link(dve.tensor_tensor(put2_f[:, :], put2_f[:, :], got[:, 0], ALU.add))
                link(dve.tensor_copy(put2[:, :], put2_f[:, :]))
                link(dve.tensor_scalar(get2[:, :], put2_f[:, :], float(T - 1), None, ALU.min))
                link(dve.tensor_copy(slot_w[:, :], got[:, 2]))
                link(dve.tensor_tensor(slot_w[:, :], slot_w[:, :], got[:, 3], ALU.add))
                dve.memset(ve1[:, :], 0.0).then_inc(s_tab2, 1)

            extra = {6: [top_first], 7: [top_second], 8: [top_weights], 9: [positions],
                     10: [lambda: choice_slots(0), lambda: choice_pick(0)], 11: [lambda: choice_vals(0)],
                     12: [lambda: choice_slots(1)], 13: [lambda: choice_pick(1)],
                     14: [lambda: choice_vals(1)], 15: [slot_tables]}
            lo_up_shared(0, 0)
            lo_up_shared(0, 1)
            for u in range(BT):
                lo_h2(u)
            for j in range(4):
                for b in range(NB):
                    n = j * NB + b
                    if 1 <= n <= NB:
                        dve.wait_ge(s_yin[n - 1], 16)
                    dve_block(j, b, n == 0, False)
                    for piece in extra.get(n, ()):
                        piece()
            with dve.Fori(4, NJ - 1) as j:
                for b in range(NB):
                    dve_block(j, b, False, False)

            def lo_g(e, t):
                after(dve, s_th3, e * CT + t + 1)
                copy_lo(g_t[:, e % 2, LO, :, t * P:(t + 1) * P],
                        ps[:, 6 + t % 2, :].rearrange("p (k m) -> p k m", k=KD),
                        g_t[:, e % 2, HI, :, t * P:(t + 1) * P], s_tl3)

            def dve_unit(e, u):
                h, c = u // NC, u % NC
                v, m, t0, t1 = e * 6 + u, CH[c], HALF[h][0], HALF[h][1]
                n = (t1 - t0) * P
                after(dve, s_sl3, v + 1)
                after(dve, s_u3, v + 1)
                dve.tensor_tensor(gated[0:m, u % 2, 0:n], gated[0:m, u % 2, 0:n], ps[0:m, 1, 0:n],
                                  ALU.mult).then_inc(s_mul3, 1)
                after(dve, s_ah3, v + 1)
                copy_lo(a3_t[0:m, c, LO, t0 * P:t1 * P], gated[0:m, u % 2, 0:n],
                        a3_t[0:m, c, HI, t0 * P:t1 * P], s_al3)

            def weighted(e, t):
                after(dve, s_d3, e * CT + t + 1)
                after(dve, s_oin[t], 16 * (e + 1))
                dve.scalar_tensor_tensor(out=out_new[:, t], in0=ps[:, 2 + t % 4, :],
                                         scalar=slot_w[:, bass.ds(e * CT + t, 1)], in1=out_new[:, t],
                                         op0=ALU.mult, op1=ALU.add).then_inc(s_y3, 1)

            for b in range(NB):
                dve_block(NJ - 1, b, False, True)
                if b < NC:
                    lo_expert_up(0, b)
                for t in EARLY[b]:
                    lo_g(0, t)
            for t in range(BT):
                add_down(NJ - 1, NB - 1, t)
            def dve_expert(e, first, last):
                for u in range(6):
                    dve_unit(e, u)
                    if u < 3:
                        if first:
                            lo_expert_down(0, u)
                        else:
                            weighted(e - 1, 2 + u)
                        if not last:
                            lo_g(e + 1, u)
                    if u >= 3:
                        if not last:
                            if u == 4:
                                lo_g(e + 1, 3)
                            if u == 5:
                                lo_g(e + 1, 4)
                            lo_expert_up(e + 1, u - 3)
                            lo_expert_down(e + 1, u - 3)
                        if u < 5:
                            weighted(e, u - 3)

            dve_expert(0, True, False)
            with dve.Fori(1, E - 1) as e:
                dve_expert(e, False, False)
            dve_expert(E - 1, False, True)
            for t in range(HALF[1][0], CT):
                weighted(E - 1, t)

        @block.tensor
        def _(pe):
            pe.wait_ge(s_const, 9)
            pe.wait_ge(s_mem1, 1)
            flat = member1[:, :, :].rearrange("p e j -> p (e j)")
            pe.matmul(ps[:, 4, 0:EC * NT], ones[:, :], flat, start=True, stop=True)
            pe.matmul(ps[:, 4, EC * NT:2 * EC * NT], not_below[:, :], flat, start=True, stop=True).then_inc(s_cnt1, 1)

            def turn_ctx(n):
                e, k0 = n // 2, n % 2 * 2
                if n % 2 == 0:
                    pe.wait_ge(s_ctx[e], 16)
                if n >= 3:
                    pe.wait_ge(s_ctl, n - 2)
                for k in range(2):
                    for r in range(KD):
                        mm = pe.transpose(ps[:, CTX_BANK[n % 3] + k, r * P:(r + 1) * P],
                                          ctx_raw[:, e, r, (k0 + k) * P:(k0 + k + 1) * P], ident[:, :])
                mm.then_inc(s_ct, 1)

            for n in range(3):
                turn_ctx(n)
            pe.wait_ge(s_pick1, 2)
            for j in range(NT):
                mm = pe.matmul(ps[:, 5, 0:2 * (GT + 1)], pick1[:, j, :], vals1[:, j].rearrange("p w c -> p (w c)"),
                               start=(j == 0), stop=(j == NT - 1))
            mm.then_inc(s_perm1, 1)
            for n in range(3, EC * 2):
                turn_ctx(n)

            def turn(bank, src):
                for k in range(KD):
                    mm = pe.transpose(ps[:, bank, k * P:(k + 1) * P], src[:, k * P:(k + 1) * P], ident[:, :])
                return mm

            def by_ctx(bank, lhs, e, lo_ready, count):
                n = 0
                for a, b in ((HI, LO), (LO, HI), (HI, HI)):
                    if a == LO:
                        after(pe, lo_ready, count)
                    for k in range(KD):
                        mm = pe.matmul(ps[:, bank, :], lhs[:, a, k, :],
                                       area_a[:, bass.ds(e * (2 * KD * D) + (b * KD + k) * D, D)],
                                       start=(n == 0), stop=(n == 3 * KD - 1))
                        n += 1
                return mm

            def tile_expert(k):
                return pe.value_load(tile_ei[0:1, bass.ds(k, 1)], min_val=0, max_val=EC - 1)

            def keep_warm(bank, count):
                for n in range(count):
                    pe.matmul(ps[:, bank, :], ctx_t[:, 0, HI, 0, 0:P], ctx_t[:, 0, HI, 0, :], start=True, stop=True)

            def pe_step(i):
                if inside(i, -1, GT - 1):
                    next_expert = tile_expert(i + 1)
                if inside(i, 0, GT):
                    expert = tile_expert(i)
                    after(pe, s_a1, i + 1)
                    after(pe, s_lo2, i)
                    turn(1, gated[:, 0]).then_inc(s_t2, 1)
                if isinstance(i, int) and i == -1:
                    pe.wait_ge(s_ctl, EC * 2)
                if inside(i, -1, GT - 1):
                    after(pe, s_hi1, i + 2)
                    by_ctx(2, h1_t, next_expert, s_lo1, i + 2).then_inc(s_m1, 1)
                if inside(i, -2, GT - 2):
                    after(pe, s_h1, i + 3)
                    after(pe, s_lo1, i + 2)
                    turn(0, h1).then_inc(s_t1, 1)
                if inside(i, 0, GT):
                    after(pe, s_hi2, i + 1)
                    after(pe, s_x1, i)
                    by_ctx(3, a1_t, expert, s_lo2, i + 1).then_inc(s_m2, 1)

            keep_warm(4, 12)
            pe.wait_ge(s_ctl, EC * 2 - 1)
            pe_step(-2)
            for i in range(-1, 1):
                pe_step(i)
            with pe.Fori(1, GT - 2) as i:
                pe_step(i)
            for i in range(GT - 2, GT):
                pe_step(i)

            def turn_h2(u):
                pe.wait_ge(s_hin[u % 8], 16 * (u // 8 + 1))
                if u >= 8:
                    pe.wait_ge(s_ttl, u - 1)
                elif u >= 4:
                    pe.wait_ge(s_ttl, u - 3)
                turn(h2_bank(u), h2_in[:, u % 8]).then_inc(s_tt, 1)

            def up(j, b, g, signal):
                i = 0
                for w, m in PASSES:
                    if m == LO and g == 0 and isinstance(j, int) and j == 0:
                        pe.wait_ge(s_ttl, (b + 1) * BT)
                    for k in range(KD):
                        mm = pe.matmul(ps[:, g, :], sh_u[:, g, w, k, :], h2_t[:, m, k, b * N:(b + 1) * N],
                                       start=(i == 0), stop=(i == 3 * KD - 1))
                        i += 1
                mm.then_inc(signal, 1)

            def up_block(j, b):
                n = j * NB + b
                after(pe, s_ul, j * 2 + 1)
                after(pe, s_sl, n)
                up(j, b, 0, s_g)
                for u in turns_early(n):
                    turn_h2(u)
                after(pe, s_ul, j * 2 + 2)
                after(pe, s_mul, n)
                up(j, b, 1, s_u)
                for u in turns_late(n):
                    turn_h2(u)

            def down_block(j, b):
                n = j * NB + b
                after(pe, s_al, n + 1)
                after(pe, s_dl, j + 1)
                for t in range(BT):
                    after(pe, s_add, (n - 1) * BT + t + 1)
                    for i, (a, w) in enumerate(PASSES):
                        mm = pe.matmul(ps[:, 2 + t, :], a2_t[:, b % 2, a, t * P:(t + 1) * P], sh_d[:, w, :],
                                       start=(i == 0), stop=(i == 2))
                    mm.then_inc(s_dn, 1)

            def router_logits(b):
                if b >= 2:
                    pe.wait_ge(s_lgc, b - 1)
                i = 0
                for a in (LO, HI):
                    for k in range(KD):
                        mm = pe.matmul(ps[0:2 * E, 6 + b % 2, :], rt_w[:, k].rearrange("p h e -> p (h e)"),
                                       h2_t[:, a, k, b * N:(b + 1) * N], start=(i == 0), stop=(i == 2 * KD - 1))
                        i += 1
                mm.then_inc(s_lgt, 1)

            def turn_logits():
                pe.wait_ge(s_lgc, NB)
                for t in range(NT):
                    mm = pe.transpose(ps[:, 6, t * 2 * E:(t + 1) * 2 * E], logit_rows[:, t * P:(t + 1) * P],
                                      ident[0:2 * E, 0:2 * E])
                mm.then_inc(s_lg, 1)

            def choice_perm(k):
                pe.wait_ge(s_pick2, 4 * (k + 1))
                for j in range(NT):
                    mm = pe.matmul(ps[:, 7, 256:256 + 4 * SLOTS], pick2[:, j, :],
                                   vals2[:, j].rearrange("p w c -> p (w c)"),
                                   start=(k == 0 and j == 0), stop=(k == 1 and j == NT - 1))
                mm.then_inc(s_perm2, 1)

            keep_warm(2, 38)
            for u in range(BT):
                turn_h2(u)
            for j in range(4):
                for b in range(NB):
                    n = j * NB + b
                    if n < NB:
                        pe.wait_ge(s_tth, (n + 1) * BT)
                    up_block(j, b)
                    if n:
                        jp, bp = (j, b - 1) if b else (j - 1, NB - 1)
                        down_block(jp, bp)
                    if n == 3:
                        pe.wait_ge(s_rt_lo, 1)
                    if 3 <= n < 5:
                        router_logits(2 * n - 6)
                        router_logits(2 * n - 5)
                    if n == 5:
                        turn_logits()
                    if n == 8:
                        pe.wait_ge(s_mem2, 1)
                        flat2 = member2[:, :, :].rearrange("p t e -> p (t e)")
                        pe.matmul(ps[:, 7, 0:NT * E], ones[:, :], flat2, start=True, stop=True)
                        pe.matmul(ps[:, 7, NT * E:2 * NT * E], not_below[:, :], flat2,
                                  start=True, stop=True).then_inc(s_cnt2, 1)
                    if n == 12:
                        choice_perm(0)
                    if n == 15:
                        choice_perm(1)
            with pe.Fori(4, NJ - 1) as j:
                for b in range(NB):
                    up_block(j, b)
                    down_block(j if b else j - 1, (b - 1) % NB)

            def turn_g(e, t):
                w = e * CT + t
                after(pe, s_gin[t], 16 * (e + 1))
                after(pe, s_tl3, w - (t > 0))
                turn(6 + t % 2, g_in[:, t]).then_inc(s_t3, 1)

            def up_unit(e, u):
                h, c = u // NC, u % NC
                v, m, t0, t1 = e * 6 + u, CH[c], HALF[h][0], HALF[h][1]
                n = (t1 - t0) * P
                after(pe, s_tl3, e * CT + t1)
                for g, read, signal in ((0, s_sl3, s_g3), (1, s_mul3, s_u3)):
                    after(pe, s_ul, (NJ + e * NC + c) * 2 + g + 1)
                    after(pe, read, v)
                    i = 0
                    for w, a in PASSES:
                        for k in range(KD):
                            mm = pe.matmul(ps[0:m, g, 0:n], up_w[:, c, g, w, k, 0:m],
                                           g_t[:, e % 2, a, k, t0 * P:t1 * P],
                                           start=(i == 0), stop=(i == 3 * KD - 1))
                            i += 1
                    mm.then_inc(signal, 1)

            def down_part(e, t, chunks):
                h = 0 if t < HALF[0][1] else 1
                after(pe, s_al3, e * 6 + h * NC + chunks[-1] + 1)
                after(pe, s_dl, NJ + (e + 1) * NC)
                for a, w in PASSES:
                    for c in chunks:
                        mm = pe.matmul(ps[:, 2 + t % 4, :], a3_t[0:CH[c], c, a, t * P:(t + 1) * P],
                                       dn_w[0:CH[c], e % 2, c, w, :], start=(a == LO and c == 0),
                                       stop=(a == HI and w == HI and c == NC - 1))
                return mm

            def down_unit(e, t):
                after(pe, s_y3, e * CT + t - (t > 0))
                down_part(e, t, range(NC)).then_inc(s_d3, 1)

            for b in range(NB):
                up_block(NJ - 1, b)
                for t in EARLY[b]:
                    turn_g(0, t)
                down_block(NJ - 1 if b else NJ - 2, (b - 1) % NB)
            down_block(NJ - 1, NB - 1)

            def pe_expert(e, first, last):
                for u in range(6):
                    up_unit(e, u)
                    if u < 3 and not first:
                        down_unit(e - 1, 2 + u)
                    if 3 <= u < 5:
                        down_unit(e, u - 3)
                    if not last:
                        if u < 3:
                            turn_g(e + 1, u)
                        if u > 3:
                            turn_g(e + 1, u - 1)

            pe_expert(0, True, False)
            with pe.Fori(1, E - 1) as e:
                pe_expert(e, False, False)
            pe_expert(E - 1, False, True)
            for t in range(HALF[1][0], CT):
                after(pe, s_y3, (E - 1) * CT + t - 3)
                down_part(E - 1, t, range(NC - 1))
            for t in range(HALF[1][0], CT):
                down_part(E - 1, t, range(NC - 1, NC)).then_inc(s_d3, 1)


_INS = ['x', 'itok_BxS_13_99985', 'ctx_2048', 'L0_ffn_router', 'L0_ffn_w_up_gate', 'L0_ffn_w_down',
        'L0_ffn_shared_w_up_gate', 'L0_ffn_shared_w_down']


def kernel(**inputs):
    import numpy as np
    import concourse.bacc as bacc
    from concourse.bass_utils import run_bass_kernel_spmd

    nc = bacc.Bacc("TRN2", target_bir_lowering=False, num_devices=1)
    arrays, args = {}, []
    for name in _INS:
        a = np.ascontiguousarray(inputs[name])
        arrays[f"in_{name}"] = a
        args.append(nc.dram_tensor(f"in_{name}", a.shape, mybir.dt.from_np(a.dtype), kind="ExternalInput").ap())
    args.append(nc.dram_tensor("out_x", tuple(inputs["x"].shape), F32, kind="ExternalOutput").ap())
    routed_block_program(nc, *args)
    r = run_bass_kernel_spmd(nc, [arrays], core_ids=[0])
    return r.results[0]["out_x"]
```

```python
from contextlib import ExitStack

import concourse.bass as bass
from concourse import mybir

ALU = mybir.AluOpType
ACT = mybir.ActivationFunctionType
AX = mybir.AxisListType
F32 = mybir.dt.float32
F32R = mybir.dt.float32r
I32 = mybir.dt.int32

P = 128
HI, LO = 0, 1
PASSES = ((LO, HI), (HI, LO), (HI, HI))
EPS = 1e-5


def after(eng, sem, count):
    if not isinstance(count, int) or count > 0:
        eng.wait_ge(sem, count)


def apart(eng, passed):
    eng.sem_inc(passed, 1)


def inside(i, low, high):
    return not isinstance(i, int) or low <= i < high


def h2_bank(u):
    return (6, 7, 4, 5)[u % 4] if u < 8 else 6 + u % 2


def turns_early(n):
    return ((), (8, 9), (12, 13))[n] if isinstance(n, int) and n < 3 else ()


def turns_late(n):
    return ((), (10, 11), (14, 15))[n] if isinstance(n, int) and n < 3 else ()


def routed_block_program(nc, x, ids, ctx_w, router, w_ug, w_dn, sh_ug, sh_dn, out):
    B, S, D = x.shape
    T = B * S
    KD = D // P
    NT = T // P
    EC = ctx_w.shape[0]
    E = w_ug.shape[0]
    I = w_dn.shape[1]
    J = sh_dn.shape[0]
    NJ = J // P
    CAP = -(-T * 2 * 5 // (E * 4))
    CT = CAP // P
    GT = NT + EC - 1
    VOCAB_PART = 25000 // EC
    CH = [P, P, I - 2 * P]
    NC = len(CH)
    ROUNDS = (GT - 4) // 4
    NB = 4
    BT = NT // NB
    N = BT * P
    HALF = [(0, 2), (2, CT)]
    SLOTS = E * CT
    NBLK = NJ * NB
    ROUTING = 5
    CTX_BANK = [0, 2, 6]
    EARLY = [[], [0, 1], [2, 3], [4]]
    assert D == 512 and N == 512 and CAP == 640 and J % P == 0 and 0 < CH[2] <= P

    xf = x.rearrange("b s d -> (b s) d")
    of = out.rearrange("b s d -> (b s) d")
    x1_rows = nc.dram_tensor("x1_rows", (T, D + 1), F32).ap()
    h2_rows = nc.dram_tensor("h2_rows", (T, D), F32).ap()
    logit_dram = nc.dram_tensor("logit_dram", (T, E + 1), F32).ap()

    with ExitStack() as ctx:
        def sb(name, shape, dt=F32):
            return ctx.enter_context(nc.sbuf_tensor(name, shape, dt))

        def sem(name):
            return ctx.enter_context(nc.semaphore(name))

        area_a = sb("area_a", [P, 16384], F32R)
        area_b = sb("area_b", [P, 16384], F32R)
        ctx_t = area_a[:, :].rearrange("p (e h k m) -> p e h k m", e=EC, h=2, k=KD)
        pick1 = area_b[:, 2048:4096].rearrange("p (j c) -> p j c", j=NT)
        vals1 = area_b[:, 4096:4096 + NT * 2 * (GT + 1)].rearrange("p (j w c) -> p j w c", j=NT, w=2)
        h2_t = area_b[:, :].rearrange("p (b h k n) -> p b h k n", b=NB, h=2, k=KD)
        h1_t = area_b[:, 12288:13312].rearrange("p (h k m) -> p h k m", h=2, k=KD)
        a1_t = area_b[:, 13312:14336].rearrange("p (h k m) -> p h k m", h=2, k=KD)
        sh_u0 = area_b[:, 14336:16384].rearrange("p (g h k m) -> p g h k m", g=2, h=2, k=KD)
        pick2 = area_a[:, 0:2048].rearrange("p (j c) -> p j c", j=NT)
        vals2 = area_a[:, 2048:2048 + NT * 5 * SLOTS].rearrange("p (j w c) -> p j w c", j=NT, w=5)
        up_w = area_a[:, 0:6144].rearrange("p (c g h k m) -> p c g h k m", c=NC, g=2, h=2, k=KD)
        g_t = area_a[:, 6144:16384].rearrange("p (b h k n) -> p b h k n", b=2, h=2, k=KD)
        a2_t = area_a[:, 11264:13312].rearrange("p (b h n) -> p b h n", b=2, h=2)
        sh_d = area_a[:, 13312:14336].rearrange("p (h n) -> p h n", h=2)
        sh_u = area_a[:, 14336:16384].rearrange("p (g h k m) -> p g h k m", g=2, h=2, k=KD)
        dn_w = area_b[:, 0:6144].rearrange("p (b c h n) -> p b c h n", b=2, c=NC, h=2)
        a3_t = area_b[:, 6144:9984].rearrange("p (c h n) -> p c h n", c=NC, h=2)
        rt_w = sb("rt_w", [P, KD, 2, E], F32R)

        acc = sb("acc", [P, NT, D])
        ctx_raw = acc[:, :, :].rearrange("p (e r) d -> p e r d", e=EC)
        out_new = acc
        raw_u = sb("raw_u", [P, 2, 2, KD, P])
        raw_d = sb("raw_d", [P, 2, D])
        gated = sb("gated", [P, 2, D])
        rows = sb("rows", [P, 9 * D + 2])
        x_in = rows[:, 0:4 * D].rearrange("p (s d) -> p s d", s=4)
        h1 = rows[:, 4 * D:5 * D]
        x1 = rows[:, 5 * D:7 * D + 2].rearrange("p (s d) -> p s d", s=2)
        h2 = rows[:, 7 * D + 2:9 * D + 2].rearrange("p (s d) -> p s d", s=2)
        logit_rows = rows[0:2 * E, 0:T]
        g_in = rows[:, 0:CT * D].rearrange("p (s d) -> p s d", s=CT)
        ahead_u = rows[:, CT * D:CT * D + 2 * KD * CH[2]].rearrange("p (g k m) -> p g k m", g=2, k=KD)
        ahead_d = rows[:, 8 * D:9 * D]

        def h2_in(u):
            return (acc[:, 8 + u % 4], acc[:, 4 + u % 4], acc[:, 8 + u % 4], x_in[:, u % 4])[u // 4]

        def is_first(j, b):
            return isinstance(j, int) and (j, b) == (0, 0)

        def expert_raw(e, c):
            if isinstance(e, int) and (e, c) == (0, NC - 1):
                return ahead_u, ahead_d[0:CH[c]]
            q = NJ + e * NC + c
            return raw_u[:, q % 2, :, :, 0:CH[c]], raw_d[0:CH[c], q % 2]

        ident = sb("ident", [P, P])
        ones = sb("ones", [P, P])
        not_below = sb("not_below", [P, P])
        restart = sb("restart", [P, EC, NT])
        lane = sb("lane", [P, P])
        tok_pj = sb("tok_pj", [P, NT])
        num_tp = sb("num_tp", [P, GT + 1])
        descend = sb("descend", [P, E])
        slot0 = sb("slot0", [P, E])
        expo = sb("expo", [P, 1])
        rt_raw = sb("rt_raw", [P, KD, E])
        ids_i = sb("ids_i", [P, NT], I32)
        at_least = sb("at_least", [P, EC + 1, NT])
        member1 = sb("member1", [P, EC, NT])
        run1 = sb("run1", [P, EC, NT])
        tiles_i = sb("tiles_i", [P, EC], I32)
        tile_end = sb("tile_end", [P, EC + 1])
        slot_f = sb("slot_f", [P, NT])
        slot_i = sb("slot_i", [P, NT], I32)
        lane_i = sb("lane_i", [P, NT], I32)
        col_i = sb("col_i", [P, NT], I32)
        tile_e = sb("tile_e", [P, GT + 1])
        tile_ei = sb("tile_ei", [P, GT + 1], I32)
        put1_f = sb("put1_f", [P, GT + 1])
        unpad = sb("unpad", [P, EC])
        shift1 = sb("shift1", [P, EC - 1, GT + 1])
        put1 = sb("put1", [P, GT + 1], I32)
        pos_f = sb("pos_f", [P, GT + 1])
        tok_f = sb("tok_f", [P, NT])
        tok_i = sb("tok_i", [P, NT], I32)
        get1 = sb("get1", [P, GT + 1], I32)
        get_now = sb("get_now", [P, 4], I32)
        put_now = sb("put_now", [P, 2], I32)
        part1, part2 = sb("part1", [P, 6]), sb("part2", [P, 6])
        mv1, mv2 = sb("mv1", [P, 2]), sb("mv2", [P, 2])
        ve1, ve2 = sb("ve1", [P, 1]), sb("ve2", [P, 1])
        rstd1, rstd2 = sb("rstd1", [P, 1]), sb("rstd2", [P, 1])
        logit_out = sb("logit_out", [P, NT, E + 1])
        logit_in = sb("logit_in", [P, NT, E + 1])
        logit = logit_in[:, :, 0:E]
        cand = sb("cand", [P, NT, E])
        top = sb("top", [P, 2, NT])
        first = sb("first", [P, NT])
        hot = sb("hot", [P, 2, NT, E])
        member2 = sb("member2", [P, NT, E])
        run2 = sb("run2", [P, NT, E])
        late = sb("late", [P, NT, E])
        gap = sb("gap", [P, NT])
        exp_gap = sb("exp_gap", [P, NT])
        weight = sb("weight", [P, 2, NT])
        w_hl = sb("w_hl", [P, 2, NT], F32R)
        put2_f = sb("put2_f", [P, SLOTS])
        put2 = sb("put2", [P, SLOTS], I32)
        get2 = sb("get2", [P, SLOTS], I32)
        pos2 = sb("pos2", [P, SLOTS], I32)
        slot_w = sb("slot_w", [P, SLOTS])
        g_idx = sb("g_idx", [P, CT], I32)
        o_idx = sb("o_idx", [P, CT], I32)
        p_idx = sb("p_idx", [P, CT], I32)

        ps = ctx.enter_context(nc.psum_tensor("ps", [P, 8, 512], F32))

        s_const = sem("const_ready")
        s_passed = [sem(f"waits_passed_{who}") for who in ("dve", "pool", "sp")]
        s_ids = sem("ids_landed")
        s_ctx = [sem(f"ctx{e}_landed") for e in range(EC)]
        s_rt = sem("router_landed")
        s_warm = sem("silu_table_loaded")
        s_rt_hi, s_rt_lo = sem("router_hi"), sem("router_lo")
        s_v = sem("dve_table_step")
        s_col = sem("slot_columns_ready")
        s_edge = sem("thresholds_ready")
        s_mem1, s_cnt1 = sem("member1_ready"), sem("counts1_ready")
        s_pick1, s_perm1, s_tab1 = sem("pick1_ready"), sem("perm1_ready"), sem("table1_ready")
        s_ct, s_cth, s_ctl = sem("ctx_transposed"), sem("ctx_hi"), sem("ctx_lo")
        s_idx = sem("index_column_staged")
        s_get, s_put1 = sem("get_column_staged"), sem("put_column_staged")
        s_xin = [sem(f"x_rows_landed{c}") for c in range(4)]
        s_xout = [sem(f"x1_rows_stored{c}") for c in range(2)]
        s_hout = [sem(f"h2_rows_stored{c}") for c in range(2)]
        s_part1, s_st1, s_ve1, s_rs1, s_h1 = (sem("part1_ready"), sem("stats1_ready"), sem("vareps1_ready"),
                                              sem("rstd1_ready"), sem("h1_ready"))
        s_part2, s_st2, s_ve2, s_rs2, s_h2 = (sem("part2_ready"), sem("stats2_ready"), sem("vareps2_ready"),
                                              sem("rstd2_ready"), sem("h2_ready"))
        s_t1, s_hi1, s_lo1 = sem("h1_transposed"), sem("h1_hi"), sem("h1_lo")
        s_m1, s_sl1, s_a1 = sem("z_ready"), sem("silu1_ready"), sem("a1_ready")
        s_t2, s_hi2, s_lo2 = sem("a1_transposed"), sem("a1_hi"), sem("a1_lo")
        s_m2, s_x1 = sem("y1_ready"), sem("x1_ready")
        s_hin = [sem(f"h2_tile_landed{k}") for k in range(8)]
        s_yin = [sem(f"x1_block_landed{b}") for b in range(NB)]
        s_tt, s_tth, s_ttl = sem("h2_transposed"), sem("h2_hi"), sem("h2_lo")
        s_raw = sem("weights_landed")
        s_uh, s_ul, s_dh, s_dl = sem("up_w_hi"), sem("up_w_lo"), sem("down_w_hi"), sem("down_w_lo")
        s_uh0, s_ul0 = sem("first_up_w_hi"), sem("first_up_w_lo")
        s_g, s_u, s_sl, s_mul = sem("gate_ready"), sem("up_ready"), sem("silu2_ready"), sem("gated2_ready")
        s_ah, s_al = sem("a2_hi"), sem("a2_lo")
        s_dn, s_add = sem("down_ready"), sem("acc_added")
        s_lgt, s_lgc = sem("logit_rows_ready"), sem("logit_rows_copied")
        s_lg, s_mem2, s_cnt2 = sem("logits_ready"), sem("member2_ready"), sem("counts2_ready")
        s_scan = sem("sums2_ready")
        s_gap, s_exp = sem("gap_ready"), sem("exp_ready")
        s_pick2, s_perm2, s_tab2 = sem("pick2_ready"), sem("perm2_ready"), sem("table2_ready")
        s_out = sem("output_written")
        s_unpad = sem("padding_counted")
        s_tokin, s_tok = sem("tokens_landed"), sem("token_column_ready")
        s_lrow, s_lput, s_lback = sem("logits_by_position"), sem("logits_stored"), sem("logits_by_token")
        s_gin = [sem(f"g_rows_landed{t}") for t in range(CT)]
        s_oin = [sem(f"out_rows_landed{t}") for t in range(CT)]
        s_t3, s_th3, s_tl3 = sem("g_transposed"), sem("g_hi"), sem("g_lo")
        s_g3, s_u3, s_sl3, s_mul3 = sem("gate3_ready"), sem("up3_ready"), sem("silu3_ready"), sem("gated3_ready")
        s_ah3, s_al3, s_d3, s_y3 = sem("a3_hi"), sem("a3_lo"), sem("down3_ready"), sem("rows3_ready")
        s_put = sem("rows3_stored")

        block = ctx.enter_context(nc.Block())

        @block.sync
        def _(sp):
            def hold(sem, count):
                after(sp, sem, count)
                if not isinstance(count, int):
                    apart(sp, s_passed[2])

            def load_shared(q):
                hold(s_raw, q * 48)
                hold(s_ul, (q - 1) * 2)
                hold(s_dl, q - 1)
                for g in range(2):
                    sp.dma_start(raw_u[:, q % 2, g],
                                 sh_ug.rearrange("(k p) m -> p k m", p=P)[:, :, bass.ds(q * P + g * J, P)]
                                 ).then_inc(s_raw, 16)
                sp.dma_start(raw_d[:, q % 2], sh_dn.rearrange("(j p) d -> j p d", p=P)[q]).then_inc(s_raw, 16)

            def load_expert(e, c):
                q = NJ + e * NC + c
                up, down = expert_raw(e, c)
                hold(s_raw, q * 48)
                if isinstance(e, int) and (e, c) == (0, NC - 1):
                    hold(s_tt, NT)
                else:
                    hold(s_ul, (q - 1) * 2)
                    hold(s_dl, q - 1)
                for g in range(2):
                    sp.dma_start(up[:, g],
                                 w_ug.rearrange("e (k p) m -> e p k m", p=P)[e, :, :, g * I + c * P:g * I + c * P + CH[c]]
                                 ).then_inc(s_raw, 16)
                sp.dma_start(down, w_dn[e, c * P:c * P + CH[c], :]).then_inc(s_raw, 16)

            sp.dma_start(ids_i[:, :], ids.rearrange("b (p j) -> (b p) j", j=NT)).then_inc(s_ids, 16)
            for e in range(EC):
                sp.dma_start(ctx_raw[:, e], ctx_w[e].rearrange("(r p) d -> p r d", p=P)).then_inc(s_ctx[e], 16)
            sp.dma_start(rt_raw[:, :, :], router.rearrange("(k p) e -> p k e", p=P)).then_inc(s_rt, 16)
            load_shared(0)
            load_shared(1)

            def rows_of_block(b, stored):
                tiles = ((b + 1) * N - 1 + (EC - 1) * (P - 1)) // P + 1
                for c in range(2):
                    hold(stored[c], 16 * ((tiles + 1 - c) // 2))

            def load_h2(b):
                rows_of_block(b, s_hout)
                for u in range(b * BT, (b + 1) * BT):
                    sp.dma_start(h2_in(u), h2_rows[u * P:(u + 1) * P, :]).then_inc(s_hin[u % 8], 16)

            def load_x1(b):
                rows_of_block(b, s_xout)
                sp.dma_start(acc[:, b * BT:(b + 1) * BT, :],
                             x1_rows[b * N:(b + 1) * N, 0:D].rearrange("(r p) d -> p r d", p=P)).then_inc(s_yin[b], 16)

            load_h2(0)
            load_h2(1)
            hold(s_tt, BT)
            load_h2(2)
            load_x1(0)
            hold(s_x1, GT)
            load_h2(3)
            hold(s_tt, 2 * BT)
            load_x1(1)
            hold(s_tt, 3 * BT)
            load_x1(2)
            load_x1(3)
            sp.dma_start(tok_f[:, :].unsqueeze(2), x1_rows.rearrange("(t p) d -> p t d", p=P)[:, :, D:D + 1],
                         allow_slow_non_contiguous=True).then_inc(s_tokin, 16)
            with sp.Fori(2, NJ) as q:
                load_shared(q)
            for c in range(NC):
                load_expert(0, c)
            with sp.Fori(1, E) as e:
                for c in range(NC):
                    load_expert(e, c)

        @block.gpsimd
        def _(pool):
            def hold(sem, count):
                after(pool, sem, count)
                if not isinstance(count, int):
                    apart(pool, s_passed[1])

            pool.memset(ident[:, :], 0.0).then_inc(s_const, 1)
            pool.memset(ones[:, :], 1.0).then_inc(s_const, 1)
            pool.memset(not_below[:, :], 0.0).then_inc(s_const, 1)
            pool.memset(expo[:, :], -0.5).then_inc(s_const, 1)
            pool.iota(lane[:, :], pattern=[[1, P]], base=0, channel_multiplier=0,
                      allow_small_or_imprecise_dtypes=True).then_inc(s_const, 1)
            pool.iota(tok_pj[:, :], pattern=[[1, NT]], base=0, channel_multiplier=NT,
                      allow_small_or_imprecise_dtypes=True).then_inc(s_const, 1)
            pool.memset(restart[:, :, :], 1.0).then_inc(s_const, 1)
            pool.wait_ge(s_const, 7)
            pool.affine_select(out=ident[:, :], in_=ident[:, :], compare_op=ALU.not_equal, fill=1.0, base=0,
                               pattern=[[-1, P]], channel_multiplier=1).then_inc(s_const, 1)
            pool.affine_select(out=not_below[:, :], in_=not_below[:, :], compare_op=ALU.is_gt, fill=-1.0, base=0,
                               pattern=[[1, P]], channel_multiplier=-1).then_inc(s_const, 1)
            pool.memset(restart[:, :, 0:1], 0.0).then_inc(s_const, 1)
            pool.iota(num_tp[:, :], pattern=[[P, GT + 1]], base=0, channel_multiplier=1,
                      allow_small_or_imprecise_dtypes=True).then_inc(s_const, 1)
            pool.iota(descend[:, :], pattern=[[-1, E]], base=E, channel_multiplier=0,
                      allow_small_or_imprecise_dtypes=True).then_inc(s_const, 1)
            pool.iota(slot0[:, :], pattern=[[CAP, E]], base=0, channel_multiplier=0,
                      allow_small_or_imprecise_dtypes=True).then_inc(s_const, 1)

            def gather(k, q, c):
                hold(s_x1, k - 3)
                pool.tensor_copy(get_now[:, c:c + 1], get1[:, bass.ds(k, 1)]).then_inc(s_get, 1)
                hold(s_get, k + 1)
                pool.indirect_dma_start(x_in[:, c], None, xf,
                                        bass.IndirectOffsetOnAxis(ap=get_now[:, c:c + 1], axis=0),
                                        bounds_check=T - 1, oob_is_err=False).then_inc(s_xin[c], 16)

            def scatter_x(k, c, before):
                hold(s_xout[c], 16 * before)
                hold(s_hout[c], 16 * before)
                pool.tensor_copy(put_now[:, c:c + 1], put1[:, bass.ds(k, 1)]).then_inc(s_put1, 1)
                hold(s_put1, k + 1)
                hold(s_x1, k + 1)
                hold(s_tok, k + 1)
                pool.indirect_dma_start(x1_rows, bass.IndirectOffsetOnAxis(ap=put_now[:, c:c + 1], axis=0),
                                        x1[:, c], None, bounds_check=T - 1, oob_is_err=False).then_inc(s_xout[c], 16)

            def scatter_h(k, c):
                hold(s_h2, k + 1)
                pool.indirect_dma_start(h2_rows, bass.IndirectOffsetOnAxis(ap=put_now[:, c:c + 1], axis=0),
                                        h2[:, c], None, bounds_check=T - 1, oob_is_err=False).then_inc(s_hout[c], 16)

            def root(st, mv, ve, s_ve, rstd, s_rs, k):
                hold(st, k + 1)
                pool.tensor_scalar(ve[:, :], mv[:, 1:2], EPS, 1.0, ALU.add, ALU.mult).then_inc(s_ve, 1)
                hold(s_ve, k + 1)
                pool.tensor_tensor(rstd[:, :], ve[:, :], expo[:, :], ALU.pow).then_inc(s_rs, 1)

            def pool_step(i, q, c):
                if inside(i, 0, GT - 4):
                    gather(i + 4, q + 1, c)
                if inside(i, 0, GT):
                    scatter_x(i, c % 2, 2 * q + c // 2)
                    root(s_st2, mv2, ve2, s_ve2, rstd2, s_rs2, i)
                    scatter_h(i, c % 2)
                if inside(i, -4, GT - 4):
                    root(s_st1, mv1, ve1, s_ve1, rstd1, s_rs1, i + 4)

            pool.wait_ge(s_tab1, 1)
            for k in range(4):
                gather(k, 0, k)
            for i in range(-4, 4):
                if i == 0:
                    pool.wait_ge(s_tab1, 2)
                pool_step(i, i // 4, i % 4)
            with pool.Fori(1, ROUNDS) as q:
                for c in range(4):
                    pool_step(4 * q + c, q, c)
            for i in range(4 * ROUNDS, GT):
                pool_step(i, i // 4, i % 4)

            def gather_g(e, tiles):
                if 0 in tiles:
                    for t in range(CT):
                        hold(s_gin[t], 16 * e)
                    pool.tensor_copy(g_idx[:, :], pos2[:, bass.ds(e * CT, CT)]).then_inc(s_idx, 1)
                    hold(s_idx, 1 if isinstance(e, int) and e == 0 else e * 3 - 1)
                for t in tiles:
                    hold(s_t3, (e - 1) * CT + t + 1)
                    pool.indirect_dma_start(g_in[:, t], None, h2_rows,
                                            bass.IndirectOffsetOnAxis(ap=g_idx[:, t:t + 1], axis=0),
                                            bounds_check=T - 1, oob_is_err=False).then_inc(s_gin[t], 16)

            def gather_out(e, more):
                hold(s_put, 16 * CT * e)
                staged = e * 3 + (4 if more else 3)
                pool.tensor_copy(o_idx[:, :], get2[:, bass.ds(e * CT, CT)]).then_inc(s_idx, 1)
                pool.tensor_copy(p_idx[:, :], put2[:, bass.ds(e * CT, CT)]).then_inc(s_idx, 1)
                hold(s_idx, staged)
                for t in range(CT):
                    pool.indirect_dma_start(out_new[:, t], None, of,
                                            bass.IndirectOffsetOnAxis(ap=o_idx[:, t:t + 1], axis=0),
                                            bounds_check=T - 1, oob_is_err=False).then_inc(s_oin[t], 16)
                for t in range(CT):
                    hold(s_oin[t], 16 * (e + 1))

            def store_out(e, t):
                hold(s_y3, e * CT + t + 1)
                pool.indirect_dma_start(of, bass.IndirectOffsetOnAxis(ap=p_idx[:, t:t + 1], axis=0),
                                        out_new[:, t], None, bounds_check=T - 1, oob_is_err=False).then_inc(s_put, 16)

            def store_block(b):
                for t in range(b * BT, (b + 1) * BT):
                    pool.wait_ge(s_add, NBLK * BT - NT + t + 1)
                    pool.indirect_dma_start(of, bass.IndirectOffsetOnAxis(ap=tok_i[:, t:t + 1], axis=0),
                                            acc[:, t], None, bounds_check=T - 1, oob_is_err=False).then_inc(s_out, 16)

            def pool_expert(e, first, ahead, last):
                if not first:
                    for t in range(HALF[1][0], CT):
                        store_out(e - 1, t)
                gather_out(e, not last)
                if ahead:
                    gather_g(e + 2, (0, 1, 2))
                for t in range(*HALF[0]):
                    store_out(e, t)
                if ahead:
                    gather_g(e + 2, (3, 4))

            pool.wait_ge(s_lrow, 1)
            for t in range(NT):
                pool.indirect_dma_start(logit_dram, bass.IndirectOffsetOnAxis(ap=tok_i[:, t:t + 1], axis=0),
                                        logit_out[:, t], None, bounds_check=T - 1, oob_is_err=False).then_inc(s_lput, 16)
            pool.wait_ge(s_lput, 16 * NT)
            pool.dma_start(logit_in[:, :, :], logit_dram.rearrange("(t p) c -> p t c", p=P)).then_inc(s_lback, 16)

            pool.wait_ge(s_tt, NT)
            pool.wait_ge(s_tab2, 1)
            gather_g(0, range(CT))
            store_block(0)
            store_block(1)
            gather_g(1, range(CT))
            store_block(2)
            store_block(3)
            pool.wait_ge(s_out, 16 * NT)
            pool_expert(0, True, True, False)
            with pool.Fori(1, E - 2) as e:
                pool_expert(e, False, True, False)
            pool_expert(E - 2, False, False, False)
            pool_expert(E - 1, False, False, True)
            for t in range(HALF[1][0], CT):
                store_out(E - 1, t)
            pool.wait_ge(s_put, 16 * SLOTS)

        @block.scalar
        def _(act):
            def copy_hi(dst, src, signal):
                act.activation(dst, src, ACT.Copy).then_inc(signal, 1)

            act.wait_ge(s_const, 2)
            act.activation(gated[:, 1, 0:1], ones[:, 0:1], ACT.Silu).then_inc(s_warm, 1)
            for n in range(EC * 2):
                e, k = n // 2, n % 2 * 2
                act.wait_ge(s_ct, n + 1)
                copy_hi(ctx_t[:, e, HI, k:k + 2, :], ps[:, CTX_BANK[n % 3]:CTX_BANK[n % 3] + 2, :], s_cth)
            act.wait_ge(s_rt, 16)
            copy_hi(rt_w[:, :, HI, :], rt_raw[:, :, :], s_rt_hi)
            act.wait_ge(s_warm, 1)

            def act_step(i):
                if inside(i, 0, GT):
                    after(act, s_t2, i + 1)
                    copy_hi(a1_t[:, HI], ps[:, 1, :].rearrange("p (k m) -> p k m", k=KD), s_hi2)
                if inside(i, -1, GT - 1):
                    after(act, s_m1, i + 2)
                    act.activation(gated[:, 0], ps[:, 2, :], ACT.Silu).then_inc(s_sl1, 1)
                if inside(i, -2, GT - 2):
                    after(act, s_t1, i + 3)
                    copy_hi(h1_t[:, HI], ps[:, 0, :].rearrange("p (k m) -> p k m", k=KD), s_hi1)

            for i in range(-2, 0):
                act_step(i)
            with act.Fori(0, GT - 2) as i:
                act_step(i)

            def hi_up_shared(j, g):
                after(act, s_raw, 48 * (j + 1))
                after(act, s_g if g == 0 else s_u, j * NB)
                copy_hi(sh_u[:, g, HI], raw_u[:, j % 2, g], s_uh)

            def hi_down_shared(j):
                after(act, s_raw, 48 * (j + 1))
                after(act, s_dn, j * NB * BT)
                copy_hi(sh_d[:, HI], raw_d[:, j % 2], s_dh)

            def hi_expert_up(e, c):
                q = NJ + e * NC + c
                after(act, s_raw, 48 * (q + 1))
                after(act, s_u3, (e - 1) * 6 + 4 + c)
                for g in range(2):
                    copy_hi(up_w[:, c, g, HI, :, 0:CH[c]], expert_raw(e, c)[0][:, g], s_uh)

            def hi_expert_down(e, c):
                q = NJ + e * NC + c
                after(act, s_d3, (e - 1) * CT)
                copy_hi(dn_w[0:CH[c], e % 2, c, HI], expert_raw(e, c)[1], s_dh)

            def hi_h2(u):
                act.wait_ge(s_tt, u + 1)
                copy_hi(h2_t[:, u // BT, HI, :, u % BT * P:(u % BT + 1) * P],
                        ps[:, h2_bank(u), :].rearrange("p (k m) -> p k m", k=KD), s_tth)

            def act_block(j, b, last):
                n = j * NB + b
                after(act, s_g, n + 1)
                after(act, s_al, n - 1)
                act.activation(gated[:, b % 2], ps[:, 0, :], ACT.Silu).then_inc(s_sl, 1)
                for u in turns_early(n):
                    hi_h2(u)
                if b == NB - 1 and not last:
                    hi_up_shared(j + 1, 0)
                    hi_up_shared(j + 1, 1)
                after(act, s_mul, n + 1)
                after(act, s_dn, (n - 1) * BT)
                copy_hi(a2_t[:, b % 2, HI], gated[:, b % 2], s_ah)
                for u in turns_late(n):
                    hi_h2(u)
                if b == 0:
                    hi_down_shared(j)

            act.wait_ge(s_raw, 48)
            for g in range(2):
                copy_hi(sh_u0[:, g, HI], raw_u[:, 0, g], s_uh0)
            for u in range(BT):
                hi_h2(u)
            act_step(GT - 2)
            act_step(GT - 1)
            for u in range(BT, 2 * BT):
                hi_h2(u)
            act.wait_ge(s_m2, GT)
            hi_up_shared(0, 0)
            hi_up_shared(0, 1)
            for j in range(ROUTING):
                for b in range(NB):
                    act_block(j, b, False)
                    n = j * NB + b
                    if 3 <= n < 5:
                        for lb in (2 * n - 6, 2 * n - 5):
                            act.wait_ge(s_lgt, lb + 1)
                            copy_hi(logit_rows[:, lb * N:(lb + 1) * N], ps[0:2 * E, 6 + lb % 2, :], s_lgc)
                    if n == 12:
                        act.wait_ge(s_gap, 1)
                        act.activation(exp_gap[:, :], gap[:, :], ACT.Exp).then_inc(s_exp, 1)
            with act.Fori(ROUTING, NJ - 1) as j:
                for b in range(NB):
                    act_block(j, b, False)

            def hi_g(e, t):
                w = e * CT + t
                after(act, s_t3, w + 1)
                after(act, s_u3, (e - 1) * 6)
                copy_hi(g_t[:, e % 2, HI, :, t * P:(t + 1) * P],
                        ps[:, 6 + t % 2, :].rearrange("p (k m) -> p k m", k=KD), s_th3)

            def act_unit(e, u):
                h, c = u // NC, u % NC
                v, m, t0, t1 = e * 6 + u, CH[c], HALF[h][0], HALF[h][1]
                n = (t1 - t0) * P
                after(act, s_g3, v + 1)
                after(act, s_al3, v - 1)
                act.activation(gated[0:m, u % 2, 0:n], ps[0:m, 0, 0:n], ACT.Silu).then_inc(s_sl3, 1)
                after(act, s_mul3, v + 1)
                after(act, s_d3, (e - 1) * CT + t1)
                copy_hi(a3_t[0:m, c, HI, t0 * P:t1 * P], gated[0:m, u % 2, 0:n], s_ah3)

            act.wait_ge(s_perm2, 2)
            for b in range(NB):
                act_block(NJ - 1, b, True)
                if b < NC:
                    hi_expert_up(0, b)
                for t in EARLY[b]:
                    hi_g(0, t)
            act.wait_ge(s_u, NBLK)
            for c in range(NC):
                hi_expert_down(0, c)
            act.wait_ge(s_dn, NBLK * BT)

            def act_expert(e, last):
                for u in range(6):
                    act_unit(e, u)
                    if not last:
                        if u < 3:
                            hi_g(e + 1, u)
                        if u == 4:
                            hi_g(e + 1, 3)
                        if u == 5:
                            hi_g(e + 1, 4)
                        if u >= 3:
                            hi_expert_up(e + 1, u - 3)
                            hi_expert_down(e + 1, u - 3)

            act_expert(0, False)
            with act.Fori(1, E - 1) as e:
                act_expert(e, False)
            act_expert(E - 1, True)

        @block.vector
        def _(dve):
            steps = [0]

            def link(ins):
                steps[0] += 1
                ins.then_inc(s_v, 1)
                dve.wait_ge(s_v, steps[0])

            def copy_lo(dst, src, hi, signal):
                dve.tensor_tensor(dst, src, hi.bitcast(F32), ALU.subtract).then_inc(signal, 1)

            def slot_parts():
                dve.tensor_single_scalar(col_i[:, :], slot_i[:, :], 7, ALU.arith_shift_right).then_inc(s_col, 1)
                link(dve.tensor_single_scalar(lane_i[:, :], slot_i[:, :], P - 1, ALU.bitwise_and))

            dve.memset(at_least[:, 0], 1.0).then_inc(s_edge, 1)
            dve.memset(at_least[:, EC], 0.0).then_inc(s_edge, 1)
            dve.memset(tile_end[:, 0:1], 0.0).then_inc(s_edge, 1)
            dve.wait_ge(s_ids, 16)
            for e in range(1, EC):
                dve.tensor_scalar(at_least[:, e], ids_i[:, :], float(VOCAB_PART * e), None, ALU.is_ge).then_inc(s_edge, 1)
            dve.wait_ge(s_edge, EC + 2)
            dve.tensor_tensor(member1[:, :, :], at_least[:, 0:EC], at_least[:, 1:EC + 1],
                              ALU.subtract).then_inc(s_mem1, 1)
            dve.wait_ge(s_cnt1, 1)
            dve.wait_ge(s_const, 13)
            totals = ps[:, 4, 0:EC * NT]
            within = ps[:, 4, EC * NT:2 * EC * NT].rearrange("p (e j) -> p e j", e=EC)
            link(dve.tensor_tensor_scan(run1[:, :, :].rearrange("p e j -> p (e j)"),
                                        restart[:, :, :].rearrange("p e j -> p (e j)"), totals, 0.0, ALU.mult, ALU.add))
            link(dve.tensor_scalar(tiles_i[:, :], run1[:, :, NT - 1], float(P - 1), None, ALU.add))
            link(dve.tensor_single_scalar(tiles_i[:, :], tiles_i[:, :], 7, ALU.arith_shift_right))
            dve.scalar_tensor_tensor(out=unpad[:, :], in0=tiles_i[:, :], scalar=-float(P), in1=run1[:, :, NT - 1],
                                     op0=ALU.mult, op1=ALU.add).then_inc(s_unpad, 1)
            link(dve.tensor_tensor_scan(tile_end[:, 1:EC + 1], ones[:, 0:EC], tiles_i[:, :], 0.0, ALU.mult, ALU.add))
            dve.wait_ge(s_unpad, 1)
            link(dve.tensor_tensor(run1[:, :, :], run1[:, :, :], within, ALU.add))
            link(dve.scalar_tensor_tensor(out=run1[:, :, :], in0=tile_end[:, 0:EC].unsqueeze(2).to_broadcast([P, EC, NT]),
                                          scalar=float(P), in1=run1[:, :, :], op0=ALU.mult, op1=ALU.add))
            link(dve.tensor_tensor(run1[:, :, :], run1[:, :, :], member1[:, :, :], ALU.mult))
            link(dve.tensor_reduce(slot_f[:, :], run1[:, :, :].rearrange("p e j -> p j e"), AX.X, ALU.add))
            link(dve.tensor_copy(slot_i[:, :], slot_f[:, :]))
            slot_parts()
            dve.tensor_tensor(pick1[:, :, :], lane[:, :].unsqueeze(1).to_broadcast([P, NT, P]),
                              lane_i[:, :].unsqueeze(2).to_broadcast([P, NT, P]), ALU.is_equal).then_inc(s_pick1, 1)
            G = GT + 1
            dve.wait_ge(s_col, 1)
            link(dve.tensor_tensor(vals1[:, :, 1, :], lane[:, 0:G].unsqueeze(1).to_broadcast([P, NT, G]),
                                   col_i[:, :].unsqueeze(2).to_broadcast([P, NT, G]), ALU.is_equal))
            dve.tensor_tensor(vals1[:, :, 0, :], vals1[:, :, 1, :].bitcast(F32),
                              tok_pj[:, :].unsqueeze(2).to_broadcast([P, NT, G]), ALU.mult).then_inc(s_pick1, 1)
            link(dve.tensor_scalar(tile_e[:, :], lane[:, 0:G], tile_end[:, 1:2], None, ALU.is_ge))
            for e in range(2, EC):
                link(dve.scalar_tensor_tensor(out=tile_e[:, :] if e < EC - 1 else tile_ei[:, :], in0=lane[:, 0:G],
                                              scalar=tile_end[:, e:e + 1], in1=tile_e[:, :], op0=ALU.is_ge, op1=ALU.add))

            def lo_ctx(n):
                e, k = n // 2, n % 2 * 2
                dve.wait_ge(s_cth, n + 1)
                copy_lo(ctx_t[:, e, LO, k:k + 2, :], ps[:, CTX_BANK[n % 3]:CTX_BANK[n % 3] + 2, :],
                        ctx_t[:, e, HI, k:k + 2, :], s_ctl)

            for n in range(2):
                lo_ctx(n)
            dve.wait_ge(s_perm1, 1)
            found = ps[:, 5, 0:2 * G].rearrange("p (w c) -> p w c", w=2)
            link(dve.tensor_scalar(put1_f[:, :], found[:, 1], -float(T), float(T), ALU.mult, ALU.add))
            link(dve.tensor_tensor(put1_f[:, :], put1_f[:, :], found[:, 0], ALU.add))
            dve.tensor_scalar(get1[:, :], put1_f[:, :], float(T - 1), None, ALU.min).then_inc(s_tab1, 1)

            def position_table():
                for e in range(1, EC):
                    link(dve.tensor_scalar(shift1[:, e - 1], lane[:, 0:G], tile_end[:, e:e + 1], unpad[:, e - 1:e],
                                           ALU.is_ge, ALU.mult))
                    link(dve.tensor_tensor(pos_f[:, :], pos_f[:, :] if e > 1 else num_tp[:, :], shift1[:, e - 1], ALU.add))
                link(dve.scalar_tensor_tensor(out=pos_f[:, :], in0=pos_f[:, :], scalar=-float(T), in1=found[:, 1],
                                              op0=ALU.add, op1=ALU.mult))
                dve.tensor_scalar(put1[:, :], pos_f[:, :], float(T), None, ALU.add).then_inc(s_tab1, 1)

            def stats(src, part, s_part, mv, s_st, k):
                apart(dve, s_passed[0])
                dve.bn_stats(part[:, :], src).then_inc(s_part, 1)
                after(dve, s_part, k + 1)
                apart(dve, s_passed[0])
                dve.bn_aggr(mv[:, :], part[:, :]).then_inc(s_st, 1)

            def stats_x(k, q, c):
                after(dve, s_xin[c], 16 * (q + 1))
                after(dve, s_h1, k)
                stats(x_in[:, c], part1, s_part1, mv1, s_st1, k)

            def norm_x(k, c):
                after(dve, s_rs1, k + 1)
                after(dve, s_t1, k)
                dve.tensor_scalar(h1, x_in[:, c], mv1[:, 0:1], rstd1[:, 0:1],
                                  ALU.subtract, ALU.mult).then_inc(s_h1, 1)

            def lo_h1(k):
                after(dve, s_hi1, k + 1)
                copy_lo(h1_t[:, LO], ps[:, 0, :].rearrange("p (k m) -> p k m", k=KD), h1_t[:, HI], s_lo1)

            def lo_a1(k):
                after(dve, s_hi2, k + 1)
                copy_lo(a1_t[:, LO], ps[:, 1, :].rearrange("p (k m) -> p k m", k=KD), a1_t[:, HI], s_lo2)

            def stats_x1(k, c):
                after(dve, s_x1, k + 1)
                after(dve, s_h2, k)
                stats(x1[:, c % 2, 0:D], part2, s_part2, mv2, s_st2, k)

            def norm_x1(k, q, c):
                after(dve, s_rs2, k + 1)
                after(dve, s_hout[c % 2], 16 * (2 * q + c // 2))
                dve.tensor_scalar(h2[:, c % 2], x1[:, c % 2, 0:D], mv2[:, 0:1], rstd2[:, 0:1],
                                  ALU.subtract, ALU.mult).then_inc(s_h2, 1)

            def x1_of(i, q, c):
                if inside(i, 0, GT):
                    after(dve, s_m2, i + 1)
                    after(dve, s_xout[c % 2], 16 * (2 * q + c // 2))
                    dve.tensor_tensor(x1[:, c % 2, 0:D], x_in[:, c], ps[:, 3, :], ALU.add).then_inc(s_x1, 1)
                    dve.tensor_copy(x1[:, c % 2, D:D + 1], put1_f[:, bass.ds(i, 1)]).then_inc(s_tok, 1)

            def dve_rest(i, q, c):
                if inside(i, -2, GT - 3):
                    norm_x(i + 3, (c + 3) % 4)
                if inside(i, -1, GT - 1):
                    lo_a1(i + 1)
                if inside(i, 0, GT):
                    stats_x1(i, c)
                if inside(i, -2, GT - 2):
                    after(dve, s_sl1, i + 3)
                    dve.tensor_tensor(gated[:, 0], gated[:, 0], ps[:, 2, :],
                                      ALU.mult).then_inc(s_a1, 1)
                if inside(i, -2, GT - 3):
                    lo_h1(i + 3)
                if inside(i, 0, GT):
                    norm_x1(i, q, c)
                if inside(i, -4, GT - 4):
                    stats_x(i + 4, q + 1, c)

            def dve_step(i, q, c):
                x1_of(i, q, c)
                dve_rest(i, q, c)

            for n in range(2, EC * 2 - 2):
                lo_ctx(n)
            dve_step(-4, -1, 0)
            lo_ctx(EC * 2 - 2)
            norm_x(0, 0)
            lo_ctx(EC * 2 - 1)
            lo_h1(0)
            stats_x(1, 0, 1)
            for i in range(-2, 4):
                if i == 0:
                    position_table()
                dve_step(i, i // 4, i % 4)
            dve.wait_ge(s_rt_hi, 1)
            copy_lo(rt_w[:, :, LO, :], rt_raw[:, :, :], rt_w[:, :, HI, :], s_rt_lo)
            with dve.Fori(1, ROUNDS) as q:
                for c in range(4):
                    dve_step(4 * q + c, q, c)
            for i in range(4 * ROUNDS, GT - 3):
                dve_step(i, i // 4, i % 4)

            def lo_up_shared(j, g):
                after(dve, s_uh, j * 2 + g + 1)
                copy_lo(sh_u[:, g, LO], raw_u[:, j % 2, g], sh_u[:, g, HI], s_ul)

            def lo_down_shared(j):
                after(dve, s_dh, j + 1)
                copy_lo(sh_d[:, LO], raw_d[:, j % 2], sh_d[:, HI], s_dl)

            def lo_expert_up(e, c):
                q = NJ + e * NC + c
                for g in range(2):
                    after(dve, s_uh, q * 2 + g + 1)
                    copy_lo(up_w[:, c, g, LO, :, 0:CH[c]], expert_raw(e, c)[0][:, g],
                            up_w[:, c, g, HI, :, 0:CH[c]], s_ul)

            def lo_expert_down(e, c):
                q = NJ + e * NC + c
                after(dve, s_dh, q + 1)
                copy_lo(dn_w[0:CH[c], e % 2, c, LO], expert_raw(e, c)[1], dn_w[0:CH[c], e % 2, c, HI], s_dl)

            def lo_h2(u):
                dve.wait_ge(s_tth, u + 1)
                b, cols = u // BT, slice(u % BT * P, (u % BT + 1) * P)
                copy_lo(h2_t[:, b, LO, :, cols], ps[:, h2_bank(u), :].rearrange("p (k m) -> p k m", k=KD),
                        h2_t[:, b, HI, :, cols], s_ttl)

            def add_down(j, b, t):
                after(dve, s_dn, (j * NB + b) * BT + t + 1)
                y = acc[:, b * BT + t, :]
                dve.tensor_tensor(y, y, ps[:, 2 + t, :], ALU.add).then_inc(s_add, 1)

            def dve_block(j, b, first, last):
                n = j * NB + b
                jp, bp = (j, b - 1) if b else (j - 1, NB - 1)
                if b == NB - 1 and not last:
                    lo_up_shared(j + 1, 0)
                for u in turns_early(n):
                    lo_h2(u)
                after(dve, s_sl, n + 1)
                after(dve, s_u, n + 1)
                dve.tensor_tensor(gated[:, b % 2], gated[:, b % 2], ps[:, 1, :], ALU.mult).then_inc(s_mul, 1)
                if b == NB - 1 and not last:
                    lo_up_shared(j + 1, 1)
                if first:
                    norm_x1(GT - 1, (GT - 1) // 4, (GT - 1) % 4)
                for u in turns_late(n):
                    lo_h2(u)
                if isinstance(n, int) and 1 <= n <= NB:
                    dve.wait_ge(s_yin[n - 1], 16)
                if not first:
                    add_down(jp, bp, 0)
                    add_down(jp, bp, 1)
                after(dve, s_ah, n + 1)
                copy_lo(a2_t[:, b % 2, LO], gated[:, b % 2], a2_t[:, b % 2, HI], s_al)
                if not first:
                    add_down(jp, bp, 2)
                    add_down(jp, bp, 3)
                if b == 0:
                    lo_down_shared(j)

            over_e = [P, NT, E]

            def choose(k):
                link(dve.tensor_reduce(top[:, k], cand[:, :, :], AX.X, ALU.max))
                link(dve.tensor_tensor(hot[:, k], cand[:, :, :], top[:, k].unsqueeze(2).to_broadcast(over_e), ALU.is_equal))
                link(dve.tensor_tensor(hot[:, k], hot[:, k], descend[:, :].unsqueeze(1).to_broadcast(over_e), ALU.mult))
                link(dve.tensor_reduce(first[:, :], hot[:, k], AX.X, ALU.max))
                link(dve.tensor_tensor(hot[:, k], descend[:, :].unsqueeze(1).to_broadcast(over_e),
                                       first[:, :].unsqueeze(2).to_broadcast(over_e), ALU.is_equal))

            def logits_out():
                dve.wait_ge(s_lg, 1)
                halves = ps[:, 6, 0:NT * 2 * E].rearrange("p (t h e) -> p t h e", t=NT, h=2)
                link(dve.tensor_copy(logit_out[:, :, 0:E], halves[:, :, LO]))
                link(dve.tensor_tensor(logit_out[:, :, 0:E], logit_out[:, :, 0:E], halves[:, :, HI], ALU.add))
                link(dve.tensor_copy(logit_out[:, :, E], num_tp[:, 0:NT]))
                dve.wait_ge(s_tokin, 16)
                dve.tensor_copy(tok_i[:, :], tok_f[:, :]).then_inc(s_lrow, 1)

            def top_first():
                dve.wait_ge(s_lback, 16)
                link(dve.tensor_copy(cand[:, :, :], logit))
                choose(0)

            def top_second():
                link(dve.scalar_tensor_tensor(out=cand[:, :, :], in0=hot[:, 0], scalar=-3e38, in1=logit,
                                              op0=ALU.mult, op1=ALU.add))
                choose(1)
                dve.tensor_tensor(member2[:, :, :], hot[:, 0], hot[:, 1], ALU.add).then_inc(s_mem2, 1)
                dve.tensor_tensor(gap[:, :], top[:, 1], top[:, 0], ALU.subtract).then_inc(s_gap, 1)

            def top_weights():
                dve.wait_ge(s_exp, 1)
                link(dve.tensor_scalar(first[:, :], exp_gap[:, :], 1.0, None, ALU.add))
                link(dve.reciprocal(weight[:, 0], first[:, :]))
                link(dve.tensor_tensor(weight[:, 1], exp_gap[:, :], weight[:, 0], ALU.mult))

            def positions():
                dve.wait_ge(s_cnt2, 1)
                totals2 = ps[:, 7, 0:NT * E].rearrange("p (t e) -> p t e", t=NT)
                within2 = ps[:, 7, NT * E:2 * NT * E].rearrange("p (t e) -> p t e", t=NT)
                for e in range(E):
                    dve.tensor_tensor_scan(run2[:, :, e], ones[:, 0:NT], totals2[:, :, e], 0.0,
                                           ALU.mult, ALU.add).then_inc(s_scan, 1)
                dve.wait_ge(s_scan, E)
                link(dve.tensor_tensor(run2[:, :, :], run2[:, :, :], within2, ALU.add))
                link(dve.tensor_scalar(late[:, :, :], run2[:, :, :], float(CAP), float(2 * E * CAP), ALU.is_ge, ALU.mult))
                link(dve.tensor_tensor(late[:, :, :], late[:, :, :], run2[:, :, :], ALU.add))
                link(dve.tensor_tensor(late[:, :, :], late[:, :, :], slot0[:, :].unsqueeze(1).to_broadcast(over_e), ALU.add))

            def top_weights_and_positions():
                top_weights()
                positions()

            def choice_slots(k):
                link(dve.tensor_tensor(run2[:, :, :], hot[:, k], late[:, :, :], ALU.mult))
                link(dve.tensor_reduce(slot_f[:, :], run2[:, :, :], AX.X, ALU.add))
                link(dve.tensor_copy(slot_i[:, :], slot_f[:, :]))
                slot_parts()
                link(dve.tensor_copy(w_hl[:, HI], weight[:, k]))
                link(dve.tensor_tensor(w_hl[:, LO], weight[:, k], w_hl[:, HI].bitcast(F32), ALU.subtract))

            def choice_pick(k):
                if k:
                    dve.wait_ge(s_perm2, 1)
                dve.tensor_tensor(pick2[:, :, :], lane[:, :].unsqueeze(1).to_broadcast([P, NT, P]),
                                  lane_i[:, :].unsqueeze(2).to_broadcast([P, NT, P]), ALU.is_equal).then_inc(s_pick2, 1)

            def choice_vals(k):
                cols = [P, NT, SLOTS]
                dve.wait_ge(s_col, k + 2)
                link(dve.tensor_tensor(vals2[:, :, 1, :], lane[:, 0:SLOTS].unsqueeze(1).to_broadcast(cols),
                                       col_i[:, :].unsqueeze(2).to_broadcast(cols), ALU.is_equal))
                for w, v in ((0, num_tp[:, 0:NT]), (4, logit_in[:, :, E]), (2, w_hl[:, HI].bitcast(F32)), (3, w_hl[:, LO].bitcast(F32))):
                    dve.tensor_tensor(vals2[:, :, w, :], vals2[:, :, 1, :].bitcast(F32),
                                      v.unsqueeze(2).to_broadcast(cols), ALU.mult).then_inc(s_pick2, 1)

            def slot_tables():
                dve.wait_ge(s_perm2, 2)
                got = ps[:, 7, 256:256 + 5 * SLOTS].rearrange("p (w c) -> p w c", w=5)
                link(dve.tensor_copy(pos2[:, :], got[:, 4]))
                link(dve.tensor_scalar(put2_f[:, :], got[:, 1], -float(T), float(T), ALU.mult, ALU.add))
                link(dve.tensor_tensor(put2_f[:, :], put2_f[:, :], got[:, 0], ALU.add))
                link(dve.tensor_copy(put2[:, :], put2_f[:, :]))
                link(dve.tensor_scalar(get2[:, :], put2_f[:, :], float(T - 1), None, ALU.min))
                link(dve.tensor_copy(slot_w[:, :], got[:, 2]))
                link(dve.tensor_tensor(slot_w[:, :], slot_w[:, :], got[:, 3], ALU.add))
                dve.memset(ve1[:, :], 0.0).then_inc(s_tab2, 1)

            extra = {6: logits_out, 10: top_first, 11: top_second, 12: top_weights_and_positions,
                     13: lambda: choice_slots(0), 14: lambda: choice_pick(0), 15: lambda: choice_vals(0),
                     16: lambda: choice_slots(1), 17: lambda: choice_pick(1), 18: lambda: choice_vals(1),
                     19: slot_tables}
            i = GT - 3
            x1_of(i, i // 4, i % 4)
            for u in range(BT):
                lo_h2(u)
            dve_rest(i, i // 4, i % 4)
            for g in range(2):
                dve.wait_ge(s_uh0, g + 1)
                copy_lo(sh_u0[:, g, LO], raw_u[:, 0, g], sh_u0[:, g, HI], s_ul0)
            i, k = GT - 2, GT - 1
            x1_of(i, i // 4, i % 4)
            lo_a1(k)
            for u in range(BT, 2 * BT):
                lo_h2(u)
            stats_x1(i, i % 4)
            x1_of(k, k // 4, k % 4)
            lo_up_shared(0, 0)
            norm_x1(i, i // 4, i % 4)
            lo_up_shared(0, 1)
            stats_x1(k, k % 4)
            for j in range(ROUTING):
                for b in range(NB):
                    n = j * NB + b
                    dve_block(j, b, n == 0, False)
                    if n in extra:
                        extra[n]()
            with dve.Fori(ROUTING, NJ - 1) as j:
                for b in range(NB):
                    dve_block(j, b, False, False)

            def lo_g(e, t):
                after(dve, s_th3, e * CT + t + 1)
                copy_lo(g_t[:, e % 2, LO, :, t * P:(t + 1) * P],
                        ps[:, 6 + t % 2, :].rearrange("p (k m) -> p k m", k=KD),
                        g_t[:, e % 2, HI, :, t * P:(t + 1) * P], s_tl3)

            def dve_unit(e, u):
                h, c = u // NC, u % NC
                v, m, t0, t1 = e * 6 + u, CH[c], HALF[h][0], HALF[h][1]
                n = (t1 - t0) * P
                after(dve, s_sl3, v + 1)
                after(dve, s_u3, v + 1)
                dve.tensor_tensor(gated[0:m, u % 2, 0:n], gated[0:m, u % 2, 0:n], ps[0:m, 1, 0:n],
                                  ALU.mult).then_inc(s_mul3, 1)
                after(dve, s_ah3, v + 1)
                copy_lo(a3_t[0:m, c, LO, t0 * P:t1 * P], gated[0:m, u % 2, 0:n],
                        a3_t[0:m, c, HI, t0 * P:t1 * P], s_al3)

            def weighted(e, t):
                after(dve, s_d3, e * CT + t + 1)
                after(dve, s_oin[t], 16 * (e + 1))
                dve.scalar_tensor_tensor(out=out_new[:, t], in0=ps[:, 2 + t % 4, :],
                                         scalar=slot_w[:, bass.ds(e * CT + t, 1)], in1=out_new[:, t],
                                         op0=ALU.mult, op1=ALU.add).then_inc(s_y3, 1)

            for b in range(NB):
                dve_block(NJ - 1, b, False, True)
                if b < NC:
                    lo_expert_up(0, b)
                for t in EARLY[b]:
                    lo_g(0, t)
            for t in range(BT):
                add_down(NJ - 1, NB - 1, t)
            def dve_expert(e, first, last):
                for u in range(6):
                    dve_unit(e, u)
                    if u < 3:
                        if first:
                            lo_expert_down(0, u)
                        else:
                            weighted(e - 1, 2 + u)
                        if not last:
                            lo_g(e + 1, u)
                    if u >= 3:
                        if not last:
                            if u == 4:
                                lo_g(e + 1, 3)
                            if u == 5:
                                lo_g(e + 1, 4)
                            lo_expert_up(e + 1, u - 3)
                            lo_expert_down(e + 1, u - 3)
                        if u < 5:
                            weighted(e, u - 3)

            dve_expert(0, True, False)
            with dve.Fori(1, E - 1) as e:
                dve_expert(e, False, False)
            dve_expert(E - 1, False, True)
            for t in range(HALF[1][0], CT):
                weighted(E - 1, t)

        @block.tensor
        def _(pe):
            pe.wait_ge(s_const, 9)
            pe.wait_ge(s_mem1, 1)
            flat = member1[:, :, :].rearrange("p e j -> p (e j)")
            pe.matmul(ps[:, 4, 0:EC * NT], ones[:, :], flat, start=True, stop=True)
            pe.matmul(ps[:, 4, EC * NT:2 * EC * NT], not_below[:, :], flat, start=True, stop=True).then_inc(s_cnt1, 1)

            def turn_ctx(n):
                e, k0 = n // 2, n % 2 * 2
                if n % 2 == 0:
                    pe.wait_ge(s_ctx[e], 16)
                if n >= 3:
                    pe.wait_ge(s_ctl, n - 2)
                for k in range(2):
                    for r in range(KD):
                        mm = pe.transpose(ps[:, CTX_BANK[n % 3] + k, r * P:(r + 1) * P],
                                          ctx_raw[:, e, r, (k0 + k) * P:(k0 + k + 1) * P], ident[:, :])
                mm.then_inc(s_ct, 1)

            for n in range(3):
                turn_ctx(n)
            pe.wait_ge(s_pick1, 2)
            for j in range(NT):
                mm = pe.matmul(ps[:, 5, 0:2 * (GT + 1)], pick1[:, j, :], vals1[:, j].rearrange("p w c -> p (w c)"),
                               start=(j == 0), stop=(j == NT - 1))
            mm.then_inc(s_perm1, 1)
            for n in range(3, EC * 2):
                turn_ctx(n)

            def turn(bank, src):
                for k in range(KD):
                    mm = pe.transpose(ps[:, bank, k * P:(k + 1) * P], src[:, k * P:(k + 1) * P], ident[:, :])
                return mm

            def by_ctx(bank, lhs, e, lo_ready, count):
                n = 0
                for a, b in ((HI, LO), (LO, HI), (HI, HI)):
                    if a == LO:
                        after(pe, lo_ready, count)
                    for k in range(KD):
                        mm = pe.matmul(ps[:, bank, :], lhs[:, a, k, :],
                                       area_a[:, bass.ds(e * (2 * KD * D) + (b * KD + k) * D, D)],
                                       start=(n == 0), stop=(n == 3 * KD - 1))
                        n += 1
                return mm

            def tile_expert(k):
                return pe.value_load(tile_ei[0:1, bass.ds(k, 1)], min_val=0, max_val=EC - 1)

            def keep_warm(bank, count):
                for n in range(count):
                    pe.matmul(ps[:, bank, :], ctx_t[:, 0, HI, 0, 0:P], ctx_t[:, 0, HI, 0, :], start=True, stop=True)

            def pe_step(i, between=()):
                if inside(i, -1, GT - 1):
                    next_expert = tile_expert(i + 1)
                if inside(i, 0, GT):
                    expert = tile_expert(i)
                    after(pe, s_a1, i + 1)
                    after(pe, s_lo2, i)
                    turn(1, gated[:, 0]).then_inc(s_t2, 1)
                for u in between:
                    turn_h2(u)
                if isinstance(i, int) and i == -1:
                    pe.wait_ge(s_ctl, EC * 2)
                if inside(i, -1, GT - 1):
                    after(pe, s_hi1, i + 2)
                    by_ctx(2, h1_t, next_expert, s_lo1, i + 2).then_inc(s_m1, 1)
                if inside(i, -2, GT - 2):
                    after(pe, s_h1, i + 3)
                    after(pe, s_lo1, i + 2)
                    turn(0, h1).then_inc(s_t1, 1)
                if inside(i, 0, GT):
                    after(pe, s_hi2, i + 1)
                    after(pe, s_x1, i)
                    by_ctx(3, a1_t, expert, s_lo2, i + 1).then_inc(s_m2, 1)

            keep_warm(4, 12)
            pe.wait_ge(s_ctl, EC * 2 - 1)
            pe_step(-2)
            for i in range(-1, 1):
                pe_step(i)
            with pe.Fori(1, GT - 2) as i:
                pe_step(i)
            def turn_h2(u):
                pe.wait_ge(s_hin[u % 8], 16 * (u // 8 + 1))
                if u >= 8:
                    pe.wait_ge(s_ttl, u - 1)
                elif u >= 4:
                    pe.wait_ge(s_ttl, u - 3)
                turn(h2_bank(u), h2_in(u)).then_inc(s_tt, 1)

            def up(j, b, g, signal):
                weights = sh_u0 if is_first(j, b) else sh_u
                i = 0
                for w, m in PASSES:
                    if m == LO and g == 0 and isinstance(j, int) and j == 0:
                        pe.wait_ge(s_ttl, (b + 1) * BT)
                    for k in range(KD):
                        mm = pe.matmul(ps[:, g, :], weights[:, g, w, k, :], h2_t[:, b, m, k, :],
                                       start=(i == 0), stop=(i == 3 * KD - 1))
                        i += 1
                mm.then_inc(signal, 1)

            def weights_split(j, b, g):
                if is_first(j, b):
                    pe.wait_ge(s_ul0, g + 1)
                else:
                    after(pe, s_ul, j * 2 + g + 1)

            def gate_block(j, b):
                weights_split(j, b, 0)
                after(pe, s_sl, j * NB + b)
                up(j, b, 0, s_g)

            def up_block(j, b):
                n = j * NB + b
                if not is_first(j, b):
                    gate_block(j, b)
                for u in turns_early(n):
                    turn_h2(u)
                weights_split(j, b, 1)
                after(pe, s_mul, n)
                up(j, b, 1, s_u)
                for u in turns_late(n):
                    turn_h2(u)

            def down_block(j, b):
                n = j * NB + b
                after(pe, s_al, n + 1)
                after(pe, s_dl, j + 1)
                for t in range(BT):
                    after(pe, s_add, (n - 1) * BT + t + 1)
                    for i, (a, w) in enumerate(PASSES):
                        mm = pe.matmul(ps[:, 2 + t, :], a2_t[:, b % 2, a, t * P:(t + 1) * P], sh_d[:, w, :],
                                       start=(i == 0), stop=(i == 2))
                    mm.then_inc(s_dn, 1)

            def router_logits(b):
                if b >= 2:
                    pe.wait_ge(s_lgc, b - 1)
                i = 0
                for a in (LO, HI):
                    for k in range(KD):
                        mm = pe.matmul(ps[0:2 * E, 6 + b % 2, :], rt_w[:, k].rearrange("p h e -> p (h e)"),
                                       h2_t[:, b, a, k, :], start=(i == 0), stop=(i == 2 * KD - 1))
                        i += 1
                mm.then_inc(s_lgt, 1)

            def turn_logits():
                pe.wait_ge(s_lgc, NB)
                for t in range(NT):
                    mm = pe.transpose(ps[:, 6, t * 2 * E:(t + 1) * 2 * E], logit_rows[:, t * P:(t + 1) * P],
                                      ident[0:2 * E, 0:2 * E])
                mm.then_inc(s_lg, 1)

            def choice_perm(k):
                pe.wait_ge(s_pick2, 5 * (k + 1))
                for j in range(NT):
                    mm = pe.matmul(ps[:, 7, 256:256 + 5 * SLOTS], pick2[:, j, :],
                                   vals2[:, j].rearrange("p w c -> p (w c)"),
                                   start=(k == 0 and j == 0), stop=(k == 1 and j == NT - 1))
                mm.then_inc(s_perm2, 1)

            for u in range(BT):
                turn_h2(u)
            pe_step(GT - 2)
            pe.wait_ge(s_lo1, GT)
            pe.wait_ge(s_tth, BT)
            gate_block(0, 0)
            pe_step(GT - 1, range(BT, 2 * BT))
            pe.wait_ge(s_lo2, GT)
            for j in range(ROUTING):
                for b in range(NB):
                    n = j * NB + b
                    if 0 < n < NB:
                        pe.wait_ge(s_tth, (n + 1) * BT)
                    up_block(j, b)
                    if n:
                        jp, bp = (j, b - 1) if b else (j - 1, NB - 1)
                        down_block(jp, bp)
                    if n == 3:
                        pe.wait_ge(s_rt_lo, 1)
                    if 3 <= n < 5:
                        router_logits(2 * n - 6)
                        router_logits(2 * n - 5)
                    if n == 5:
                        turn_logits()
                    if n == 12:
                        pe.wait_ge(s_mem2, 1)
                        flat2 = member2[:, :, :].rearrange("p t e -> p (t e)")
                        pe.matmul(ps[:, 7, 0:NT * E], ones[:, :], flat2, start=True, stop=True)
                        pe.matmul(ps[:, 7, NT * E:2 * NT * E], not_below[:, :], flat2,
                                  start=True, stop=True).then_inc(s_cnt2, 1)
                    if n == 16:
                        choice_perm(0)
                    if n == 19:
                        choice_perm(1)
            with pe.Fori(ROUTING, NJ - 1) as j:
                for b in range(NB):
                    up_block(j, b)
                    down_block(j if b else j - 1, (b - 1) % NB)

            def turn_g(e, t):
                w = e * CT + t
                after(pe, s_gin[t], 16 * (e + 1))
                after(pe, s_tl3, w - (t > 0))
                turn(6 + t % 2, g_in[:, t]).then_inc(s_t3, 1)

            def up_unit(e, u):
                h, c = u // NC, u % NC
                v, m, t0, t1 = e * 6 + u, CH[c], HALF[h][0], HALF[h][1]
                n = (t1 - t0) * P
                after(pe, s_tl3, e * CT + t1)
                for g, read, signal in ((0, s_sl3, s_g3), (1, s_mul3, s_u3)):
                    after(pe, s_ul, (NJ + e * NC + c) * 2 + g + 1)
                    after(pe, read, v)
                    i = 0
                    for w, a in PASSES:
                        for k in range(KD):
                            mm = pe.matmul(ps[0:m, g, 0:n], up_w[:, c, g, w, k, 0:m],
                                           g_t[:, e % 2, a, k, t0 * P:t1 * P],
                                           start=(i == 0), stop=(i == 3 * KD - 1))
                            i += 1
                    mm.then_inc(signal, 1)

            def down_part(e, t, chunks):
                h = 0 if t < HALF[0][1] else 1
                after(pe, s_al3, e * 6 + h * NC + chunks[-1] + 1)
                after(pe, s_dl, NJ + (e + 1) * NC)
                for a, w in PASSES:
                    for c in chunks:
                        mm = pe.matmul(ps[:, 2 + t % 4, :], a3_t[0:CH[c], c, a, t * P:(t + 1) * P],
                                       dn_w[0:CH[c], e % 2, c, w, :], start=(a == LO and c == 0),
                                       stop=(a == HI and w == HI and c == NC - 1))
                return mm

            def down_unit(e, t):
                after(pe, s_y3, e * CT + t - (t > 0))
                down_part(e, t, range(NC)).then_inc(s_d3, 1)

            for b in range(NB):
                up_block(NJ - 1, b)
                for t in EARLY[b]:
                    turn_g(0, t)
                down_block(NJ - 1 if b else NJ - 2, (b - 1) % NB)
            down_block(NJ - 1, NB - 1)

            def pe_expert(e, first, last):
                for u in range(6):
                    up_unit(e, u)
                    if u < 3 and not first:
                        down_unit(e - 1, 2 + u)
                    if 3 <= u < 5:
                        down_unit(e, u - 3)
                    if not last:
                        if u < 3:
                            turn_g(e + 1, u)
                        if u > 3:
                            turn_g(e + 1, u - 1)

            pe_expert(0, True, False)
            with pe.Fori(1, E - 1) as e:
                pe_expert(e, False, False)
            pe_expert(E - 1, False, True)
            for t in range(HALF[1][0], CT):
                after(pe, s_y3, (E - 1) * CT + t - 3)
                down_part(E - 1, t, range(NC - 1))
            for t in range(HALF[1][0], CT):
                down_part(E - 1, t, range(NC - 1, NC)).then_inc(s_d3, 1)


_INS = ['x', 'itok_BxS_13_99985', 'ctx_2048', 'L0_ffn_router', 'L0_ffn_w_up_gate', 'L0_ffn_w_down',
        'L0_ffn_shared_w_up_gate', 'L0_ffn_shared_w_down']


def kernel(**inputs):
    import numpy as np
    import concourse.bacc as bacc
    from concourse.bass_utils import run_bass_kernel_spmd

    nc = bacc.Bacc("TRN2", target_bir_lowering=False, num_devices=1)
    arrays, args = {}, []
    for name in _INS:
        a = np.ascontiguousarray(inputs[name])
        arrays[f"in_{name}"] = a
        args.append(nc.dram_tensor(f"in_{name}", a.shape, mybir.dt.from_np(a.dtype), kind="ExternalInput").ap())
    args.append(nc.dram_tensor("out_x", tuple(inputs["x"].shape), F32, kind="ExternalOutput").ap())
    routed_block_program(nc, *args)
    r = run_bass_kernel_spmd(nc, [arrays], core_ids=[0])
    return r.results[0]["out_x"]
```
